# Optimizing a Trainium2 kernel written in Bass

```python
import numpy as np
import jax
import jax.numpy as jnp

def _softmax(x, axis=-1):
    return jax.nn.softmax(x, axis=axis)

def _gelu(x):
    return jax.nn.gelu(x, approximate=True)

def _silu(x):
    return jax.nn.silu(x)

def _sigmoid(x):
    return jax.nn.sigmoid(x)

def _layernorm(x, axis=-1, eps=1e-05):
    m = jnp.mean(x, axis=axis, keepdims=True)
    v = jnp.var(x, axis=axis, keepdims=True)
    return (x - m) / jnp.sqrt(v + eps)

def _scatter_add(tgt, idx, src, axis=0):
    return tgt.at[idx].add(src)

def _segment_sum(src, seg, n):
    return jax.ops.segment_sum(src, seg, n)
kernel_name = 'mk_gnn_ffn_d1_gnn_r8_6ed4af'

def setup_inputs(seed: int=0):
    np.random.seed(seed)
    _w = jnp.asarray

    def _rec_inputs():
        import jax
        import jax.numpy as jnp
        _gk = jax.random.key(seed)
        x = -0.0003713 + 1 * jax.random.normal(jax.random.fold_in(_gk, 1), (6250, 256), jnp.float32)
        _s = jax.random.randint(jax.random.fold_in(_gk, 2), (100000,), 0, 6250, jnp.int32)
        _d = jax.random.randint(jax.random.fold_in(_gk, 3), (100000,), 0, 6250, jnp.int32)
        _loop = jnp.arange(6250, dtype=jnp.int32)
        src = jnp.concatenate([_s, _d, _loop])
        dst = jnp.concatenate([_d, _s, _loop])
        _o = jnp.argsort(dst, stable=True)
        src = src[_o]
        dst = dst[_o]
        return (x, src, dst)
    x, src, dst = _rec_inputs()

    def _L0_gnn_setup():
        import jax, jax.numpy as jnp
        import numpy as np
        N = 6250
        E = 50000
        IN_DIM = 256
        H = 8
        D = 32
        LN_EPS = 1e-05
        key = jax.random.key(seed)
        k_x, k_e, k_w, k_a = jax.random.split(key, 4)
        x = jax.random.normal(k_x, (N, IN_DIM), dtype=jnp.float32)
        edge_index = jax.random.randint(k_e, (2, E), 0, N, dtype=jnp.int32)
        w_lim = np.sqrt(6.0 / (IN_DIM + H * D)) * np.sqrt(2.0)
        W = jax.random.uniform(k_w, (IN_DIM, H * D), minval=-w_lim, maxval=w_lim, dtype=jnp.float32)
        a_lim = np.sqrt(6.0 / (2 * D + 1))
        k_as, k_ad = jax.random.split(k_a)
        a_src = jnp.broadcast_to(jax.random.uniform(k_as, (1, D), minval=-a_lim, maxval=a_lim, dtype=jnp.float32), (H, D)).copy()
        a_dst = jnp.broadcast_to(jax.random.uniform(k_ad, (1, D), minval=-a_lim, maxval=a_lim, dtype=jnp.float32), (H, D)).copy()
        gamma = jnp.ones((H * D,), dtype=jnp.float32)
        beta = jnp.zeros((H * D,), dtype=jnp.float32)
        return {'x': x, 'edge_index': edge_index, 'W': W, 'a_src': a_src, 'a_dst': a_dst, 'gamma': gamma, 'beta': beta}
    _L0_gnn_all = _L0_gnn_setup()
    _L0_gnn_in = {k: v for k, v in _L0_gnn_all.items() if k in ('W', 'a_src', 'a_dst', 'gamma', 'beta')}
    del _L0_gnn_all

    def _L0_ffn_setup():
        import jax, jax.numpy as jnp
        import numpy as np
        B, S, H, F, E, K = (8, 512, 256, 512, 16, 2)
        EPS = 1e-05
        key = jax.random.key(seed)
        ks = jax.random.split(key, 9)
        sc = 0.02
        return {'x': jax.random.normal(ks[0], (B, S, H), dtype=jnp.float32), 'gate_w': jax.random.normal(ks[1], (H, E), dtype=jnp.float32) * sc, 'gate_b': jnp.zeros((E,), dtype=jnp.float32), 'w1': jax.random.normal(ks[2], (E, H, F), dtype=jnp.float32) * sc, 'b1': jnp.zeros((E, F), dtype=jnp.float32), 'w2': jax.random.normal(ks[3], (E, F, H), dtype=jnp.float32) * sc, 'b2': jnp.zeros((E, H), dtype=jnp.float32), 'gamma': jnp.ones((H,), dtype=jnp.float32), 'beta': jnp.zeros((H,), dtype=jnp.float32)}
    _L0_ffn_all = _L0_ffn_setup()
    _L0_ffn_in = {k: v for k, v in _L0_ffn_all.items() if k in ('gate_w', 'gate_b', 'w1', 'b1', 'w2', 'b2', 'gamma', 'beta')}
    del _L0_ffn_all
    return {'x': x, 'src': src, 'dst': dst, 'L0_gnn_W': _L0_gnn_in['W'], 'L0_gnn_a_src': _L0_gnn_in['a_src'], 'L0_gnn_a_dst': _L0_gnn_in['a_dst'], 'L0_gnn_gamma': _L0_gnn_in['gamma'], 'L0_gnn_beta': _L0_gnn_in['beta'], 'L0_ffn_gate_w': _L0_ffn_in['gate_w'], 'L0_ffn_gate_b': _L0_ffn_in['gate_b'], 'L0_ffn_w1': _L0_ffn_in['w1'], 'L0_ffn_b1': _L0_ffn_in['b1'], 'L0_ffn_w2': _L0_ffn_in['w2'], 'L0_ffn_b2': _L0_ffn_in['b2'], 'L0_ffn_gamma': _L0_ffn_in['gamma'], 'L0_ffn_beta': _L0_ffn_in['beta']}

def reference(x, src, dst, L0_gnn_W, L0_gnn_a_src, L0_gnn_a_dst, L0_gnn_gamma, L0_gnn_beta, L0_ffn_gate_w, L0_ffn_gate_b, L0_ffn_w1, L0_ffn_b1, L0_ffn_w2, L0_ffn_b2, L0_ffn_gamma, L0_ffn_beta):
    import jax
    import jax.numpy as jnp

    def _L0_gnn_ref(x, edge_index, W, a_src, a_dst, gamma, beta):
        import jax, jax.numpy as jnp
        import numpy as np
        N = 6250
        E = 50000
        IN_DIM = 256
        H = 8
        D = 32
        LN_EPS = 1e-05
        n = x.shape[0]
        src, dst = (edge_index[0], edge_index[1])
        hh = (x @ W).reshape(n, H, D)
        s_src = jnp.einsum('nhd,hd->nh', hh, a_src)
        s_dst = jnp.einsum('nhd,hd->nh', hh, a_dst)
        scores = jax.nn.leaky_relu(s_src[src] + s_dst[dst], negative_slope=0.2)
        m = jax.ops.segment_max(scores, dst, num_segments=n)
        e = jnp.exp(scores - m[dst])
        denom = jax.ops.segment_sum(e, dst, num_segments=n)
        alpha = e / denom[dst]
        msgs = hh[src] * alpha[:, :, None]
        out = jax.ops.segment_sum(msgs, dst, num_segments=n).reshape(n, H * D)
        out = out + x
        mu = jnp.mean(out, axis=-1, keepdims=True)
        var = jnp.mean(jnp.square(out - mu), axis=-1, keepdims=True)
        out = (out - mu) / jnp.sqrt(var + LN_EPS) * gamma + beta
        return jax.nn.elu(out)

    def _L0_ffn_ref(x, gate_w, gate_b, w1, b1, w2, b2, gamma, beta):
        import jax, jax.numpy as jnp
        import numpy as np
        B, S, H, F, E, K = (8, 512, 256, 512, 16, 2)
        EPS = 1e-05
        gate_logits = x @ gate_w + gate_b
        topk_vals, topk_idx = jax.lax.top_k(gate_logits, K)
        topk_w = jax.nn.softmax(topk_vals, axis=-1)
        h = jax.nn.relu(jnp.einsum('bsh,ehf->bsef', x, w1) + b1)
        expert_out = jnp.einsum('bsef,efh->bseh', h, w2) + b2
        sel = jnp.take_along_axis(expert_out, topk_idx[:, :, :, None], axis=2)
        moe = jnp.sum(topk_w[..., None] * sel, axis=2)
        y = x + moe
        mu = jnp.mean(y, axis=-1, keepdims=True)
        var = jnp.var(y, axis=-1, keepdims=True)
        return (y - mu) / jnp.sqrt(var + EPS) * gamma + beta
    edge_index = jnp.stack([src, dst])
    x = x + _L0_gnn_ref(_layernorm(x, axis=-1), edge_index, L0_gnn_W, L0_gnn_a_src, L0_gnn_a_dst, L0_gnn_gamma, L0_gnn_beta)
    x = x + _L0_ffn_ref(_layernorm(x, axis=-1)[None], L0_ffn_gate_w, L0_ffn_gate_b, L0_ffn_w1, L0_ffn_b1, L0_ffn_w2, L0_ffn_b2, L0_ffn_gamma, L0_ffn_beta)[0]
    return x

_drawn_inputs = setup_inputs


def setup_inputs(seed=0):
    import zlib

    import numpy as np

    out = dict(_drawn_inputs(seed))
    spreads = {'L0_gnn_gamma': (1.0, 0.2),
     'L0_gnn_beta': (0.0, 0.1),
     'L0_ffn_gate_b': (0.0, 0.318),
     'L0_ffn_b1': (0.0, 0.8),
     'L0_ffn_b2': (0.0, 0.296),
     'L0_ffn_gamma': (1.0, 0.2),
     'L0_ffn_beta': (0.0, 0.1)}
    factors = {}
    for name, (base, spread) in spreads.items():
        noise = np.random.default_rng([zlib.crc32(name.encode()), seed]).standard_normal(out[name].shape)
        drawn = base * np.exp(spread * noise) if base else spread * noise
        out[name] = jnp.asarray(drawn.astype(out[name].dtype))
    for name, factor in factors.items():
        out[name] = (out[name] * factor).astype(out[name].dtype)
    return out
```

```python
from contextlib import ExitStack

import concourse.bass as bass
import numpy as np
from concourse import mybir

F32 = mybir.dt.float32
BF16 = mybir.dt.bfloat16
I32 = mybir.dt.int32
U32 = mybir.dt.uint32
ALU = mybir.AluOpType
ACT = mybir.ActivationFunctionType
AX = mybir.AxisListType

P = 128
N, D = 6250, 256
E = 206250
HEADS, HD = 8, 32
TILES = (N + P - 1) // P
LAST = N - (TILES - 1) * P
FULL = TILES - 1
ROW = D + 2 * HEADS
SUM = D + HEADS
PROJ = D + 2 * HEADS
GRP = 7
NGRP = TILES // GRP
CHUNKS = (E + P - 1) // P
CB = (CHUNKS + P - 1) // P
CFULL = E // P
CREST = E - CFULL * P
PADC = CB * P
COLS = PADC + 8
NODST = 9999.0
BODY = 8
WEIGH, SUMS, JOIN = 2, 3, 4
AHEAD = 5
RING = 4
SLOPE = 0.2
IBLK = 1024
MAXSTEPS = TILES * ((CHUNKS + 1) // 2 + 1)
SLACK = (RING + 1) * BODY
IBLKS = (MAXSTEPS + SLACK) // IBLK + 1
EPS = 1e-5
EXPERTS, FF = 16, 512
KD, KF = D // P, FF // P
CAP = (N + P - 1) // P * P + P
PADROWS = EXPERTS * CAP
PADFFN = PADROWS + 2 * P
MAXFFN = 2 * N // P + EXPERTS
FFN_BODY = 4
FFN_LAG = 3
FFN_AHEAD = 3
FFN_SPARE = FFN_LAG + FFN_BODY + FFN_AHEAD
DROWS = PADFFN + FFN_SPARE * P
FFN_LIST = 128
ZERO_TILES = 41
FFN_TILES = -(-(MAXFFN + FFN_LAG + FFN_BODY) // ZERO_TILES) * ZERO_TILES
SAFE = 60.0


LIST_OF = ((AHEAD, True), (AHEAD, False), (0, True), (0, False), (-1, False), (-JOIN, False))
LISTS = len(LIST_OF)
NEXT_CHUNK, NEXT_TILE, CHUNK, TILE, LOOK_TILE, OLD_TILE = range(LISTS)


class Chain:

    def __init__(self, eng, sem):
        self.eng, self.sem, self.n, self.base = eng, sem, 0, 0

    def __call__(self, ins):
        self.n += 1
        ins.then_inc(self.sem, 1)
        self.eng.wait_ge(self.sem, self.base + self.n)

    def loop(self, it, first, per):
        self.start, self.per = self.n, per
        self.base = (it - first) * per

    def end(self, passes):
        assert self.n == self.start + self.per, (self.n, self.start, self.per)
        self.n, self.base = self.start + self.per * passes, 0


def build(nc, x, src, dst, W, a_src, a_dst, gamma, beta, gate_w, gate_b, w1, b1, w2, b2, fgamma, fbeta, out, stage=9):
    ctx = ExitStack()
    with ctx:
        def sb(name, shape, dt=F32):
            return ctx.enter_context(nc.sbuf_tensor(name, shape, dt))

        def sem(name):
            return ctx.enter_context(nc.semaphore(name))

        ctx.enter_context(nc.allow_non_contiguous_dma(reason="small constants"))
        table = nc.dram_tensor("table", [TILES * P, ROW], F32).ap()
        schedule = nc.dram_tensor("schedule", [IBLKS * IBLK // BODY, LISTS * BODY], I32).ap()

        dispatched = nc.dram_tensor("dispatched", [DROWS, D], F32).ap()
        expert_out = nc.dram_tensor("expert_out", [FFN_TILES * P, D], F32).ap()

        x_all = sb("x_all", [P, TILES, D])
        ident = sb("ident", [P, P])
        mean_var = sb("mean_var", [P, TILES, 2])
        rstd = sb("rstd", [P, TILES])
        nmr = sb("nmr", [P, TILES])
        slots = sb("slots", [P, TILES, 2], I32)
        gates = sb("gates", [P, TILES, 2])
        taken = sb("taken", [P, EXPERTS])
        zeroed = sem("zeroed")
        with ExitStack() as graph:
            def gsb(name, shape, dt=F32):
                return graph.enter_context(nc.sbuf_tensor(name, shape, dt))

            acc = gsb("acc", [P, TILES, SUM])
            with ExitStack() as edge:
                def esb(name, shape, dt=F32):
                    return edge.enter_context(nc.sbuf_tensor(name, shape, dt))

                node_iota = esb("node_iota", [P, P])
                neg_first = esb("neg_first", [P, TILES])
                dst_tab = esb("dst_tab", [P, TILES, 2 * HEADS])
                src_sc = esb("src_sc", [P, TILES, HEADS])
                srcT = esb("srcT", [P, COLS], I32)
                dstT = esb("dstT", [P, COLS])
                tile_lo = esb("tile_lo", [P, TILES])
                tile_n = esb("tile_n", [P, TILES])
                counts = esb("counts", [P, 4], I32)
                stage1(nc, x, src, dst, W, a_src, a_dst, table, x_all, acc, ident, node_iota, neg_first, mean_var,
                       rstd, nmr, dst_tab, src_sc, srcT, dstT, tile_lo, tile_n, expert_out, zeroed)
                stage2(nc, schedule, zeroed, dst_tab, src_sc, tile_lo, tile_n, counts)
                stage3(nc, table, schedule, acc, ident, node_iota, neg_first, dst_tab, srcT, dstT, counts)
            stage4(nc, gamma, beta, gate_w, gate_b, dispatched, x_all, acc, ident, mean_var, rstd, nmr, slots,
                   gates, taken)
        rows_l = sb("rows_l", [P, FFN_LIST], I32)
        expert_l = sb("expert_l", [P, FFN_LIST + 4], I32)
        passes_i = sb("passes_i", [P, 1], I32)
        stage5(nc, dispatched, taken, slots, rows_l, expert_l, passes_i)
        stage6(nc, w1, b1, w2, b2, dispatched, expert_out, ident, rows_l, expert_l, passes_i)
        stage7(nc, fgamma, fbeta, expert_out, out, x_all, mean_var, rstd, nmr, slots, gates)


def stage1(nc, x, src, dst, W, a_src, a_dst, table, x_all, acc, ident, node_iota, neg_first, mean_var, rstd, nmr,
           dst_tab, src_sc, srcT, dstT, tile_lo, tile_n, expert_out, zeroed):
    with ExitStack() as ctx:
        def sb(name, shape, dt=F32):
            return ctx.enter_context(nc.sbuf_tensor(name, shape, dt))

        def pb(name, shape, dt=F32):
            return ctx.enter_context(nc.psum_tensor(name, shape, dt))

        def sem(name):
            return ctx.enter_context(nc.semaphore(name))

        w_ext = sb("w_ext", [P, 2, PROJ])
        w_T = sb("w_T", [P, 2, D])
        a_col = sb("a_col", [P, 2, 2])
        a_blk = sb("a_blk", [P, 2, 2 * HEADS])
        stats = sb("stats", [P, GRP, 6])
        mv = sb("mv", [P, GRP, 2])
        spare = sb("spare", [P, 1])
        edges_i = sb("edges_i", [P, 2, CB, P], I32)
        edges_f = sb("edges_f", [P, 2, CB, P])
        chunk_min = sb("chunk_min", [P, CB])
        chunk_max = sb("chunk_max", [P, CB])
        chunk_no = sb("chunk_no", [P, CB])
        tile_first = sb("tile_first", [P, TILES])
        over_a = sb("over_a", [P, TILES, CB])
        over_b = sb("over_b", [P, TILES, CB])
        lohi = sb("lohi", [P, 2, TILES])
        lohi_r = sb("lohi_r", [P, 2, TILES])
        span_i = sb("span_i", [P, TILES], I32)
        odd_i = sb("odd_i", [P, TILES], I32)
        span = sb("span", [P, TILES])
        odd = sb("odd", [P, TILES])
        xn = sb("xn", [P, GRP, D])
        xnT = sb("xnT", [P, GRP, D])
        rows = sb("rows", [P, GRP, ROW])
        ps_t = [pb(f"ps_t{i}", [P, 512]) for i in range(2)]
        ps_h = [pb(f"ps_h{i}", [P, 512]) for i in range(2)]
        ps_e = [pb(f"ps_e{i}", [P, 512]) for i in range(2)]

        x_in = [sem(f"x_in{i}") for i in range(NGRP)]
        w_in = sem("w_in")
        edges_in = sem("edges_in")
        consts = sem("consts")
        acc_zero = sem("acc_zero")
        dve_chain = sem("dve_chain")
        edges_clear = sem("edges_clear")
        x_clear = sem("x_clear")
        var_ready = sem("var_ready")
        std_ready = sem("std_ready")
        norm_ready = sem("norm_ready")
        w_tr = sem("w_tr")
        w_tr_copied = sem("w_tr_copied")
        wa_done = sem("wa_done")
        wext_ready = sem("wext_ready")
        xn_ready = sem("xn_ready")
        xn_tr = sem("xn_tr")
        xnT_ready = sem("xnT_ready")
        proj_done = sem("proj_done")
        rows_ready = sem("rows_ready")
        rows_out = [sem(f"rows_out{k}") for k in range(GRP)]
        edges_f_ready = sem("edges_f_ready")
        edge_tr = sem("edge_tr")
        edge_tr_copied = sem("edge_tr_copied")
        lohi_ready = sem("lohi_ready")
        lohi_all = sem("lohi_all")

        block = ctx.enter_context(nc.Block())
        EG = (2 * CB + 3) // 4

        @block.sync
        def _(sp):
            sp.wait_ge(x_clear, 1)
            for g in range(NGRP):
                t0 = g * GRP
                nt = GRP if g < NGRP - 1 else GRP - 1
                sp.dma_start(x_all[:, t0:t0 + nt, :],
                             x[t0 * P:(t0 + nt) * P, :].rearrange("(t p) d -> p t d", p=P)).then_inc(x_in[g], 16)
            sp.dma_start(x_all[0:LAST, FULL, :], x[FULL * P:N, :]).then_inc(x_in[NGRP - 1], 16)
            for it in range(1):
                for k in range(GRP):
                    sp.wait_ge(rows_ready, k + 1)
                    sp.dma_start(table[k * P:(k + 1) * P, :], rows[:, k, :]).then_inc(rows_out[k], 16)
            with sp.Fori(1, NGRP) as it:
                for k in range(GRP):
                    sp.wait_ge(rows_ready, it * GRP + (k + 1))
                    sp.dma_start(table[bass.ds(it * (GRP * P) + k * P, P), :], rows[:, k, :]).then_inc(rows_out[k], 16)
            sp.wait_ge(acc_zero, 1)
            for t in range(0, FFN_TILES, ZERO_TILES):
                sp.dma_start(expert_out[t * P:(t + ZERO_TILES) * P, :].rearrange("(t p) d -> p t d", p=P),
                             acc[:, 0:ZERO_TILES, 0:D]).then_inc(zeroed, 16)
            for k in range(GRP):
                sp.wait_ge(rows_out[k], 16 * NGRP)

        @block.gpsimd
        def _(pool):
            pool.memset(ident[:, :], 0.0).then_inc(consts, 1)
            pool.memset(a_blk[:, :, :], 0.0).then_inc(consts, 1)
            pool.wait_ge(consts, 2)
            pool.affine_select(out=ident[:, :], in_=ident[:, :], compare_op=ALU.not_equal, fill=1.0, base=0,
                               pattern=[[-1, P]], channel_multiplier=1).then_inc(consts, 1)
            pool.iota(chunk_no[:, :], pattern=[[P, CB]], base=0, channel_multiplier=1,
                      allow_small_or_imprecise_dtypes=True).then_inc(consts, 1)
            pool.iota(tile_first[:, :], pattern=[[P, TILES]], base=0, channel_multiplier=0,
                      allow_small_or_imprecise_dtypes=True).then_inc(consts, 1)
            pool.iota(neg_first[:, :], pattern=[[-P, TILES]], base=0, channel_multiplier=0,
                      allow_small_or_imprecise_dtypes=True).then_inc(consts, 1)
            pool.iota(node_iota[:, :], pattern=[[1, P]], base=0, channel_multiplier=0,
                      allow_small_or_imprecise_dtypes=True).then_inc(consts, 1)
            pool.memset(acc[:, :, :], 0.0).then_inc(acc_zero, 1)
            pool.wait_ge(acc_zero, 1)
            pool.wait_ge(lohi_ready, 2)
            pool.partition_all_reduce(lohi_r[:, :, :], lohi[:, :, :], P, bass.bass_isa.ReduceOp.max).then_inc(lohi_all, 1)
            pool.wait_ge(lohi_all, 1)

        @block.scalar
        def _(act):
            act.dma_start(w_ext[:, :, 0:D], W.rearrange("(a p) n -> p a n", p=P)).then_inc(w_in, 16)
            act.dma_start(a_col[:, 0, :], a_src.rearrange("(a h) d -> (h d) a", a=2)).then_inc(w_in, 16)
            act.dma_start(a_col[:, 1, :], a_dst.rearrange("(a h) d -> (h d) a", a=2)).then_inc(w_in, 16)
            act.wait_ge(edges_clear, 1)
            for i, e in enumerate((src, dst)):
                act.dma_start(edges_i[:, i, 0:CB - 1, :],
                              e[0:(CB - 1) * P * P].rearrange("(b p e) -> p b e", p=P, e=P)).then_inc(edges_in, 16)
                lo = (CB - 1) * P * P
                act.dma_start(edges_i[0:CFULL % P, i, CB - 1, :],
                              e[lo:CFULL * P].rearrange("(p e) -> p e", e=P)).then_inc(edges_in, 16)
                act.dma_start(edges_i[CFULL % P:CFULL % P + 1, i, CB - 1, 0:CREST],
                              e[CFULL * P:E].rearrange("(p e) -> p e", p=1)).then_inc(edges_in, 16)
            for a in range(2):
                act.wait_ge(w_tr, a + 1)
                act.activation(w_T[:, a, :], ps_t[a][:, 0:D], ACT.Copy).then_inc(w_tr_copied, 1)
            for a in range(2):
                act.wait_ge(wa_done, a + 1)
                act.activation(w_ext[:, a, D:PROJ], ps_h[a][:, 0:2 * HEADS], ACT.Copy).then_inc(wext_ready, 1)
            act.wait_ge(var_ready, 1)
            act.activation(rstd[:, :], nmr[:, :], ACT.Sqrt).then_inc(std_ready, 1)
            act.wait_ge(norm_ready, 1)
            act.preload_act_table(ACT.Exp)

            def tile(k, g, first):
                t = g
                if not first:
                    act.wait_ge(xn_tr, g - (GRP - 1))
                act.activation(xn[:, k, :], x_all[:, bass.ds(t, 1), :].rearrange("p a d -> p (a d)"), ACT.Identity,
                               bias=nmr[:, bass.ds(t, 1)], scale=rstd[:, bass.ds(t, 1)]).then_inc(xn_ready, 1)
                act.wait_ge(xn_tr, g + 1)
                if not first:
                    act.wait_ge(proj_done, g - (GRP - 1))
                act.activation(xnT[:, k, :], ps_t[k % 2][:, 0:D], ACT.Copy).then_inc(xnT_ready, 1)

            for k in range(GRP):
                tile(k, k, True)
            with act.Fori(1, NGRP) as it:
                for k in range(GRP):
                    tile(k, it * GRP + k, False)

        @block.vector
        def _(dve):
            link = Chain(dve, dve_chain)
            dve.memset(x_all[:, FULL, :], 0.0).then_inc(x_clear, 1)
            dve.memset(edges_i[:, 0, CB - 1, :], 0)
            dve.memset(edges_i[:, 1, CB - 1, :], int(NODST)).then_inc(edges_clear, 1)
            dve.memset(srcT[:, PADC:COLS], 0)
            dve.memset(dstT[:, PADC:COLS], NODST)
            dve.wait_ge(w_in, 48)
            dve.wait_ge(consts, 2)
            for a in range(2):
                for q in range(4):
                    for s in range(2):
                        dve.tensor_copy(a_blk[q * HD:(q + 1) * HD, a, s * HEADS + 4 * a + q:s * HEADS + 4 * a + q + 1],
                                        a_col[q * HD:(q + 1) * HD, s, a:a + 1]).then_inc(edges_f_ready, 1)
            dve.wait_ge(edges_in, 96)
            for i in range(2):
                dve.tensor_copy(edges_f[:, i, :, :], edges_i[:, i, :, :]).then_inc(edges_f_ready, 1)
            for g in range(NGRP):
                dve.wait_ge(x_in[g], 16 if g < NGRP - 1 else 32)
            with dve.Fori(0, NGRP) as it:
                link.loop(it, 0, 3)
                for k in range(GRP):
                    st = dve.bn_stats(stats[:, k, :], x_all[:, bass.ds(it * GRP + k, 1), :].rearrange("p a d -> p (a d)"))
                link(st)
                dve.memset(spare[:, :], 0.0)
                for k in range(GRP):
                    aggr = dve.bn_aggr(mv[:, k, :], stats[:, k, :])
                link(aggr)
                link(dve.tensor_copy(mean_var[:, bass.ds(it * GRP, GRP), :], mv[:, :, :]))
            link.end(NGRP)
            dve.tensor_scalar(nmr[:, :], mean_var[:, :, 1], EPS, None, ALU.add).then_inc(var_ready, 1)
            dve.wait_ge(edges_f_ready, 18)
            dve.tensor_reduce(chunk_min[:, :], edges_f[:, 1, :, :], AX.X, ALU.min)
            link(dve.tensor_reduce(chunk_max[:, :], edges_f[:, 1, :, :], AX.X, ALU.max))
            dve.wait_ge(std_ready, 1)
            link(dve.reciprocal(rstd[:, :], rstd[:, :]))
            dve.scalar_tensor_tensor(nmr[:, :], mean_var[:, :, 0], -1.0, rstd[:, :], ALU.mult, ALU.mult).then_inc(norm_ready, 1)

            def per_tile(v):
                return v.unsqueeze(2).to_broadcast([P, TILES, CB])

            def per_chunk(v):
                return v.unsqueeze(1).to_broadcast([P, TILES, CB])

            def seg_steps():
                dve.wait_ge(consts, 7)
                dve.tensor_tensor(over_a[:, :, :], per_chunk(chunk_max[:, :]), per_tile(tile_first[:, :]), ALU.is_ge)
                link(dve.tensor_scalar(span[:, :], tile_first[:, :], float(P - 1), None, ALU.add))
                link(dve.tensor_tensor(over_b[:, :, :], per_chunk(chunk_min[:, :]), per_tile(span[:, :]), ALU.is_le))
                link(dve.tensor_tensor(over_a[:, :, :], over_a[:, :, :], over_b[:, :, :], ALU.mult))
                link(dve.tensor_scalar(chunk_max[:, :], chunk_no[:, :], 1.0, None, ALU.add))
                link(dve.tensor_tensor(over_b[:, :, :], over_a[:, :, :], per_chunk(chunk_max[:, :]), ALU.mult))
                link(dve.tensor_reduce(lohi[:, 1, :], over_b[:, :, :], AX.X, ALU.max))
                link(dve.tensor_scalar(chunk_max[:, :], chunk_no[:, :], -1.0, 4096.0, ALU.mult, ALU.add))
                link(dve.tensor_tensor(over_b[:, :, :], over_a[:, :, :], per_chunk(chunk_max[:, :]), ALU.mult))
                dve.tensor_reduce(lohi[:, 0, :], over_b[:, :, :], AX.X, ALU.max).then_inc(lohi_ready, 2)

            seg_steps()

            def tile(k, g, first):
                dve.wait_ge(proj_done, g + 1)
                if not first:
                    dve.wait_ge(rows_out[k], 16 * it)
                dve.tensor_copy(rows[:, k, 0:SUM], ps_h[k % 2][:, 0:SUM])
                dve.tensor_scalar(rows[:, k, SUM:ROW], ps_h[k % 2][:, D:SUM], SLOPE, None, ALU.mult)
                dve.tensor_copy(src_sc[:, bass.ds(g, 1), :].rearrange("p a d -> p (a d)"), ps_h[k % 2][:, D:SUM])
                dve.tensor_copy(dst_tab[:, bass.ds(g, 1), 0:HEADS].rearrange("p a d -> p (a d)"),
                                ps_h[k % 2][:, SUM:PROJ]).then_inc(rows_ready, 1)

            for k in range(GRP):
                tile(k, k, True)
            with dve.Fori(1, NGRP) as it:
                for k in range(GRP):
                    tile(k, it * GRP + k, False)
            for q in range(EG):
                dve.wait_ge(edge_tr, min(4 * q + 4, 2 * CB))
                for j in range(4 * q, min(4 * q + 4, 2 * CB)):
                    to = (srcT if j < CB else dstT)[:, (j % CB) * P:(j % CB + 1) * P]
                    last = dve.tensor_copy(to, ps_e[q % 2][:, (j % 4) * P:(j % 4 + 1) * P])
                last.then_inc(edge_tr_copied, 1)
            dve.wait_ge(edge_tr_copied, EG)
            dve.wait_ge(lohi_all, 1)
            link(dve.tensor_scalar(tile_lo[:, :], lohi_r[:, 0, :], -1.0, 4096.0, ALU.mult, ALU.add))
            link(dve.tensor_tensor(span[:, :], lohi_r[:, 1, :], tile_lo[:, :], ALU.subtract))
            link(dve.tensor_scalar(span[:, :], span[:, :], 0.0, None, ALU.max))
            link(dve.tensor_copy(span_i[:, :], span[:, :]))
            link(dve.tensor_scalar(odd_i[:, :], span_i[:, :], 1, None, ALU.bitwise_and))
            link(dve.tensor_copy(odd[:, :], odd_i[:, :]))
            link(dve.tensor_tensor(span[:, :], span[:, :], odd[:, :], ALU.add))
            link(dve.tensor_scalar(tile_n[:, :], span[:, :], 0.5, None, ALU.mult))

        @block.tensor
        def _(pe):
            pe.wait_ge(consts, 3)
            pe.wait_ge(w_in, 48)
            for j in range(2):
                for k in range(2):
                    last = pe.transpose(ps_t[j][:, k * P:(k + 1) * P], w_ext[:, k, j * P:(j + 1) * P], ident[:, :])
                last.then_inc(w_tr, 1)
            pe.wait_ge(w_tr_copied, 2)
            pe.wait_ge(edges_f_ready, 16)
            for k in range(2):
                for j in range(2):
                    last = pe.matmul(ps_h[k][:, 0:2 * HEADS], w_T[:, j, k * P:(k + 1) * P], a_blk[:, j, :],
                                     start=(j == 0), stop=(j == 1))
                last.then_inc(wa_done, 1)
            pe.wait_ge(wext_ready, 2)

            def tile(k, g, first):
                pe.wait_ge(xn_ready, g + 1)
                if not (first and k < 2):
                    pe.wait_ge(xnT_ready, g - 1 if k else g)
                for a in range(2):
                    last = pe.transpose(ps_t[k % 2][:, a * P:(a + 1) * P], xn[:, k, a * P:(a + 1) * P], ident[:, :])
                last.then_inc(xn_tr, 1)
                pe.wait_ge(xnT_ready, g + 1)
                if not (first and k < 2):
                    pe.wait_ge(rows_ready, g - 1 if k else g)
                for a in range(2):
                    last = pe.matmul(ps_h[k % 2][:, 0:PROJ], xnT[:, k, a * P:(a + 1) * P], w_ext[:, a, :],
                                     start=(a == 0), stop=(a == 1))
                last.then_inc(proj_done, 1)

            for k in range(GRP):
                tile(k, k, True)
            with pe.Fori(1, NGRP) as it:
                for k in range(GRP):
                    tile(k, it * GRP + k, False)
            pe.wait_ge(edges_f_ready, 18)
            for q in range(EG):
                if q >= 2:
                    pe.wait_ge(edge_tr_copied, q - 1)
                for j in range(4 * q, min(4 * q + 4, 2 * CB)):
                    pe.transpose(ps_e[q % 2][:, (j % 4) * P:(j % 4 + 1) * P], edges_f[:, j // CB, j % CB, :],
                                 ident[:, :]).then_inc(edge_tr, 1)


def stage2(nc, schedule, zeroed, dst_tab, src_sc, tile_lo, tile_n, counts):
    with ExitStack() as ctx:
        def sb(name, shape, dt=F32):
            return ctx.enter_context(nc.sbuf_tensor(name, shape, dt))

        def sem(name):
            return ctx.enter_context(nc.semaphore(name))

        B = TILES + 1
        K = IBLK // P
        assert K == BODY
        first = sb("first", [P, B])
        ones = sb("ones", [P, TILES])
        key = sb("key", [P, B])
        delta = sb("delta", [P, B])
        delta3 = sb("delta3", [P, B])
        step_no = sb("step_no", [P, K])
        step_cur = sb("step_cur", [P, K])
        ge = sb("ge", [P, K, B])
        res = sb("res", [P, K])
        res_i = sb("res_i", [P, LISTS, K], I32)
        blk_f = sb("blk_f", [P, 4])
        best = sb("best", [P, 2, HEADS])
        best_all = sb("best_all", [P, 2, HEADS])
        leak = sb("leak", [P, TILES, HEADS])
        dve_chain = sem("dve_chain2")
        iotas = sem("iotas")
        best_ready = sem("best_ready")
        best_reduced = sem("best_reduced")
        bound_steps = sem("bound_steps")
        counts_ready = sem("counts_ready")
        list_ready = sem("list_ready")
        list_out = sem("list_out")
        list_kept = sem("list_kept")
        block = ctx.enter_context(nc.Block())

        @block.gpsimd
        def _(pool):
            pool.iota(step_no[:, :], pattern=[[1, K]], base=0, channel_multiplier=K,
                      allow_small_or_imprecise_dtypes=True).then_inc(iotas, 1)
            pool.wait_ge(best_ready, 1)
            pool.partition_all_reduce(best_all[:, :, :], best[:, :, :], P, bass.bass_isa.ReduceOp.max).then_inc(best_reduced, 1)

        @block.vector
        def _(dve):
            link = Chain(dve, dve_chain)
            dve.tensor_reduce(best[:, 0, :], src_sc[:, :, :].rearrange("p t h -> p h t"), AX.X, ALU.max)
            link(dve.tensor_reduce(best[:, 1, :], src_sc[:, :, :].rearrange("p t h -> p h t"), AX.X, ALU.min))
            dve.tensor_scalar(best[:, 1, :], best[:, 1, :], -1.0, None, ALU.mult).then_inc(best_ready, 1)
            dve.memset(ones[:, :], 1.0)
            link(dve.memset(first[:, 0:1], 0.0))
            link(dve.tensor_tensor_scan(first[:, 1:B], ones[:, :], tile_n[:, :], 0.0, ALU.mult, ALU.add))
            link(dve.scalar_tensor_tensor(key[:, 0:TILES], first[:, 0:TILES], -2.0, tile_lo[:, :], ALU.mult, ALU.add))
            link(dve.tensor_scalar(key[:, TILES:B], first[:, TILES:B], -2.0, float(PADC), ALU.mult, ALU.add))
            link(dve.tensor_copy(delta[:, 0:1], key[:, 0:1]))
            link(dve.tensor_tensor(delta[:, 1:B], key[:, 1:B], key[:, 0:TILES], ALU.subtract))
            link(dve.tensor_scalar(blk_f[:, 0:1], first[:, TILES:B], 1.0, None, ALU.mult))
            link(dve.tensor_copy(counts[:, 3:4], blk_f[:, 0:1]))
            link(dve.tensor_scalar(blk_f[:, 1:2], blk_f[:, 0:1], float(JOIN + BODY - 1), None, ALU.add))
            link(dve.tensor_scalar(blk_f[:, 2:3], blk_f[:, 0:1], float(SLACK + IBLK), None, ALU.add))
            link(dve.tensor_copy(counts[:, 0:2], blk_f[:, 1:3]))
            shift = BODY.bit_length() - 1
            link(dve.tensor_scalar(counts[:, 0:1], counts[:, 0:1], shift, None, ALU.arith_shift_right))
            dve.tensor_scalar(counts[:, 1:2], counts[:, 1:2], 10, None, ALU.arith_shift_right).then_inc(counts_ready, 1)
            dve.wait_ge(counts_ready, 1)
            dve.wait_ge(iotas, 1)
            blocks = dve.value_load(counts[0:1, 1:2], min_val=1, max_val=IBLKS)

            def tiles(v):
                return v.unsqueeze(1).to_broadcast([P, K, B])

            def steps(v):
                return v.unsqueeze(2).to_broadcast([P, K, B])

            per = 2 + sum(6 if chunk else 4 for _, chunk in LIST_OF)
            with dve.Fori(0, blocks) as b:
                link.loop(b, 0, per)
                for q, (shift, chunk) in enumerate(LIST_OF):
                    link(dve.tensor_scalar(step_cur[:, :], step_no[:, :], float(shift), None, ALU.add))
                    link(dve.tensor_tensor(ge[:, :, :], steps(step_cur[:, :]), tiles(first[:, :]), ALU.is_ge))
                    if chunk:
                        link(dve.tensor_tensor(ge[:, :, :], ge[:, :, :], tiles(delta[:, :]), ALU.mult))
                        link(dve.tensor_reduce(res[:, :], ge[:, :, :], AX.X, ALU.add))
                        link(dve.scalar_tensor_tensor(res[:, :], step_cur[:, :], 2.0, res[:, :], ALU.mult, ALU.add))
                        link(dve.tensor_scalar(res_i[:, q, :], res[:, :], float(PADC + 4), None, ALU.min))
                    else:
                        link(dve.tensor_reduce(res[:, :], ge[:, :, 1:B], AX.X, ALU.add))
                        link(dve.tensor_scalar(res_i[:, q, :], res[:, :], float(TILES - 1), None, ALU.min))
                link(dve.tensor_scalar(step_no[:, :], step_no[:, :], float(IBLK), None, ALU.add))
                dve.memset(blk_f[:, 3:4], 0.0).then_inc(list_ready, 1)
                dve.wait_ge(list_out, 16 * b + 16)
                link(dve.memset(blk_f[:, 2:3], 0.0))
            dve.wait_ge(best_reduced, 1)
            link.end(blocks)
            dve.tensor_tensor(leak[:, :, :], dst_tab[:, :, 0:HEADS],
                              best_all[:, 0, :].unsqueeze(1).to_broadcast([P, TILES, HEADS]), ALU.add).then_inc(bound_steps, 1)
            dve.wait_ge(bound_steps, 1)
            link(dve.scalar_tensor_tensor(leak[:, :, :], leak[:, :, :], SLOPE, leak[:, :, :], ALU.mult, ALU.max))
            link(dve.scalar_tensor_tensor(dst_tab[:, :, HEADS:2 * HEADS], dst_tab[:, :, 0:HEADS], SLOPE, leak[:, :, :],
                                          ALU.mult, ALU.subtract))
            dve.tensor_tensor(dst_tab[:, :, 0:HEADS], dst_tab[:, :, 0:HEADS], leak[:, :, :],
                              ALU.subtract).then_inc(bound_steps, 1)
            dve.wait_ge(bound_steps, 2)

        @block.sync
        def _(sp):
            sp.wait_ge(counts_ready, 1)
            blocks = sp.value_load(counts[0:1, 1:2], min_val=1, max_val=IBLKS)
            with sp.Fori(0, blocks) as b:
                sp.wait_ge(list_ready, b + 1)
                sp.dma_start(schedule[bass.ds(b * P, P), :], res_i[:, :, :].rearrange("p q k -> p (q k)")).then_inc(list_out, 16)
            sp.wait_ge(list_out, 16 * blocks)
            sp.sem_inc(list_kept, 1)
            sp.wait_ge(zeroed, 16 * (FFN_TILES // ZERO_TILES))


def stage3(nc, table, schedule, acc, ident, node_iota, neg_first, dst_tab, srcT,
           dstT, counts):
    with ExitStack() as ctx:
        def sb(name, shape, dt=F32):
            return ctx.enter_context(nc.sbuf_tensor(name, shape, dt))

        def pb(name, shape, dt=F32):
            return ctx.enter_context(nc.psum_tensor(name, shape, dt))

        def sem(name):
            return ctx.enter_context(nc.semaphore(name))

        MSGS = 4
        MAXBODY = (MAXSTEPS + JOIN + BODY - 1) // BODY
        gat = sb("gat", [P, BODY, 2, ROW])
        idx = sb("idx", [P, BODY, 2], I32)
        rel = sb("rel", [P, BODY, 2])
        lists = sb("lists", [1, RING, LISTS, BODY], I32)
        hot = sb("hot", [P, BODY, 2, P])
        hotT = sb("hotT", [P, 2, 2, P])
        both = sb("both", [P, 2, 2, 2 * HEADS])
        score = sb("score", [P, 2, 2, HEADS])
        msg = sb("msg", [P, MSGS, 2, SUM])
        ps_hot = [pb(f"ps_hot{i}", [P, 512]) for i in range(2)]
        ps_look = [pb(f"ps_look{i}", [P, 512]) for i in range(2)]
        ps_sum = [pb(f"ps_sum{i}", [P, 512]) for i in range(2)]
        landed = [sem(f"landed{k}") for k in range(BODY)]
        lists_in = sem("lists_in")
        rows_landed = sem("rows_landed")
        idx_ready = sem("idx_ready")
        rel_ready = sem("rel_ready")
        pool_turn = sem("pool_turn")
        sp_turn = sem("sp_turn")
        hot_ready = sem("hot_ready")
        hot_tr = sem("hot_tr")
        hotT_ready = sem("hotT_ready")
        look_done = sem("look_done")
        both_ready = sem("both_ready")
        score_ready = sem("score_ready")
        weight_ready = sem("weight_ready")
        msg_ready = sem("msg_ready")
        sum_done = sem("sum_done")
        added = sem("added")
        block = ctx.enter_context(nc.Block())

        def registers(eng, name):
            return [eng.alloc_register(f"{name}{k}") for k in range(BODY)]

        def load_list(eng, regs, which, it):
            at = (it & (RING - 1)) * (LISTS * BODY) + which * BODY
            flat = lists[:, :, :, :].rearrange("o r l k -> o (r l k)")
            for k in range(0, BODY, 4):
                eng.load(regs[k:k + 4], flat[0:1, bass.ds(at + k, 4)])

        def chunk_of(eng, reg):
            return eng.snap(reg, min_val=0, max_val=PADC + 4)

        def tile_of(eng, reg):
            return eng.snap(reg, min_val=0, max_val=TILES - 1)

        def body_count(eng):
            return eng.value_load(counts[0:1, 0:1], min_val=2, max_val=MAXBODY)

        @block.gpsimd
        def _(pool):
            bodies = body_count(pool)

            def step(k, g, head):
                if not head:
                    pool.wait_ge(msg_ready, g - (BODY - 1))
                pool.wait_ge(idx_ready, g + 1)
                pool.sem_inc(pool_turn, 1)
                for j in range(2):
                    pool.indirect_dma_start(gat[:, k, j, :], None, table,
                                            bass.IndirectOffsetOnAxis(ap=idx[:, k, j:j + 1], axis=0)).then_inc(landed[k], 16)

            for k in range(BODY):
                step(k, k, True)
            with pool.Fori(1, bodies) as it:
                for k in range(BODY):
                    step(k, it * BODY + k, False)

        @block.sync
        def _(sp):
            bodies = body_count(sp)
            sp.dma_start(lists[0:1, 0:2, :, :].rearrange("o r l k -> o (r l k)"),
                         schedule[0:2, :].rearrange("(o r) n -> o (r n)", o=1)).then_inc(lists_in, 32)
            with sp.Fori(0, bodies) as it:
                sp.wait_ge(lists_in, it * 16 + 32)
                sp.sem_inc(sp_turn, 1)
                sp.dma_start(lists[:, :, :, :].rearrange("o r l k -> o r (l k)")[0:1, bass.ds((it + 2) & (RING - 1), 1), :],
                             schedule[bass.ds(it + 2, 1), :].unsqueeze(0)).then_inc(lists_in, 16)
                for k in range(BODY):
                    sp.wait_ge(landed[k], it * 32 + 32)
                    sp.sem_inc(rows_landed, 1)
            sp.wait_ge(lists_in, bodies * 16 + 32)
            sp.sem_inc(sp_turn, 1)

        @block.scalar
        def _(act):
            act.preload_act_table(ACT.Exp)
            chunks, tiles = registers(act, "next_chunk"), registers(act, "next_tile")
            bodies = body_count(act)
            act.wait_ge(lists_in, 32)

            def lay_out(slot, chunk, tile):
                c, t = chunk_of(act, chunk), tile_of(act, tile)
                act.activation(idx[:, slot, :], srcT[:, bass.ds(c, 2)], ACT.Copy).then_inc(idx_ready, 1)
                act.activation(rel[:, slot, :], dstT[:, bass.ds(c, 2)], ACT.Identity, bias=neg_first[:, bass.ds(t, 1)]).then_inc(rel_ready, 1)

            load_list(act, chunks, CHUNK, 0)
            load_list(act, tiles, TILE, 0)
            for k in range(AHEAD):
                lay_out(k, chunks[k], tiles[k])

            def step(k, g, head):
                if not (head and k < WEIGH):
                    act.wait_ge(score_ready, g - WEIGH + 1)
                    if not (head and k < WEIGH + MSGS):
                        act.wait_ge(sum_done, g - WEIGH - MSGS + 1)
                    m = (k - WEIGH) % MSGS
                    act.activation(msg[:, m, :, D:SUM], score[:, m % 2, :, :], ACT.Exp).then_inc(weight_ready, 1)
                act.wait_ge(hot_tr, g + 1)
                if not (head and k < 2):
                    act.wait_ge(look_done, g - 1)
                act.activation(hotT[:, k % 2, :, :].rearrange("p a b -> p (a b)"), ps_hot[k % 2][:, 0:2 * P],
                               ACT.Copy).then_inc(hotT_ready, 1)
                if not (head and k < BODY - AHEAD):
                    act.wait_ge(rows_landed, g - (BODY - AHEAD) + 1)
                lay_out((k + AHEAD) % BODY, chunks[k], tiles[k])

            def body(it, head):
                load_list(act, chunks, NEXT_CHUNK, it)
                load_list(act, tiles, NEXT_TILE, it)
                for k in range(BODY):
                    step(k, it * BODY + k, head)

            body(0, True)
            with act.Fori(1, bodies) as it:
                act.wait_ge(lists_in, it * 16 + 16)
                body(it, False)

        @block.tensor
        def _(pe):
            tiles = registers(pe, "tile")
            bodies = body_count(pe)
            pe.wait_ge(lists_in, 32)

            def look(k, g, head, tile):
                pe.wait_ge(hotT_ready, g + 1)
                if not (head and k < 2):
                    pe.wait_ge(both_ready, g - 1)
                for j in range(2):
                    last = pe.matmul(ps_look[k % 2][:, j * 2 * HEADS:(j + 1) * 2 * HEADS], hotT[:, k % 2, j, :],
                                     dst_tab[:, bass.ds(tile_of(pe, tile), 1), :].rearrange("p a b -> p (a b)"),
                                     start=True, stop=True)
                last.then_inc(look_done, 1)

            def step(k, g, head):
                pe.wait_ge(hot_ready, g + 1)
                if not (head and k < 2):
                    pe.wait_ge(hotT_ready, g - 1)
                for j in range(2):
                    last = pe.transpose(ps_hot[k % 2][:, j * P:(j + 1) * P], hot[:, k, j, :], ident[:, :])
                last.then_inc(hot_tr, 1)
                if not (head and k < 1):
                    look((k - 1) % BODY, g - 1, head, tiles[k])
                if not (head and k < SUMS):
                    pe.wait_ge(msg_ready, g - SUMS + 1)
                    if not (head and k < SUMS + 2):
                        pe.wait_ge(added, g - SUMS - 1)
                    for j in range(2):
                        last = pe.matmul(ps_sum[(k - SUMS) % 2][:, 0:SUM], hot[:, (k - SUMS) % BODY, j, :],
                                         msg[:, (k - SUMS) % MSGS, j, :], start=(j == 0), stop=(j == 1))
                    last.then_inc(sum_done, 1)

            def body(it, head):
                load_list(pe, tiles, LOOK_TILE, it)
                for k in range(BODY):
                    step(k, it * BODY + k, head)

            body(0, True)
            with pe.Fori(1, bodies) as it:
                pe.wait_ge(lists_in, it * 16 + 16)
                body(it, False)

        @block.vector
        def _(dve):
            olds = registers(dve, "old_tile")
            bodies = body_count(dve)
            dve.wait_ge(lists_in, 32)

            def step(k, g, head):
                m = (k - WEIGH) % MSGS
                if not (head and k < WEIGH):
                    dve.wait_ge(rows_landed, g - WEIGH + 1)
                    dve.wait_ge(look_done, g - WEIGH + 1)
                    dve.tensor_tensor(both[:, m % 2, :, :], gat[:, (k - WEIGH) % BODY, :, D:ROW],
                                      ps_look[m % 2][:, 0:4 * HEADS].rearrange("p (j s) -> p j s", j=2),
                                      ALU.add).then_inc(both_ready, 1)
                dve.wait_ge(rel_ready, g + 1)
                if not (head and k < BODY):
                    dve.wait_ge(sum_done, g - BODY + 1)
                dve.tensor_tensor(hot[:, k, :, :], node_iota[:, :].unsqueeze(1).to_broadcast([P, 2, P]),
                                  rel[:, k, :].unsqueeze(2).to_broadcast([P, 2, P]), ALU.is_equal).then_inc(hot_ready, 1)
                if head and k < WEIGH:
                    return
                dve.wait_ge(both_ready, g - WEIGH + 1)
                dve.tensor_tensor(score[:, m % 2, :, :], both[:, m % 2, :, 0:HEADS], both[:, m % 2, :, HEADS:2 * HEADS],
                                  ALU.max).then_inc(score_ready, 1)
                if not (head and k < JOIN):
                    o = tile_of(dve, olds[k])
                    dve.wait_ge(sum_done, g - JOIN + 1)
                    if not (head and k < JOIN + 1):
                        dve.wait_ge(added, g - JOIN)
                    to = acc[:, bass.ds(o, 1), :].rearrange("p a b -> p (a b)")
                    dve.tensor_tensor(to, to, ps_sum[(k - JOIN) % 2][:, 0:SUM], ALU.add).then_inc(added, 1)
                dve.wait_ge(weight_ready, g - WEIGH + 1)
                dve.tensor_tensor(msg[:, m, :, 0:D].rearrange("p j (h d) -> p j h d", d=HD),
                                  gat[:, (k - WEIGH) % BODY, :, 0:D].rearrange("p j (h d) -> p j h d", d=HD),
                                  msg[:, m, :, D:SUM].unsqueeze(3).to_broadcast([P, 2, HEADS, HD]),
                                  ALU.mult).then_inc(msg_ready, 1)

            def body(it, head):
                load_list(dve, olds, OLD_TILE, it)
                for k in range(BODY):
                    step(k, it * BODY + k, head)

            body(0, True)
            with dve.Fori(1, bodies) as it:
                dve.wait_ge(lists_in, it * 16 + 16)
                body(it, False)


def spread_tiles(v, n=GRP):
    return v.unsqueeze(1).to_broadcast([P, n, D])


def group_stats(dve, link, source, stats, mv, spare, mean_var, it):
    dve.memset(spare[:, 1:2], 0.0)
    for k in range(GRP):
        last = dve.bn_stats(stats[:, k, :], source(k))
    link(last)
    dve.memset(spare[:, 1:2], 0.0)
    for k in range(GRP):
        last = dve.bn_aggr(mv[:, k, :], stats[:, k, :])
    link(last)
    link(dve.tensor_copy(mean_var[:, bass.ds(it * GRP, GRP), :], mv[:, :, :]))


def one(v):
    return v.rearrange("p a d -> p (a d)")


def stage4(nc, gamma, beta, gate_w, gate_b, dispatched, x_all, acc, ident, mean_var, rstd, nmr, slots, gates, taken):
    with ExitStack() as ctx:
        def sb(name, shape, dt=F32):
            return ctx.enter_context(nc.sbuf_tensor(name, shape, dt))

        def pb(name, shape, dt=F32):
            return ctx.enter_context(nc.psum_tensor(name, shape, dt))

        def sem(name):
            return ctx.enter_context(nc.semaphore(name))

        gam = sb("gam", [P, D])
        bet = sb("bet", [P, D])
        gw = sb("gw", [P, KD, EXPERTS])
        gb = sb("gb", [1, EXPERTS])
        ones_row = sb("ones_row", [1, P])
        ones_sq = sb("ones_sq", [P, P], BF16)
        before = sb("before", [P, P], BF16)
        expert_no = sb("expert_no", [P, EXPERTS])
        expert_row = sb("expert_row", [P, EXPERTS])
        row_no = sb("row_no", [P, 2, GRP])
        valid = sb("valid", [P, TILES])
        pads = sb("pads", [P, TILES, 2])
        stats = sb("stats4", [P, GRP, 6])
        mv = sb("mv4", [P, GRP, 2])
        spare = sb("spare4", [P, 2])
        rden = sb("rden", [P, GRP, HEADS])
        grp_a = sb("grp_a", [P, GRP, D])
        grp_b = sb("grp_b", [P, GRP, D])
        yT = sb("yT", [P, GRP, D])
        top = sb("top", [P, GRP, 8])
        top_i = sb("top_i", [P, GRP, 8], U32)
        top_f = sb("top_f", [P, GRP, 2])
        logits = sb("logits", [P, GRP, EXPERTS])
        diff = sb("diff", [P, GRP])
        ediff = sb("ediff", [P, GRP])
        rsum = sb("rsum", [P, GRP])
        pick = sb("pick", [P, 2, GRP, EXPERTS])
        both = sb("both4", [P, GRP, EXPERTS])
        both_h = sb("both_h", [P, GRP, EXPERTS], BF16)
        base = sb("base", [P, GRP + 1, EXPERTS])
        place = sb("place", [P, GRP, EXPERTS])
        hit = sb("hit", [P, 2, GRP, EXPERTS])
        slot_f = sb("slot_f", [P, 2, GRP])
        slot_g = sb("slot_g", [P, 2, GRP], I32)
        ps_t = [pb(f"ps4_t{i}", [P, 512]) for i in range(2)]
        ps_l = pb("ps4_l", [P, 512])
        ps_before = pb("ps4_before", [P, 512])
        ps_total = pb("ps4_total", [P, 512])

        par_in = sem("par_in")
        consts = sem("consts4")
        dve_chain = sem("dve_chain4")
        norm_a = sem("norm_a")
        norm_a_used = sem("norm_a_used")
        var2 = sem("var2")
        std2 = sem("std2")
        scale2 = sem("scale2")
        norm_b = sem("norm_b")
        low_ready = sem("low_ready")
        exp_ready = sem("exp_ready")
        norm_b_used = sem("norm_b_used")
        var3 = sem("var3")
        std3 = sem("std3")
        scale3 = sem("scale3")
        y_ready = sem("y_ready")
        y_tr = sem("y_tr")
        yT_ready = sem("yT_ready")
        logits_done = sem("logits_done")
        logits_read = sem("logits_read")
        diff_ready = sem("diff_ready")
        ediff_ready = sem("ediff_ready")
        both_ready = sem("both_ready4")
        ranks_done = sem("ranks_done")
        slots_ready = sem("slots_ready")
        pool_turn = sem("pool_turn4")
        sent = [sem(f"sent{k}") for k in range(GRP)]
        block = ctx.enter_context(nc.Block())

        def tile(k, it):
            return bass.ds(it * GRP + k, 1)

        def group(it):
            return bass.ds(it * GRP, GRP)

        @block.sync
        def _(sp):
            sp.dma_start(gam[:, :], gamma.unsqueeze(0).to_broadcast([P, D])).then_inc(par_in, 16)
            sp.dma_start(bet[:, :], beta.unsqueeze(0).to_broadcast([P, D])).then_inc(par_in, 16)
            sp.dma_start(gw[:, :, :], gate_w.rearrange("(a p) e -> p a e", p=P)).then_inc(par_in, 16)
            sp.dma_start(gb[:, :], gate_b.unsqueeze(0)).then_inc(par_in, 16)

        @block.gpsimd
        def _(pool):
            pool.memset(ones_row[:, :], 1.0).then_inc(consts, 1)
            pool.memset(ones_sq[:, :], 1.0).then_inc(consts, 1)
            pool.memset(before[:, :], 1.0).then_inc(consts, 1)
            pool.memset(valid[:, :], 1.0).then_inc(consts, 1)
            pool.memset(pads[:, :, :], 0.0).then_inc(consts, 1)
            pool.memset(base[:, 0, :], 0.0).then_inc(consts, 1)
            pool.iota(expert_no[:, :], pattern=[[1, EXPERTS]], base=0, channel_multiplier=0,
                      allow_small_or_imprecise_dtypes=True).then_inc(consts, 1)
            pool.iota(expert_row[:, :], pattern=[[CAP, EXPERTS]], base=0, channel_multiplier=0,
                      allow_small_or_imprecise_dtypes=True).then_inc(consts, 1)
            pool.wait_ge(consts, 8)
            pool.affine_select(out=before[:, :], in_=before[:, :], compare_op=ALU.is_gt, fill=0.0, base=0,
                               pattern=[[1, P]], channel_multiplier=-1).then_inc(consts, 1)
            pool.affine_select(out=valid[:, FULL:TILES], in_=valid[:, FULL:TILES], compare_op=ALU.is_gt, fill=0.0,
                               base=LAST, pattern=[[0, 1]], channel_multiplier=-1).then_inc(consts, 1)
            pool.iota(pads[:, FULL, :], pattern=[[P, 2]], base=PADROWS, channel_multiplier=1,
                      allow_small_or_imprecise_dtypes=True).then_inc(consts, 1)
            pool.wait_ge(consts, 11)
            pool.affine_select(out=pads[:, FULL, :], in_=pads[:, FULL, :], compare_op=ALU.is_ge, fill=0.0,
                               base=-LAST, pattern=[[0, 2]], channel_multiplier=1).then_inc(consts, 1)
            pool.wait_ge(consts, 12)
            with pool.Fori(0, NGRP) as it:
                pool.wait_ge(slots_ready, it + 1)
                pool.sem_inc(pool_turn, 1)
                for k in range(GRP):
                    for c in range(2):
                        pool.indirect_dma_start(dispatched, bass.IndirectOffsetOnAxis(ap=slot_g[:, c, k:k + 1], axis=0),
                                                grp_a[:, k, :], None).then_inc(sent[k], 16)
            for k in range(GRP):
                pool.wait_ge(sent[k], 32 * NGRP)

        @block.scalar
        def _(act):
            with act.Fori(0, NGRP) as it:
                for k in range(GRP):
                    act.wait_ge(norm_a_used, it + 1)
                    act.activation(grp_a[:, k, :], one(x_all[:, tile(k, it), :]), ACT.Identity,
                                   bias=nmr[:, tile(k, it)], scale=rstd[:, tile(k, it)]).then_inc(norm_a, 1)
            act.wait_ge(var2, 1)
            act.activation(rstd[:, :], nmr[:, :], ACT.Sqrt).then_inc(std2, 1)
            act.wait_ge(scale2, 1)
            act.preload_act_table(ACT.Exp)
            with act.Fori(0, NGRP) as it:
                for k in range(GRP):
                    act.wait_ge(norm_b_used, it + 1)
                    act.activation(grp_a[:, k, :], acc[:, tile(k, it), 0:D].rearrange("p a d -> p (a d)"), ACT.Identity,
                                   bias=nmr[:, tile(k, it)], scale=rstd[:, tile(k, it)]).then_inc(norm_b, 1)
                act.wait_ge(low_ready, it + 1)
                act.activation(grp_b[:, :, :], grp_b[:, :, :], ACT.Exp).then_inc(exp_ready, 1)
            act.wait_ge(var3, 1)
            act.activation(rstd[:, :], nmr[:, :], ACT.Sqrt).then_inc(std3, 1)
            act.wait_ge(scale3, 1)
            act.preload_act_table(ACT.Exp)

            def router(it, head):
                for k in range(GRP):
                    if not head:
                        act.wait_ge(sent[k], 32 * it)
                    act.activation(grp_a[:, k, :], one(x_all[:, tile(k, it), :]), ACT.Identity,
                                   bias=nmr[:, tile(k, it)], scale=rstd[:, tile(k, it)]).then_inc(y_ready, 1)
                    act.wait_ge(y_tr, it * GRP + k + 1)
                    if not head:
                        act.wait_ge(logits_done, it)
                    act.activation(yT[:, k, :], ps_t[k % 2][:, 0:D], ACT.Copy).then_inc(yT_ready, 1)
                act.wait_ge(diff_ready, it + 1)
                act.activation(ediff[:, :], diff[:, :], ACT.Exp).then_inc(ediff_ready, 1)

            router(0, True)
            with act.Fori(1, NGRP) as it:
                router(it, False)

        @block.tensor
        def _(pe):
            pe.wait_ge(par_in, 64)
            pe.wait_ge(consts, 12)

            def router(it, head):
                if not head:
                    pe.wait_ge(logits_read, it)
                for k in range(GRP):
                    pe.wait_ge(y_ready, it * GRP + k + 1)
                    if not (head and k < 2):
                        pe.wait_ge(yT_ready, it * GRP + k - (1 if k else 0))
                    for a in range(KD):
                        last = pe.transpose(ps_t[k % 2][:, a * P:(a + 1) * P], grp_a[:, k, a * P:(a + 1) * P], ident[:, :])
                    last.then_inc(y_tr, 1)
                    pe.wait_ge(yT_ready, it * GRP + k + 1)
                    to = ps_l[:, k * EXPERTS:(k + 1) * EXPERTS]
                    pe.matmul(to, yT[:, k, 0:P], gw[:, 0, :], start=True, stop=False)
                    pe.matmul(to, yT[:, k, P:D], gw[:, 1, :], start=False, stop=False)
                    last = pe.matmul(to, ones_row[:, :], gb[:, :], start=False, stop=True)
                last.then_inc(logits_done, 1)
                pe.wait_ge(both_ready, it + 1)
                flat = both_h[:, :, :].rearrange("p k e -> p (k e)")
                pe.matmul(ps_before[:, 0:GRP * EXPERTS], before[:, :], flat, start=True, stop=True)
                pe.matmul(ps_total[:, 0:GRP * EXPERTS], ones_sq[:, :], flat, start=True, stop=True).then_inc(ranks_done, 1)

            router(0, True)
            with pe.Fori(1, NGRP) as it:
                router(it, False)

        @block.vector
        def _(dve):
            link = Chain(dve, dve_chain)
            dve.memset(spare[:, 0:1], 0.0).then_inc(norm_a_used, 1)
            with dve.Fori(0, NGRP) as it:
                link.loop(it, 0, 8)
                link(dve.tensor_scalar(rden[:, :, :], acc[:, group(it), D:SUM], 1e-30, None, ALU.max))
                link(dve.reciprocal(rden[:, :, :], rden[:, :, :]))
                num = acc[:, group(it), 0:D].rearrange("p k (h d) -> p k h d", d=HD)
                link(dve.tensor_tensor(num, num, rden[:, :, :].unsqueeze(3).to_broadcast([P, GRP, HEADS, HD]), ALU.mult))
                dve.wait_ge(norm_a, it * GRP + GRP)
                rows = acc[:, group(it), 0:D]
                link(dve.tensor_tensor(rows, rows, grp_a[:, :, :], ALU.add))
                link(dve.memset(spare[:, 0:1], 0.0))
                dve.memset(spare[:, 0:1], 0.0).then_inc(norm_a_used, 1)
                group_stats(dve, link, lambda k: one(acc[:, tile(k, it), 0:D]), stats, mv, spare, mean_var, it)
            link.end(NGRP)
            scales(dve, link, mean_var, rstd, nmr, var2, std2, scale2)
            dve.wait_ge(par_in, 64)
            dve.memset(spare[:, 0:1], 0.0).then_inc(norm_b_used, 1)
            with dve.Fori(0, NGRP) as it:
                link.loop(it, 0, 7)
                dve.wait_ge(norm_b, it * GRP + GRP)
                link(dve.tensor_tensor(grp_a[:, :, :], grp_a[:, :, :], spread_tiles(gam[:, :]), ALU.mult))
                link(dve.tensor_tensor(grp_a[:, :, :], grp_a[:, :, :], spread_tiles(bet[:, :]), ALU.add))
                dve.tensor_scalar(grp_b[:, :, :], grp_a[:, :, :], 0.0, None, ALU.min).then_inc(low_ready, 1)
                dve.wait_ge(exp_ready, it + 1)
                link(dve.scalar_tensor_tensor(grp_b[:, :, :], grp_a[:, :, :], 0.0, grp_b[:, :, :], ALU.max, ALU.add))
                dve.memset(spare[:, 0:1], 0.0).then_inc(norm_b_used, 1)
                rows = x_all[:, group(it), :]
                link(dve.scalar_tensor_tensor(rows, grp_b[:, :, :], -1.0, rows, ALU.add, ALU.add))
                group_stats(dve, link, lambda k: one(x_all[:, tile(k, it), :]), stats, mv, spare, mean_var, it)
            link.end(NGRP)
            scales(dve, link, mean_var, rstd, nmr, var3, std3, scale3)
            dve.wait_ge(consts, 12)

            def experts(v):
                return v.unsqueeze(1).to_broadcast([P, GRP, EXPERTS])

            def per_tile(v):
                return v.unsqueeze(2).to_broadcast([P, GRP, EXPERTS])

            def router(it, head):
                dve.wait_ge(logits_done, it + 1)
                link(dve.tensor_copy(logits[:, :, :].rearrange("p k e -> p (k e)"), ps_l[:, 0:GRP * EXPERTS]))
                dve.memset(spare[:, 0:1], 0.0).then_inc(logits_read, 1)
                for k in range(GRP):
                    last = dve.max(top[:, k, :], logits[:, k, :])
                link(last)
                dve.memset(spare[:, 0:1], 0.0)
                for k in range(GRP):
                    last = dve.max_index(top_i[:, k, :], top[:, k, :], logits[:, k, :])
                link(last)
                dve.tensor_tensor(diff[:, :], top[:, :, 1], top[:, :, 0], ALU.subtract).then_inc(diff_ready, 1)
                link(dve.tensor_copy(top_f[:, :, :], top_i[:, :, 0:2]))
                for c in range(2):
                    last = dve.tensor_tensor(pick[:, c, :, :], experts(expert_no[:, :]), per_tile(top_f[:, :, c]), ALU.is_equal)
                link(last)
                link(dve.tensor_tensor(both[:, :, :], pick[:, 0, :, :], pick[:, 1, :, :], ALU.add))
                dve.tensor_tensor(both_h[:, :, :], both[:, :, :], per_tile(valid[:, group(it)]), ALU.mult).then_inc(both_ready, 1)
                dve.wait_ge(ediff_ready, it + 1)
                link(dve.tensor_scalar(rsum[:, :], ediff[:, :], 1.0, None, ALU.add))
                link(dve.reciprocal(rsum[:, :], rsum[:, :]))
                dve.tensor_copy(gates[:, group(it), 0], rsum[:, :])
                dve.tensor_tensor(gates[:, group(it), 1], rsum[:, :], ediff[:, :], ALU.mult)
                dve.wait_ge(ranks_done, it + 1)
                for k in range(GRP):
                    link(dve.tensor_tensor(base[:, k + 1, :], base[:, k, :], ps_total[:, k * EXPERTS:(k + 1) * EXPERTS], ALU.add))
                link(dve.tensor_tensor(place[:, :, :], base[:, 0:GRP, :],
                                       ps_before[:, 0:GRP * EXPERTS].rearrange("p (k e) -> p k e", k=GRP), ALU.add))
                link(dve.tensor_tensor(place[:, :, :], place[:, :, :], experts(expert_row[:, :]), ALU.add))
                for c in range(2):
                    last = dve.tensor_tensor(hit[:, c, :, :], place[:, :, :], pick[:, c, :, :], ALU.mult)
                link(last)
                link(dve.tensor_reduce(slot_f[:, :, :], hit[:, :, :, :], AX.X, ALU.add))
                v2 = valid[:, group(it)].unsqueeze(1).to_broadcast([P, 2, GRP])
                link(dve.tensor_tensor(slot_f[:, :, :], slot_f[:, :, :], v2, ALU.mult))
                link(dve.tensor_tensor(slot_f[:, :, :], slot_f[:, :, :], pads[:, group(it), :].rearrange("p k c -> p c k"), ALU.add))
                if not head:
                    for k in range(GRP):
                        dve.wait_ge(sent[k], 32 * it)
                dve.tensor_copy(slots[:, group(it), :].rearrange("p k c -> p c k"), slot_f[:, :, :])
                dve.tensor_copy(slot_g[:, :, :], slot_f[:, :, :]).then_inc(slots_ready, 1)
                link(dve.tensor_copy(base[:, 0, :], base[:, GRP, :]))

            ROUTER_LINKS = 22
            link.loop(0, 0, ROUTER_LINKS)
            router(0, True)
            link.end(1)
            with dve.Fori(1, NGRP) as it:
                link.loop(it, 1, ROUTER_LINKS)
                router(it, False)
            link.end(NGRP - 1)
            link(dve.tensor_copy(taken[:, :], base[:, 0, :]))


def scales(dve, link, mean_var, rstd, nmr, var, std, scale):
    dve.tensor_scalar(nmr[:, :], mean_var[:, :, 1], EPS, None, ALU.add).then_inc(var, 1)
    dve.wait_ge(std, 1)
    link(dve.reciprocal(rstd[:, :], rstd[:, :]))
    dve.scalar_tensor_tensor(nmr[:, :], mean_var[:, :, 0], -1.0, rstd[:, :], ALU.mult, ALU.mult).then_inc(scale, 1)


def stage5(nc, dispatched, taken, slots, rows_l, expert_l, passes_i):
    with ExitStack() as ctx:
        def sb(name, shape, dt=F32):
            return ctx.enter_context(nc.sbuf_tensor(name, shape, dt))

        def sem(name):
            return ctx.enter_context(nc.semaphore(name))

        X1 = EXPERTS + 1
        L = FFN_LIST
        zeros = sb("zeros", [P, D])
        need_i = sb("need_i", [P, EXPERTS], I32)
        need = sb("need", [P, EXPERTS])
        ones = sb("ones5", [P, EXPERTS])
        begin = sb("begin", [P, X1])
        key = sb("key5", [P, X1])
        delta = sb("delta5", [P, X1])
        region = sb("region", [P, X1])
        tile_no = sb("tile_no", [P, L])
        ge = sb("ge5", [P, L, X1])
        slot_f = sb("slot_f5", [P, TILES * 2])
        shift_by = sb("shift_by", [P, TILES * 2])
        over = sb("over5", [P, TILES * 2, X1])
        res = sb("res5", [P, L])
        row_end = sb("row_end", [P, EXPERTS])
        row_end_i = sb("row_end_i", [P, EXPERTS], I32)
        passes_f = sb("passes_f", [P, 1])
        consts = sem("consts5")
        dve_chain = sem("dve_chain5")
        ends_ready = sem("ends_ready")
        zeros_out = sem("zeros_out")
        block = ctx.enter_context(nc.Block())

        @block.gpsimd
        def _(pool):
            pool.memset(zeros[:, :], 0.0).then_inc(consts, 1)
            pool.iota(tile_no[:, :], pattern=[[1, L]], base=0, channel_multiplier=0,
                      allow_small_or_imprecise_dtypes=True).then_inc(consts, 1)
            pool.iota(region[:, :], pattern=[[CAP, X1]], base=0, channel_multiplier=0,
                      allow_small_or_imprecise_dtypes=True).then_inc(consts, 1)

        @block.sync
        def _(sp):
            sp.wait_ge(consts, 3)
            for j in range(FFN_SPARE):
                sp.dma_start(dispatched[PADFFN + j * P:PADFFN + (j + 1) * P, :], zeros[:, :]).then_inc(zeros_out, 16)
            sp.wait_ge(ends_ready, 1)
            for e in range(EXPERTS):
                end = sp.value_load(row_end_i[0:1, e:e + 1], min_val=0, max_val=DROWS - P)
                sp.dma_start(dispatched[bass.ds(end, P), :], zeros[:, :]).then_inc(zeros_out, 16)
            sp.wait_ge(zeros_out, 16 * (EXPERTS + FFN_SPARE))

        @block.vector
        def _(dve):
            link = Chain(dve, dve_chain)
            dve.wait_ge(consts, 3)
            link(dve.tensor_tensor(row_end[:, :], taken[:, :], region[:, 0:EXPERTS], ALU.add))
            dve.tensor_copy(row_end_i[:, :], row_end[:, :]).then_inc(ends_ready, 1)
            link(dve.tensor_scalar(need[:, :], taken[:, :], float(P - 1), None, ALU.add))
            link(dve.tensor_copy(need_i[:, :], need[:, :]))
            link(dve.tensor_scalar(need_i[:, :], need_i[:, :], P.bit_length() - 1, None, ALU.arith_shift_right))
            link(dve.tensor_copy(need[:, :], need_i[:, :]))
            dve.memset(ones[:, :], 1.0)
            link(dve.memset(begin[:, 0:1], 0.0))
            link(dve.tensor_tensor_scan(begin[:, 1:X1], ones[:, :], need[:, :], 0.0, ALU.mult, ALU.add))
            link(dve.scalar_tensor_tensor(key[:, :], begin[:, :], -float(P), region[:, :], ALU.mult, ALU.add))
            link(dve.tensor_scalar(key[:, EXPERTS:X1], key[:, EXPERTS:X1], float(PADFFN - PADROWS), None, ALU.add))
            link(dve.tensor_copy(delta[:, 0:1], key[:, 0:1]))
            link(dve.tensor_tensor(delta[:, 1:X1], key[:, 1:X1], key[:, 0:EXPERTS], ALU.subtract))
            link(dve.tensor_tensor(ge[:, :, :], tile_no[:, :].unsqueeze(2).to_broadcast([P, L, X1]),
                                   begin[:, :].unsqueeze(1).to_broadcast([P, L, X1]), ALU.is_ge))
            link(dve.tensor_reduce(res[:, :], ge[:, :, 1:X1], AX.X, ALU.add))
            dve.memset(expert_l[:, 0:4], 0)
            link(dve.tensor_scalar(expert_l[:, 4:L + 4], res[:, :], float(EXPERTS - 1), None, ALU.min))
            link(dve.tensor_tensor(ge[:, :, :], ge[:, :, :], delta[:, :].unsqueeze(1).to_broadcast([P, L, X1]), ALU.mult))
            link(dve.tensor_reduce(res[:, :], ge[:, :, :], AX.X, ALU.add))
            link(dve.scalar_tensor_tensor(res[:, :], tile_no[:, :], float(P), res[:, :], ALU.mult, ALU.add))
            link(dve.tensor_scalar(rows_l[:, :], res[:, :], float(DROWS - P), None, ALU.min))
            flat = slots[:, :, :].rearrange("p t c -> p (t c)")
            link(dve.tensor_copy(slot_f[:, :], flat))
            link(dve.tensor_tensor(over[:, :, :], slot_f[:, :].unsqueeze(2).to_broadcast([P, TILES * 2, X1]),
                                   region[:, :].unsqueeze(1).to_broadcast([P, TILES * 2, X1]), ALU.is_ge))
            link(dve.tensor_tensor(over[:, :, :], over[:, :, :], delta[:, :].unsqueeze(1).to_broadcast([P, TILES * 2, X1]), ALU.mult))
            link(dve.tensor_reduce(shift_by[:, :], over[:, :, :], AX.X, ALU.add))
            link(dve.tensor_tensor(flat, slot_f[:, :], shift_by[:, :], ALU.subtract))
            link(dve.tensor_scalar(passes_f[:, :], begin[:, EXPERTS:X1], float(FFN_LAG + FFN_BODY - 1), None, ALU.add))
            link(dve.tensor_copy(passes_i[:, :], passes_f[:, :]))
            link(dve.tensor_scalar(passes_i[:, :], passes_i[:, :], FFN_BODY.bit_length() - 1, None, ALU.arith_shift_right))


def stage6(nc, w1, b1, w2, b2, dispatched, expert_out, ident, rows_l, expert_l, passes_i):
    with ExitStack() as ctx:
        def sb(name, shape, dt=F32):
            return ctx.enter_context(nc.sbuf_tensor(name, shape, dt))

        def pb(name, shape, dt=F32):
            return ctx.enter_context(nc.psum_tensor(name, shape, dt))

        def sem(name):
            return ctx.enter_context(nc.semaphore(name))

        B = FFN_BODY
        w1_sb = sb("w1_sb", [P, EXPERTS, KD, FF])
        w2_sb = sb("w2_sb", [P, EXPERTS, KF, D])
        b1T = sb("b1T", [P, EXPERTS, KF])
        b2_t = sb("b2_t", [P, B, D])
        xt = sb("xt", [P, B, D])
        xT = sb("xT", [P, 2, D])
        hid = sb("hid", [P, 2, FF])
        hidT = sb("hidT", [P, 2, FF])
        o_sb = sb("o_sb", [P, 2, D])
        ps_x = [pb(f"ps_x{i}", [P, 512]) for i in range(2)]
        ps_h = [pb(f"ps5_h{i}", [P, 512]) for i in range(2)]
        ps_ht = [pb(f"ps_ht{i}", [P, 512]) for i in range(2)]
        ps_o = [pb(f"ps_o{i}", [P, 512]) for i in range(2)]

        w_in = sem("w_in5")
        b2_in = [sem(f"b2_in{i}") for i in range(B)]
        x_in = [sem(f"x5_in{i}") for i in range(B)]
        x_tr = sem("x_tr")
        xT_ready = sem("xT_ready")
        h_done = sem("h_done")
        h_copied = sem("h_copied")
        h_tr = sem("h_tr")
        hT_ready = sem("hT_ready")
        o_done = sem("o_done")
        o_ready = sem("o_ready")
        o_out = [sem(f"o_out{i}") for i in range(2)]
        sp_turn = sem("sp_turn5")
        block = ctx.enter_context(nc.Block())
        W_IN = 16 * 9
        MAXPASS = (MAXFFN + FFN_LAG + B - 1) // B

        def pass_count(eng):
            return eng.value_load(passes_i[0:1, 0:1], min_val=3, max_val=MAXPASS)

        def expert(eng, i, back):
            return eng.value_load(expert_l[0:1, bass.ds(i + (4 - back), 1)], min_val=0, max_val=EXPERTS - 1)

        def row(eng, i):
            return eng.value_load(rows_l[0:1, bass.ds(i, 1)], min_val=0, max_val=DROWS - P)

        @block.sync
        def _(sp):
            for q in range(4):
                e = slice(4 * q, 4 * q + 4)
                sp.dma_start(w1_sb[:, e, :, :].rearrange("p e a f -> p (e a) f"),
                             w1[e, :, :].rearrange("e (a p) f -> p (e a) f", p=P)).then_inc(w_in, 16)
            passes = pass_count(sp)

            def load(s, i, head):
                r = row(sp, i)
                if not head:
                    sp.wait_ge(x_tr, i - B + 1)
                    sp.sem_inc(sp_turn, 1)
                sp.dma_start(xt[:, s, :], dispatched[bass.ds(r, P), :]).then_inc(x_in[s], 16)

            def store(s, i):
                sp.wait_ge(o_ready, i + 1)
                sp.sem_inc(sp_turn, 1)
                sp.dma_start(expert_out[bass.ds(i * P, P), :], o_sb[:, s, :]).then_inc(o_out[s], 16)

            def load_b2(s, i):
                e = expert(sp, i, 0)
                sp.dma_start(b2_t[:, s, :], b2[bass.ds(e, 1), :].to_broadcast([P, D])).then_inc(b2_in[s], 16)

            for i in range(FFN_AHEAD):
                load(i, i, True)
            for i in range(B):
                load_b2(i, i)
            for i in range(B):
                load((i + FFN_AHEAD) % B, i + FFN_AHEAD, i + FFN_AHEAD < B)
                if i >= FFN_LAG:
                    store((i - FFN_LAG) % 2, i - FFN_LAG)
                    load_b2((i + 1) % B, i + 1)
            with sp.Fori(1, passes) as it:
                for k in range(B):
                    load((k + FFN_AHEAD) % B, it * B + k + FFN_AHEAD, False)
                    store((k - FFN_LAG) % 2, it * B + (k - FFN_LAG))
                    load_b2((k + 1) % B, it * B + (k + 1))
            sp.sem_inc(o_out[0], 16)
            sp.sem_inc(o_out[1], 32)
            for q in range(2):
                sp.wait_ge(o_out[q], passes * (16 * B // 2))
            for k in range(B):
                sp.wait_ge(b2_in[k], passes * 16 + (16 if k == 0 else 0))
            sp.sem_inc(sp_turn, 1)

        @block.scalar
        def _(act):
            for q in range(4):
                e = slice(4 * q, 4 * q + 4)
                act.dma_start(w2_sb[:, e, :, :].rearrange("p e a f -> p (e a) f"),
                              w2[e, :, :].rearrange("e (a p) f -> p (e a) f", p=P)).then_inc(w_in, 16)
            act.dma_start(b1T[:, :, :].rearrange("p e a -> p (e a)"), b1.rearrange("e (a p) -> p (e a)", p=P)).then_inc(w_in, 16)
            act.preload_act_table(ACT.Relu)
            act.wait_ge(w_in, W_IN)
            passes = pass_count(act)

            def step(k, i, head):
                s = k % 2
                act.wait_ge(x_tr, i + 1)
                if not (head and i < 2):
                    act.wait_ge(h_done, i - 1)
                act.activation(xT[:, s, :], ps_x[s][:, 0:D], ACT.Copy).then_inc(xT_ready, 1)
                if not (head and i < 2):
                    e = expert(act, i, 2)
                    act.wait_ge(h_tr, i - 1)
                    if not (head and i < 4):
                        act.wait_ge(o_done, i - 3)
                    for j in range(KF):
                        last = act.activation(hidT[:, s, j * P:(j + 1) * P], ps_ht[s][:, j * P:(j + 1) * P], ACT.Relu,
                                              bias=b1T[:, bass.ds(e, 1), j:j + 1].rearrange("p a b -> p (a b)"))
                    last.then_inc(hT_ready, 1)

            for i in range(2 * B):
                step(i % B, i, True)
            with act.Fori(2, passes) as it:
                for k in range(B):
                    step(k, it * B + k, False)

        @block.tensor
        def _(pe):
            pe.wait_ge(w_in, W_IN)
            passes = pass_count(pe)

            def step(k, i, head):
                s, o = k % 2, 1 - k % 2
                pe.wait_ge(x_in[k], 16 * (i // B + 1) if head else (i - k) * (16 // B) + 16)
                if not (head and i < 2):
                    pe.wait_ge(xT_ready, i - 1)
                for a in range(KD):
                    last = pe.transpose(ps_x[s][:, a * P:(a + 1) * P], xt[:, k, a * P:(a + 1) * P], ident[:, :])
                last.then_inc(x_tr, 1)
                if not (head and i < 1):
                    e = expert(pe, i, 1)
                    pe.wait_ge(xT_ready, i)
                    if not (head and i < 3):
                        pe.wait_ge(h_copied, i - 2)
                    for a in range(KD):
                        last = pe.matmul(ps_h[o][:, :], xT[:, o, a * P:(a + 1) * P],
                                         w1_sb[:, bass.ds(e, 1), a, :].rearrange("p a b -> p (a b)"),
                                         start=(a == 0), stop=(a == KD - 1))
                    last.then_inc(h_done, 1)
                if not (head and i < 2):
                    pe.wait_ge(h_copied, i - 1)
                    if not (head and i < 4):
                        pe.wait_ge(hT_ready, i - 3)
                    for j in range(KF):
                        last = pe.transpose(ps_ht[s][:, j * P:(j + 1) * P], hid[:, s, j * P:(j + 1) * P], ident[:, :])
                    last.then_inc(h_tr, 1)
                if not (head and i < 3):
                    e = expert(pe, i, 3)
                    pe.wait_ge(hT_ready, i - 2)
                    if not (head and i < 5):
                        pe.wait_ge(o_ready, i - 4)
                    for j in range(KF):
                        last = pe.matmul(ps_o[o][:, 0:D], hidT[:, o, j * P:(j + 1) * P],
                                         w2_sb[:, bass.ds(e, 1), j, :].rearrange("p a b -> p (a b)"),
                                         start=(j == 0), stop=(j == KF - 1))
                    last.then_inc(o_done, 1)

            for i in range(2 * B):
                step(i % B, i, True)
            with pe.Fori(2, passes) as it:
                for k in range(B):
                    step(k, it * B + k, False)

        @block.vector
        def _(dve):
            dve.wait_ge(w_in, W_IN)
            passes = pass_count(dve)

            def step(k, i, head):
                o = 1 - k % 2
                if not (head and i < 1):
                    dve.wait_ge(h_done, i)
                    if not (head and i < 3):
                        dve.wait_ge(h_tr, i - 2)
                    dve.tensor_copy(hid[:, o, :], ps_h[o][:, :]).then_inc(h_copied, 1)
                if not (head and i < 3):
                    dve.wait_ge(b2_in[(k - 3) % B], 16 * ((i - 3) // B + 1) if head else (i - 3 - (k - 3) % B) * (16 // B) + 16)
                    dve.wait_ge(o_done, i - 2)
                    if not (head and i < 5):
                        dve.wait_ge(o_out[o], ((i - 3) // 2) * 16 if head else (i - 3 - o) * 8)
                    dve.tensor_tensor(o_sb[:, o, :], ps_o[o][:, 0:D], b2_t[:, (k - 3) % B, :], ALU.add).then_inc(o_ready, 1)

            for i in range(2 * B):
                step(i % B, i, True)
            with dve.Fori(2, passes) as it:
                for k in range(B):
                    step(k, it * B + k, False)


def stage7(nc, fgamma, fbeta, expert_out, out, x_all, mean_var, rstd, nmr, slots, gates):
    with ExitStack() as ctx:
        def sb(name, shape, dt=F32):
            return ctx.enter_context(nc.sbuf_tensor(name, shape, dt))

        def sem(name):
            return ctx.enter_context(nc.semaphore(name))

        gam = sb("fgam", [P, D])
        bet = sb("fbet", [P, D])
        slot_g = sb("slot_g7", [P, GRP, 2], I32)
        gate_g = sb("gate_g7", [P, GRP, 2])
        back = sb("back", [P, GRP, 2, D])
        y = sb("y7", [P, GRP, D])
        part = sb("part", [P, GRP, D])
        moe = sb("moe", [P, TILES, D])
        stats = sb("stats7", [P, GRP, 6])
        mv = sb("mv7", [P, GRP, 2])
        spare = sb("spare7", [P, 2])
        normed = sb("normed", [P, 2, GRP, D])

        par_in = sem("par_in7")
        dve_chain = sem("dve_chain7")
        slots_staged = sem("slots_staged")
        pool_turn = sem("pool_turn7")
        came = [sem(f"came{k}") for k in range(GRP)]
        y_ready = sem("y_ready7")
        group_used = sem("group_used7")
        var4 = sem("var4")
        std4 = sem("std4")
        scale4 = sem("scale4")
        norm_ready = sem("norm_ready7")
        out_ready = sem("out_ready")
        out_sent = [sem(f"out_sent{i}") for i in range(2)]
        block = ctx.enter_context(nc.Block())

        def tile(k, it):
            return bass.ds(it * GRP + k, 1)

        def group(it):
            return bass.ds(it * GRP, GRP)

        @block.gpsimd
        def _(pool):
            def fetch(last):
                for k in range(GRP):
                    n = LAST if last and k == GRP - 1 else P
                    for c in range(2):
                        pool.indirect_dma_start(back[0:n, k, c, :], None, expert_out,
                                                bass.IndirectOffsetOnAxis(ap=slot_g[0:n, k, c:c + 1], axis=0)).then_inc(came[k], 16)

            with pool.Fori(0, NGRP - 1) as it:
                pool.wait_ge(slots_staged, it + 1)
                pool.sem_inc(pool_turn, 1)
                fetch(False)
            pool.wait_ge(slots_staged, NGRP)
            fetch(True)

        @block.scalar
        def _(act):
            def norm_x(it, head):
                for k in range(GRP):
                    if not head:
                        act.wait_ge(group_used, it)
                    act.activation(y[:, k, :], one(x_all[:, tile(k, it), :]), ACT.Identity,
                                   bias=nmr[:, tile(k, it)], scale=rstd[:, tile(k, it)]).then_inc(y_ready, 1)

            norm_x(0, True)
            with act.Fori(1, NGRP) as it:
                norm_x(it, False)
            act.wait_ge(var4, 1)
            act.activation(rstd[:, :], nmr[:, :], ACT.Sqrt).then_inc(std4, 1)
            act.wait_ge(scale4, 1)
            act.preload_act_table(ACT.Identity)
            for it in range(NGRP):
                for k in range(GRP):
                    if it >= 2:
                        act.wait_ge(out_sent[it % 2], 16 * (it // 2))
                    t = it * GRP + k
                    act.activation(normed[:, it % 2, k, :], moe[:, t, :], ACT.Identity,
                                   bias=nmr[:, t:t + 1], scale=rstd[:, t:t + 1]).then_inc(norm_ready, 1)

        @block.vector
        def _(dve):
            link = Chain(dve, dve_chain)
            dve.memset(back[:, GRP - 1, :, :], 0.0)

            def gather_sum(it):
                link(dve.tensor_copy(gate_g[:, :, :], gates[:, group(it), :]))
                for k in range(GRP):
                    dve.wait_ge(came[k], it * 32 + 32)
                dve.wait_ge(y_ready, it * GRP + GRP)
                for c in range(2):
                    for k in range(GRP):
                        last = dve.scalar_tensor_tensor(part[:, k, :] if c == 0 else one(moe[:, tile(k, it), :]),
                                                        back[:, k, c, :], gate_g[:, k, c:c + 1],
                                                        y[:, k, :] if c == 0 else part[:, k, :], ALU.mult, ALU.add)
                    link(last)
                dve.memset(spare[:, 0:1], 0.0).then_inc(group_used, 1)
                group_stats(dve, link, lambda k: one(moe[:, tile(k, it), :]), stats, mv, spare, mean_var, it)

            link(dve.tensor_copy(slot_g[:, :, :], slots[:, 0:GRP, :]))
            dve.memset(spare[:, 0:1], 0.0).then_inc(slots_staged, 1)
            with dve.Fori(0, NGRP - 1) as it:
                link.loop(it, 0, 7)
                gather_sum(it)
                link(dve.tensor_copy(slot_g[:, :, :], slots[:, bass.ds(it * GRP + GRP, GRP), :]))
                dve.memset(spare[:, 0:1], 0.0).then_inc(slots_staged, 1)
            link.end(NGRP - 1)
            gather_sum(NGRP - 1)
            scales(dve, link, mean_var, rstd, nmr, var4, std4, scale4)
            dve.wait_ge(par_in, 32)
            for it in range(NGRP):
                z = normed[:, it % 2, :, :]
                dve.wait_ge(norm_ready, it * GRP + GRP)
                link(dve.tensor_tensor(z, z, spread_tiles(gam[:, :]), ALU.mult))
                link(dve.tensor_tensor(z, z, spread_tiles(bet[:, :]), ALU.add))
                dve.tensor_tensor(z, z, x_all[:, it * GRP:(it + 1) * GRP, :], ALU.add).then_inc(out_ready, 1)

        @block.sync
        def _(sp):
            sp.dma_start(gam[:, :], fgamma.unsqueeze(0).to_broadcast([P, D])).then_inc(par_in, 16)
            sp.dma_start(bet[:, :], fbeta.unsqueeze(0).to_broadcast([P, D])).then_inc(par_in, 16)
            for it in range(NGRP):
                sp.wait_ge(out_ready, it + 1)
                t0 = it * GRP
                nt = GRP if it < NGRP - 1 else GRP - 1
                sp.dma_start(out[t0 * P:(t0 + nt) * P, :].rearrange("(t p) d -> p t d", p=P),
                             normed[:, it % 2, 0:nt, :]).then_inc(out_sent[it % 2], 16)
            last = (NGRP - 1) % 2
            sp.dma_start(out[FULL * P:N, :], normed[0:LAST, last, GRP - 1, :]).then_inc(out_sent[last], 16)
            sp.wait_ge(out_sent[last], 16 * ((NGRP + 1) // 2 + 1))
            sp.wait_ge(out_sent[1 - last], 16 * (NGRP // 2))


_INS = ["x", "src", "dst", "L0_gnn_W", "L0_gnn_a_src", "L0_gnn_a_dst", "L0_gnn_gamma", "L0_gnn_beta", "L0_ffn_gate_w",
        "L0_ffn_gate_b", "L0_ffn_w1", "L0_ffn_b1", "L0_ffn_w2", "L0_ffn_b2", "L0_ffn_gamma", "L0_ffn_beta"]


def kernel(**inputs):
    import concourse.bacc as _bacc
    from concourse.bass_utils import run_bass_kernel_spmd as _run

    nc = _bacc.Bacc("TRN2", target_bir_lowering=False, num_devices=1)
    arrays, args = {}, []
    for name in _INS:
        a = np.ascontiguousarray(inputs[name])
        arrays[f"in_{name}_dram"] = a
        args.append(nc.dram_tensor(f"in_{name}_dram", a.shape, mybir.dt.from_np(a.dtype), kind="ExternalInput").ap())
    args.append(nc.dram_tensor("out_0_dram", (N, D), F32, kind="ExternalOutput").ap())
    build(nc, *args)
    r = _run(nc, [arrays], core_ids=[0])
    return r.results[0]["out_0_dram"]
```

```python
from contextlib import ExitStack

import concourse.bass as bass
import numpy as np
from concourse import mybir

F32 = mybir.dt.float32
BF16 = mybir.dt.bfloat16
I32 = mybir.dt.int32
U32 = mybir.dt.uint32
ALU = mybir.AluOpType
ACT = mybir.ActivationFunctionType
AX = mybir.AxisListType

P = 128
N, D = 6250, 256
E = 206250
HEADS, HD = 8, 32
TILES = (N + P - 1) // P
LAST = N - (TILES - 1) * P
FULL = TILES - 1
ROW = D + 2 * HEADS
SUM = D + HEADS
PROJ = D + 2 * HEADS
GRP = 7
NGRP = TILES // GRP
CHUNKS = (E + P - 1) // P
CB = (CHUNKS + P - 1) // P
CFULL = E // P
CREST = E - CFULL * P
PADC = CB * P
COLS = PADC + 8
NODST = 9999.0
BODY = 8
WEIGH, SUMS, JOIN = 2, 3, 4
AHEAD = 5
RING = 4
SLOPE = 0.2
IBLK = 1024
MAXSTEPS = TILES * ((CHUNKS + 1) // 2 + 1)
SLACK = (RING + 1) * BODY
IBLKS = (MAXSTEPS + SLACK) // IBLK + 1
EPS = 1e-5
EXPERTS, FF = 16, 512
KD, KF = D // P, FF // P
CAP = (N + P - 1) // P * P + P
PADROWS = EXPERTS * CAP
PADFFN = PADROWS + 2 * P
MAXFFN = 2 * N // P + EXPERTS
FFN_BODY = 4
FFN_LAG = 3
FFN_AHEAD = 3
FFN_SPARE = FFN_LAG + FFN_BODY + FFN_AHEAD
DROWS = PADFFN + FFN_SPARE * P
FFN_LIST = 128
ZERO_TILES = 41
FFN_TILES = -(-(MAXFFN + FFN_LAG + FFN_BODY) // ZERO_TILES) * ZERO_TILES
SAFE = 60.0
FAR = 1e30


LIST_OF = ((AHEAD, True), (AHEAD, False), (0, True), (0, False), (-1, False), (-JOIN, False))
LISTS = len(LIST_OF)
NEXT_CHUNK, NEXT_TILE, CHUNK, TILE, LOOK_TILE, OLD_TILE = range(LISTS)


class Chain:

    def __init__(self, eng, sem):
        self.eng, self.sem, self.n, self.base = eng, sem, 0, 0

    def __call__(self, ins):
        self.n += 1
        ins.then_inc(self.sem, 1)
        self.eng.wait_ge(self.sem, self.base + self.n)

    def loop(self, it, first, per):
        self.start, self.per = self.n, per
        self.base = (it - first) * per

    def end(self, passes):
        assert self.n == self.start + self.per, (self.n, self.start, self.per)
        self.n, self.base = self.start + self.per * passes, 0


def build(nc, x, src, dst, W, a_src, a_dst, gamma, beta, gate_w, gate_b, w1, b1, w2, b2, fgamma, fbeta, out, stage=9):
    ctx = ExitStack()
    with ctx:
        def sb(name, shape, dt=F32):
            return ctx.enter_context(nc.sbuf_tensor(name, shape, dt))

        def sem(name):
            return ctx.enter_context(nc.semaphore(name))

        ctx.enter_context(nc.allow_non_contiguous_dma(reason="small constants"))
        table = nc.dram_tensor("table", [TILES * P, ROW], F32).ap()
        schedule = nc.dram_tensor("schedule", [IBLKS * IBLK // BODY, LISTS * BODY], I32).ap()

        dispatched = nc.dram_tensor("dispatched", [DROWS, D], F32).ap()
        expert_out = nc.dram_tensor("expert_out", [FFN_TILES * P, D], F32).ap()

        x_all = sb("x_all", [P, TILES, D])
        ident = sb("ident", [P, P])
        mean_var = sb("mean_var", [P, TILES, 2])
        rstd = sb("rstd", [P, TILES])
        nmr = sb("nmr", [P, TILES])
        slots = sb("slots", [P, TILES, 2], I32)
        gates = sb("gates", [P, TILES, 2])
        taken = sb("taken", [P, EXPERTS])
        zeroed = sem("zeroed")
        w1_in = sem("w1_in")
        w2_in = sem("w2_in")
        weights = ctx.enter_context(ExitStack())

        def right(name, shape):
            return weights.enter_context(nc.sbuf_tensor(name, shape, F32, side="right"))

        with ExitStack() as graph:
            def gsb(name, shape, dt=F32):
                return graph.enter_context(nc.sbuf_tensor(name, shape, dt))

            acc = gsb("acc", [P, TILES, SUM])
            with ExitStack() as edge:
                def esb(name, shape, dt=F32):
                    return edge.enter_context(nc.sbuf_tensor(name, shape, dt))

                node_iota = esb("node_iota", [P, P])
                neg_first = esb("neg_first", [P, TILES])
                dst_tab = esb("dst_tab", [P, TILES, 2 * HEADS])
                src_sc = esb("src_sc", [P, TILES, HEADS])
                srcT = esb("srcT", [P, COLS], I32)
                dstT = esb("dstT", [P, COLS])
                tile_lo = esb("tile_lo", [P, TILES])
                tile_n = esb("tile_n", [P, TILES])
                counts = esb("counts", [P, 4], I32)
                seg_max = esb("seg_max", [P, TILES, HEADS])
                stage1(nc, x, src, dst, W, a_src, a_dst, table, x_all, acc, ident, node_iota, neg_first, mean_var,
                       rstd, nmr, dst_tab, src_sc, srcT, dstT, tile_lo, tile_n, expert_out, zeroed)
                stage2(nc, table, schedule, zeroed, src_sc, dst_tab, tile_lo, tile_n, counts, seg_max)
                bounds(nc, table, schedule, ident, node_iota, neg_first, dst_tab, srcT, dstT, counts, seg_max)
                stage3(nc, table, schedule, acc, ident, node_iota, neg_first, dst_tab, srcT, dstT, counts)
            w1_sb = right("w1_sb", [P, EXPERTS, KD, FF])
            stage4(nc, gamma, beta, w1, w1_sb, w1_in, x_all, acc, mean_var, rstd, nmr)
        w2_sb = right("w2_sb", [P, EXPERTS, KF, D])
        route(nc, gate_w, gate_b, w2, w2_sb, w2_in, dispatched, x_all, ident, rstd, nmr, slots, gates, taken)
        rows_l = sb("rows_l", [P, FFN_LIST], I32)
        expert_l = sb("expert_l", [P, FFN_LIST + 4], I32)
        passes_i = sb("passes_i", [P, 1], I32)
        stage5(nc, dispatched, taken, slots, rows_l, expert_l, passes_i)
        stage6(nc, b1, b2, w1_sb, w2_sb, w1_in, w2_in, dispatched, expert_out, ident, rows_l, expert_l, passes_i)
        weights.close()
        stage7(nc, fgamma, fbeta, expert_out, out, x_all, mean_var, rstd, nmr, slots, gates)


def stage1(nc, x, src, dst, W, a_src, a_dst, table, x_all, acc, ident, node_iota, neg_first, mean_var, rstd, nmr,
           dst_tab, src_sc, srcT, dstT, tile_lo, tile_n, expert_out, zeroed):
    with ExitStack() as ctx:
        def sb(name, shape, dt=F32):
            return ctx.enter_context(nc.sbuf_tensor(name, shape, dt))

        def pb(name, shape, dt=F32):
            return ctx.enter_context(nc.psum_tensor(name, shape, dt))

        def sem(name):
            return ctx.enter_context(nc.semaphore(name))

        w_ext = sb("w_ext", [P, 2, PROJ])
        w_T = sb("w_T", [P, 2, D])
        a_col = sb("a_col", [P, 2, 2])
        a_blk = sb("a_blk", [P, 2, 2 * HEADS])
        stats = sb("stats", [P, GRP, 6])
        mv = sb("mv", [P, GRP, 2])
        spare = sb("spare", [P, 1])
        edges_i = sb("edges_i", [P, 2, CB, P], I32)
        edges_f = sb("edges_f", [P, 2, CB, P])
        real_dst = sb("real_dst", [P, P])
        chunk_min = sb("chunk_min", [P, CB])
        chunk_max = sb("chunk_max", [P, CB])
        chunk_no = sb("chunk_no", [P, CB])
        tile_first = sb("tile_first", [P, TILES])
        over_a = sb("over_a", [P, TILES, CB])
        over_b = sb("over_b", [P, TILES, CB])
        lohi = sb("lohi", [P, 2, TILES])
        lohi_r = sb("lohi_r", [P, 2, TILES])
        span_i = sb("span_i", [P, TILES], I32)
        odd_i = sb("odd_i", [P, TILES], I32)
        span = sb("span", [P, TILES])
        odd = sb("odd", [P, TILES])
        xn = sb("xn", [P, GRP, D])
        xnT = sb("xnT", [P, GRP, D])
        rows = sb("rows", [P, GRP, D])
        ps_t = [pb(f"ps_t{i}", [P, 512]) for i in range(2)]
        ps_h = [pb(f"ps_h{i}", [P, 512]) for i in range(2)]
        ps_e = [pb(f"ps_e{i}", [P, 512]) for i in range(2)]

        x_in = sem("x_in")
        w_in = sem("w_in")
        edges_in = sem("edges_in")
        consts = sem("consts")
        acc_zero = sem("acc_zero")
        dve_chain = sem("dve_chain")
        edges_clear = sem("edges_clear")
        x_clear = sem("x_clear")
        var_ready = sem("var_ready")
        std_ready = sem("std_ready")
        norm_ready = sem("norm_ready")
        w_tr = sem("w_tr")
        w_tr_copied = sem("w_tr_copied")
        wa_done = sem("wa_done")
        wext_ready = sem("wext_ready")
        xn_ready = sem("xn_ready")
        xn_tr = sem("xn_tr")
        xnT_ready = sem("xnT_ready")
        proj_done = sem("proj_done")
        rows_ready = sem("rows_ready")
        rows_out = [sem(f"rows_out{k}") for k in range(GRP)]
        edges_f_ready = sem("edges_f_ready")
        edge_tr = sem("edge_tr")
        edge_tr_copied = sem("edge_tr_copied")
        lohi_ready = sem("lohi_ready")
        lohi_all = sem("lohi_all")

        block = ctx.enter_context(nc.Block())
        EG = (2 * CB + 3) // 4

        @block.sync
        def _(sp):
            sp.wait_ge(x_clear, 1)
            for g in range(NGRP):
                t0 = g * GRP
                nt = GRP if g < NGRP - 1 else GRP - 1
                sp.dma_start(x_all[:, t0:t0 + nt, :],
                             x[t0 * P:(t0 + nt) * P, :].rearrange("(t p) d -> p t d", p=P)).then_inc(x_in, 16)
            sp.dma_start(x_all[0:LAST, FULL, :], x[FULL * P:N, :]).then_inc(x_in, 16)
            for it in range(1):
                for k in range(GRP):
                    sp.wait_ge(rows_ready, k + 1)
                    sp.dma_start(table[k * P:(k + 1) * P, 0:D], rows[:, k, :]).then_inc(rows_out[k], 16)
            with sp.Fori(1, NGRP) as it:
                for k in range(GRP):
                    sp.wait_ge(rows_ready, it * GRP + (k + 1))
                    sp.dma_start(table[bass.ds(it * (GRP * P) + k * P, P), 0:D], rows[:, k, :]).then_inc(rows_out[k], 16)
            sp.wait_ge(acc_zero, 1)
            for t in range(0, FFN_TILES, ZERO_TILES):
                sp.dma_start(expert_out[t * P:(t + ZERO_TILES) * P, :].rearrange("(t p) d -> p t d", p=P),
                             acc[:, 0:ZERO_TILES, 0:D]).then_inc(zeroed, 16)
            for k in range(GRP):
                sp.wait_ge(rows_out[k], 16 * NGRP)

        @block.gpsimd
        def _(pool):
            pool.memset(ident[:, :], 0.0).then_inc(consts, 1)
            pool.memset(a_blk[:, :, :], 0.0).then_inc(consts, 1)
            pool.wait_ge(consts, 2)
            pool.affine_select(out=ident[:, :], in_=ident[:, :], compare_op=ALU.not_equal, fill=1.0, base=0,
                               pattern=[[-1, P]], channel_multiplier=1).then_inc(consts, 1)
            pool.iota(chunk_no[:, :], pattern=[[P, CB]], base=0, channel_multiplier=1,
                      allow_small_or_imprecise_dtypes=True).then_inc(consts, 1)
            pool.iota(tile_first[:, :], pattern=[[P, TILES]], base=0, channel_multiplier=0,
                      allow_small_or_imprecise_dtypes=True).then_inc(consts, 1)
            pool.iota(neg_first[:, :], pattern=[[-P, TILES]], base=0, channel_multiplier=0,
                      allow_small_or_imprecise_dtypes=True).then_inc(consts, 1)
            pool.iota(node_iota[:, :], pattern=[[1, P]], base=0, channel_multiplier=0,
                      allow_small_or_imprecise_dtypes=True).then_inc(consts, 1)
            pool.memset(acc[:, :, :], 0.0).then_inc(acc_zero, 1)
            pool.wait_ge(acc_zero, 1)
            pool.wait_ge(lohi_ready, 2)
            pool.partition_all_reduce(lohi_r[:, :, :], lohi[:, :, :], P, bass.bass_isa.ReduceOp.max).then_inc(lohi_all, 1)
            pool.wait_ge(lohi_all, 1)

        @block.scalar
        def _(act):
            act.dma_start(w_ext[:, :, 0:D], W.rearrange("(a p) n -> p a n", p=P)).then_inc(w_in, 16)
            act.dma_start(a_col[:, 0, :], a_src.rearrange("(a h) d -> (h d) a", a=2)).then_inc(w_in, 16)
            act.dma_start(a_col[:, 1, :], a_dst.rearrange("(a h) d -> (h d) a", a=2)).then_inc(w_in, 16)
            act.wait_ge(edges_clear, 1)
            for i, e in enumerate((src, dst)):
                act.dma_start(edges_i[:, i, 0:CB - 1, :],
                              e[0:(CB - 1) * P * P].rearrange("(b p e) -> p b e", p=P, e=P)).then_inc(edges_in, 16)
                lo = (CB - 1) * P * P
                act.dma_start(edges_i[0:CFULL % P, i, CB - 1, :],
                              e[lo:CFULL * P].rearrange("(p e) -> p e", e=P)).then_inc(edges_in, 16)
                act.dma_start(edges_i[CFULL % P:CFULL % P + 1, i, CB - 1, 0:CREST],
                              e[CFULL * P:E].rearrange("(p e) -> p e", p=1)).then_inc(edges_in, 16)
            for a in range(2):
                act.wait_ge(w_tr, a + 1)
                act.activation(w_T[:, a, :], ps_t[a][:, 0:D], ACT.Copy).then_inc(w_tr_copied, 1)
            for a in range(2):
                act.wait_ge(wa_done, a + 1)
                act.activation(w_ext[:, a, D:PROJ], ps_h[a][:, 0:2 * HEADS], ACT.Copy).then_inc(wext_ready, 1)
            act.wait_ge(var_ready, 1)
            act.activation(rstd[:, :], nmr[:, :], ACT.Sqrt).then_inc(std_ready, 1)
            act.wait_ge(norm_ready, 1)
            act.preload_act_table(ACT.Exp)

            def tile(k, g, first):
                t = g
                if not first:
                    act.wait_ge(xn_tr, g - (GRP - 1))
                act.activation(xn[:, k, :], x_all[:, bass.ds(t, 1), :].rearrange("p a d -> p (a d)"), ACT.Identity,
                               bias=nmr[:, bass.ds(t, 1)], scale=rstd[:, bass.ds(t, 1)]).then_inc(xn_ready, 1)
                act.wait_ge(xn_tr, g + 1)
                if not first:
                    act.wait_ge(proj_done, g - (GRP - 1))
                act.activation(xnT[:, k, :], ps_t[k % 2][:, 0:D], ACT.Copy).then_inc(xnT_ready, 1)

            for k in range(GRP):
                tile(k, k, True)
            with act.Fori(1, NGRP) as it:
                for k in range(GRP):
                    tile(k, it * GRP + k, False)

        @block.vector
        def _(dve):
            link = Chain(dve, dve_chain)
            dve.memset(x_all[:, FULL, :], 0.0).then_inc(x_clear, 1)
            dve.memset(edges_i[:, 0, CB - 1, :], 0)
            dve.memset(edges_i[:, 1, CB - 1, :], int(NODST)).then_inc(edges_clear, 1)
            dve.memset(srcT[:, PADC:COLS], 0)
            dve.memset(dstT[:, PADC:COLS], NODST)
            dve.wait_ge(w_in, 48)
            dve.wait_ge(consts, 2)
            for a in range(2):
                for q in range(4):
                    for s in range(2):
                        dve.tensor_copy(a_blk[q * HD:(q + 1) * HD, a, s * HEADS + 4 * a + q:s * HEADS + 4 * a + q + 1],
                                        a_col[q * HD:(q + 1) * HD, s, a:a + 1]).then_inc(edges_f_ready, 1)
            dve.wait_ge(edges_in, 96)
            for i in range(2):
                dve.tensor_copy(edges_f[:, i, :, :], edges_i[:, i, :, :]).then_inc(edges_f_ready, 1)
            dve.wait_ge(x_in, 16 * (NGRP + 1))
            with dve.Fori(0, NGRP) as it:
                link.loop(it, 0, 3)
                for k in range(GRP):
                    st = dve.bn_stats(stats[:, k, :], x_all[:, bass.ds(it * GRP + k, 1), :].rearrange("p a d -> p (a d)"))
                link(st)
                dve.memset(spare[:, :], 0.0)
                for k in range(GRP):
                    aggr = dve.bn_aggr(mv[:, k, :], stats[:, k, :])
                link(aggr)
                link(dve.tensor_copy(mean_var[:, bass.ds(it * GRP, GRP), :], mv[:, :, :]))
            link.end(NGRP)
            dve.tensor_scalar(nmr[:, :], mean_var[:, :, 1], EPS, None, ALU.add).then_inc(var_ready, 1)
            dve.wait_ge(edges_f_ready, 18)
            dve.tensor_reduce(chunk_min[:, :], edges_f[:, 1, :, :], AX.X, ALU.min)
            link(dve.tensor_scalar(real_dst[:, :], edges_f[:, 1, CB - 1, :], NODST, -NODST - 1, ALU.is_ge, ALU.mult))
            link(dve.tensor_tensor(real_dst[:, :], real_dst[:, :], edges_f[:, 1, CB - 1, :], ALU.add))
            dve.tensor_reduce(chunk_max[:, 0:CB - 1], edges_f[:, 1, 0:CB - 1, :], AX.X, ALU.max)
            link(dve.tensor_reduce(chunk_max[:, CB - 1:CB], real_dst[:, :], AX.X, ALU.max))
            dve.wait_ge(std_ready, 1)
            link(dve.reciprocal(rstd[:, :], rstd[:, :]))
            dve.scalar_tensor_tensor(nmr[:, :], mean_var[:, :, 0], -1.0, rstd[:, :], ALU.mult, ALU.mult).then_inc(norm_ready, 1)

            def per_tile(v):
                return v.unsqueeze(2).to_broadcast([P, TILES, CB])

            def per_chunk(v):
                return v.unsqueeze(1).to_broadcast([P, TILES, CB])

            def seg_steps():
                dve.wait_ge(consts, 7)
                dve.tensor_tensor(over_a[:, :, :], per_chunk(chunk_max[:, :]), per_tile(tile_first[:, :]), ALU.is_ge)
                link(dve.tensor_scalar(span[:, :], tile_first[:, :], float(P - 1), None, ALU.add))
                link(dve.tensor_tensor(over_b[:, :, :], per_chunk(chunk_min[:, :]), per_tile(span[:, :]), ALU.is_le))
                link(dve.tensor_tensor(over_a[:, :, :], over_a[:, :, :], over_b[:, :, :], ALU.mult))
                link(dve.tensor_scalar(chunk_max[:, :], chunk_no[:, :], 1.0, None, ALU.add))
                link(dve.tensor_tensor(over_b[:, :, :], over_a[:, :, :], per_chunk(chunk_max[:, :]), ALU.mult))
                link(dve.tensor_reduce(lohi[:, 1, :], over_b[:, :, :], AX.X, ALU.max))
                link(dve.tensor_scalar(chunk_max[:, :], chunk_no[:, :], -1.0, 4096.0, ALU.mult, ALU.add))
                link(dve.tensor_tensor(over_b[:, :, :], over_a[:, :, :], per_chunk(chunk_max[:, :]), ALU.mult))
                dve.tensor_reduce(lohi[:, 0, :], over_b[:, :, :], AX.X, ALU.max).then_inc(lohi_ready, 2)

            seg_steps()

            def tile(k, g, first):
                dve.wait_ge(proj_done, g + 1)
                if not first:
                    dve.wait_ge(rows_out[k], 16 * it)
                dve.tensor_copy(rows[:, k, :], ps_h[k % 2][:, 0:D])
                dve.tensor_copy(src_sc[:, bass.ds(g, 1), :].rearrange("p a d -> p (a d)"), ps_h[k % 2][:, D:SUM])
                dve.tensor_copy(dst_tab[:, bass.ds(g, 1), 0:HEADS].rearrange("p a d -> p (a d)"),
                                ps_h[k % 2][:, SUM:PROJ]).then_inc(rows_ready, 1)

            for k in range(GRP):
                tile(k, k, True)
            with dve.Fori(1, NGRP) as it:
                for k in range(GRP):
                    tile(k, it * GRP + k, False)
            for q in range(EG):
                dve.wait_ge(edge_tr, min(4 * q + 4, 2 * CB))
                for j in range(4 * q, min(4 * q + 4, 2 * CB)):
                    to = (srcT if j < CB else dstT)[:, (j % CB) * P:(j % CB + 1) * P]
                    last = dve.tensor_copy(to, ps_e[q % 2][:, (j % 4) * P:(j % 4 + 1) * P])
                last.then_inc(edge_tr_copied, 1)
            dve.wait_ge(edge_tr_copied, EG)
            dve.wait_ge(lohi_all, 1)
            link(dve.tensor_scalar(tile_lo[:, :], lohi_r[:, 0, :], -1.0, 4096.0, ALU.mult, ALU.add))
            link(dve.tensor_tensor(span[:, :], lohi_r[:, 1, :], tile_lo[:, :], ALU.subtract))
            link(dve.tensor_scalar(span[:, :], span[:, :], 0.0, None, ALU.max))
            link(dve.tensor_copy(span_i[:, :], span[:, :]))
            link(dve.tensor_scalar(odd_i[:, :], span_i[:, :], 1, None, ALU.bitwise_and))
            link(dve.tensor_copy(odd[:, :], odd_i[:, :]))
            link(dve.tensor_tensor(span[:, :], span[:, :], odd[:, :], ALU.add))
            link(dve.tensor_scalar(tile_n[:, :], span[:, :], 0.5, None, ALU.mult))

        @block.tensor
        def _(pe):
            pe.wait_ge(consts, 3)
            pe.wait_ge(w_in, 48)
            for j in range(2):
                for k in range(2):
                    last = pe.transpose(ps_t[j][:, k * P:(k + 1) * P], w_ext[:, k, j * P:(j + 1) * P], ident[:, :])
                last.then_inc(w_tr, 1)
            pe.wait_ge(w_tr_copied, 2)
            pe.wait_ge(edges_f_ready, 16)
            for k in range(2):
                for j in range(2):
                    last = pe.matmul(ps_h[k][:, 0:2 * HEADS], w_T[:, j, k * P:(k + 1) * P], a_blk[:, j, :],
                                     start=(j == 0), stop=(j == 1))
                last.then_inc(wa_done, 1)
            pe.wait_ge(wext_ready, 2)

            def tile(k, g, first):
                pe.wait_ge(xn_ready, g + 1)
                if not (first and k < 2):
                    pe.wait_ge(xnT_ready, g - 1 if k else g)
                for a in range(2):
                    last = pe.transpose(ps_t[k % 2][:, a * P:(a + 1) * P], xn[:, k, a * P:(a + 1) * P], ident[:, :])
                last.then_inc(xn_tr, 1)
                pe.wait_ge(xnT_ready, g + 1)
                if not (first and k < 2):
                    pe.wait_ge(rows_ready, g - 1 if k else g)
                for a in range(2):
                    last = pe.matmul(ps_h[k % 2][:, 0:PROJ], xnT[:, k, a * P:(a + 1) * P], w_ext[:, a, :],
                                     start=(a == 0), stop=(a == 1))
                last.then_inc(proj_done, 1)

            for k in range(GRP):
                tile(k, k, True)
            with pe.Fori(1, NGRP) as it:
                for k in range(GRP):
                    tile(k, it * GRP + k, False)
            pe.wait_ge(edges_f_ready, 18)
            for q in range(EG):
                if q >= 2:
                    pe.wait_ge(edge_tr_copied, q - 1)
                for j in range(4 * q, min(4 * q + 4, 2 * CB)):
                    pe.transpose(ps_e[q % 2][:, (j % 4) * P:(j % 4 + 1) * P], edges_f[:, j // CB, j % CB, :],
                                 ident[:, :]).then_inc(edge_tr, 1)


def stage2(nc, table, schedule, zeroed, src_sc, dst_tab, tile_lo, tile_n, counts, seg_max):
    with ExitStack() as ctx:
        def sb(name, shape, dt=F32):
            return ctx.enter_context(nc.sbuf_tensor(name, shape, dt))

        def sem(name):
            return ctx.enter_context(nc.semaphore(name))

        B = TILES + 1
        K = IBLK // P
        assert K == BODY
        first = sb("first", [P, B])
        ones = sb("ones", [P, TILES])
        key = sb("key", [P, B])
        delta = sb("delta", [P, B])
        delta3 = sb("delta3", [P, B])
        step_no = sb("step_no", [P, K])
        step_cur = sb("step_cur", [P, K])
        ge = sb("ge", [P, K, B])
        res = sb("res", [P, K])
        res_i = sb("res_i", [P, LISTS, K], I32)
        blk_f = sb("blk_f", [P, 4])
        best = sb("best", [P, 2, HEADS])
        best_all = sb("best_all", [P, 2, HEADS])
        apart = sb("apart", [P, HEADS])
        wide = sb("wide", [P, 1])
        scores = sb("scores", [P, TILES, 2 * HEADS])
        dve_chain = sem("dve_chain2")
        iotas = sem("iotas")
        best_ready = sem("best_ready")
        best_reduced = sem("best_reduced")
        apart_ready = sem("apart_ready")
        scores_ready = sem("scores_ready2")
        scores_out = sem("scores_out")
        counts_ready = sem("counts_ready")
        list_ready = sem("list_ready")
        list_out = sem("list_out")
        list_kept = sem("list_kept")
        block = ctx.enter_context(nc.Block())

        @block.gpsimd
        def _(pool):
            pool.iota(step_no[:, :], pattern=[[1, K]], base=0, channel_multiplier=K,
                      allow_small_or_imprecise_dtypes=True).then_inc(iotas, 1)
            pool.wait_ge(best_ready, 1)
            pool.partition_all_reduce(best_all[:, :, :], best[:, :, :], P, bass.bass_isa.ReduceOp.max).then_inc(best_reduced, 1)

        @block.vector
        def _(dve):
            link = Chain(dve, dve_chain)
            dve.tensor_reduce(best[:, 0, :], src_sc[:, :, :].rearrange("p t h -> p h t"), AX.X, ALU.max)
            link(dve.tensor_reduce(best[:, 1, :], src_sc[:, :, :].rearrange("p t h -> p h t"), AX.X, ALU.min))
            dve.tensor_scalar(best[:, 1, :], best[:, 1, :], -1.0, None, ALU.mult).then_inc(best_ready, 1)
            dve.memset(ones[:, :], 1.0)
            link(dve.memset(first[:, 0:1], 0.0))
            link(dve.tensor_tensor_scan(first[:, 1:B], ones[:, :], tile_n[:, :], 0.0, ALU.mult, ALU.add))
            link(dve.scalar_tensor_tensor(key[:, 0:TILES], first[:, 0:TILES], -2.0, tile_lo[:, :], ALU.mult, ALU.add))
            link(dve.tensor_scalar(key[:, TILES:B], first[:, TILES:B], -2.0, float(PADC), ALU.mult, ALU.add))
            link(dve.tensor_copy(delta[:, 0:1], key[:, 0:1]))
            link(dve.tensor_tensor(delta[:, 1:B], key[:, 1:B], key[:, 0:TILES], ALU.subtract))
            link(dve.tensor_scalar(blk_f[:, 0:1], first[:, TILES:B], 1.0, None, ALU.mult))
            link(dve.tensor_scalar(blk_f[:, 1:2], blk_f[:, 0:1], float(JOIN + BODY - 1), None, ALU.add))
            link(dve.tensor_scalar(blk_f[:, 2:3], blk_f[:, 0:1], float(SLACK + IBLK), None, ALU.add))
            link(dve.tensor_copy(counts[:, 0:2], blk_f[:, 1:3]))
            shift = BODY.bit_length() - 1
            link(dve.tensor_scalar(counts[:, 0:1], counts[:, 0:1], shift, None, ALU.arith_shift_right))
            dve.tensor_scalar(counts[:, 1:2], counts[:, 1:2], 10, None, ALU.arith_shift_right).then_inc(counts_ready, 1)
            dve.wait_ge(counts_ready, 1)
            dve.wait_ge(iotas, 1)
            dve.wait_ge(best_reduced, 1)
            most = best_all[:, 0, :].unsqueeze(1).to_broadcast([P, TILES, HEADS])
            dve.tensor_tensor(dst_tab[:, :, 0:HEADS], dst_tab[:, :, 0:HEADS], most, ALU.add)
            link(dve.tensor_tensor(scores[:, :, 0:HEADS], src_sc[:, :, :], most, ALU.subtract))
            dve.tensor_scalar(scores[:, :, HEADS:2 * HEADS], scores[:, :, 0:HEADS], SLOPE, None, ALU.mult).then_inc(scores_ready, 1)
            dve.tensor_tensor(apart[:, :], best_all[:, 0, :], best_all[:, 1, :], ALU.add).then_inc(apart_ready, 1)
            dve.wait_ge(apart_ready, 1)
            link(dve.tensor_reduce(wide[:, :], apart[:, :], AX.X, ALU.max))
            link(dve.tensor_scalar(wide[:, :], wide[:, :], SAFE, None, ALU.is_gt))
            link(dve.tensor_scalar(apart[:, :], apart[:, :], wide[:, :], -1.0, ALU.mult, ALU.mult))
            link(dve.tensor_copy(seg_max[:, :, :], apart[:, :].unsqueeze(1).to_broadcast([P, TILES, HEADS])))
            blocks = dve.value_load(counts[0:1, 1:2], min_val=1, max_val=IBLKS)

            def tiles(v):
                return v.unsqueeze(1).to_broadcast([P, K, B])

            def steps(v):
                return v.unsqueeze(2).to_broadcast([P, K, B])

            per = 2 + sum(6 if chunk else 4 for _, chunk in LIST_OF)
            with dve.Fori(0, blocks) as b:
                link.loop(b, 0, per)
                for q, (shift, chunk) in enumerate(LIST_OF):
                    link(dve.tensor_scalar(step_cur[:, :], step_no[:, :], float(shift), None, ALU.add))
                    link(dve.tensor_tensor(ge[:, :, :], steps(step_cur[:, :]), tiles(first[:, :]), ALU.is_ge))
                    if chunk:
                        link(dve.tensor_tensor(ge[:, :, :], ge[:, :, :], tiles(delta[:, :]), ALU.mult))
                        link(dve.tensor_reduce(res[:, :], ge[:, :, :], AX.X, ALU.add))
                        link(dve.scalar_tensor_tensor(res[:, :], step_cur[:, :], 2.0, res[:, :], ALU.mult, ALU.add))
                        link(dve.tensor_scalar(res_i[:, q, :], res[:, :], float(PADC + 4), None, ALU.min))
                    else:
                        link(dve.tensor_reduce(res[:, :], ge[:, :, 1:B], AX.X, ALU.add))
                        link(dve.tensor_scalar(res_i[:, q, :], res[:, :], float(TILES - 1), None, ALU.min))
                link(dve.tensor_scalar(step_no[:, :], step_no[:, :], float(IBLK), None, ALU.add))
                dve.memset(blk_f[:, 3:4], 0.0).then_inc(list_ready, 1)
                dve.wait_ge(list_out, 16 * b + 16)
                link(dve.memset(blk_f[:, 2:3], 0.0))
            link.end(blocks)
            link(dve.tensor_scalar(blk_f[:, 0:1], first[:, TILES:B], -1.0, None, ALU.add))
            link(dve.tensor_tensor(blk_f[:, 0:1], blk_f[:, 0:1], wide[:, :], ALU.mult))
            link(dve.tensor_scalar(blk_f[:, 0:1], blk_f[:, 0:1], 1.0, None, ALU.add))
            link(dve.tensor_copy(counts[:, 2:3], blk_f[:, 0:1]))
            dve.memset(blk_f[:, 3:4], 0.0)

        @block.sync
        def _(sp):
            sp.wait_ge(scores_ready, 1)
            sp.dma_start(table.rearrange("(t p) c -> p t c", p=P)[:, :, D:ROW], scores[:, :, :]).then_inc(scores_out, 16)
            sp.wait_ge(counts_ready, 1)
            blocks = sp.value_load(counts[0:1, 1:2], min_val=1, max_val=IBLKS)
            with sp.Fori(0, blocks) as b:
                sp.wait_ge(list_ready, b + 1)
                sp.dma_start(schedule[bass.ds(b * P, P), :], res_i[:, :, :].rearrange("p q k -> p (q k)")).then_inc(list_out, 16)
            sp.wait_ge(list_out, 16 * blocks)
            sp.sem_inc(list_kept, 1)
            sp.wait_ge(scores_out, 16)
            sp.wait_ge(zeroed, 16 * (FFN_TILES // ZERO_TILES))


def bounds(nc, table, schedule, ident, node_iota, neg_first, dst_tab, srcT, dstT, counts, seg_max):
    with ExitStack() as ctx:
        def sb(name, shape, dt=F32):
            return ctx.enter_context(nc.sbuf_tensor(name, shape, dt))

        def pb(name, shape, dt=F32):
            return ctx.enter_context(nc.psum_tensor(name, shape, dt))

        def sem(name):
            return ctx.enter_context(nc.semaphore(name))

        step_row = sb("step_row", [1, LISTS * BODY], I32)
        ones = sb("ones_b", [P, P])
        idx = sb("idx_b", [P, 2], I32)
        rel = sb("rel_b", [P, 2])
        gat = sb("gat_b", [P, 2, ROW])
        hot = sb("hot_b", [P, 2, P])
        away = sb("away", [P, 2, P])
        diag = sb("diag", [P, HEADS, P])
        masked = sb("masked", [P, HEADS, P])
        cur = sb("cur", [P, HEADS])
        spare = sb("spare_b", [P, 4])
        leak = sb("leak", [P, TILES, HEADS])
        ps_hot = pb("ps_hot_b", [P, 512])
        ps_all = [pb(f"ps_all{i}", [P, 512]) for i in range(2)]
        ones_ready = sem("ones_ready")
        row_in = sem("row_in")
        idx_ready = sem("idx_ready_b")
        rel_ready = sem("rel_ready_b")
        landed = sem("landed_b")
        hot_ready = sem("hot_ready_b")
        hot_tr = sem("hot_tr_b")
        diag_ready = sem("diag_ready")
        spread = sem("spread_b")
        step_done = sem("step_done")
        pool_turn = sem("pool_turn_b")
        sp_turn = sem("sp_turn_b")
        dve_chain = sem("dve_chain_b")
        block = ctx.enter_context(nc.Block())

        def step_count(eng):
            return eng.value_load(counts[0:1, 2:3], min_val=1, max_val=MAXSTEPS)

        def from_list(eng, it, which, most):
            return eng.value_load(step_row[0:1, bass.ds((it & (BODY - 1)) + which * BODY, 1)], min_val=0, max_val=most)

        @block.sync
        def _(sp):
            steps = step_count(sp)
            sp.dma_start(step_row[:, :], schedule[0:1, :]).then_inc(row_in, 16)
            with sp.Fori(0, steps) as it:
                sp.wait_ge(step_done, it + 1)
                sp.sem_inc(sp_turn, 1)
                sp.dma_start(step_row[:, :], schedule[bass.ds((it + 1) >> (BODY.bit_length() - 1), 1), :]).then_inc(row_in, 16)
            sp.wait_ge(row_in, steps * 16 + 16)
            sp.sem_inc(sp_turn, 1)

        @block.gpsimd
        def _(pool):
            steps = step_count(pool)
            with pool.Fori(0, steps) as it:
                pool.wait_ge(idx_ready, it + 1)
                pool.sem_inc(pool_turn, 1)
                for j in range(2):
                    pool.indirect_dma_start(gat[:, j, :], None, table,
                                            bass.IndirectOffsetOnAxis(ap=idx[:, j:j + 1], axis=0)).then_inc(landed, 16)

        @block.scalar
        def _(act):
            act.preload_act_table(ACT.Exp)
            steps = step_count(act)
            with act.Fori(0, steps) as it:
                act.wait_ge(row_in, it * 16 + 16)
                c = from_list(act, it, CHUNK, PADC + 4)
                t = from_list(act, it, TILE, TILES - 1)
                act.activation(idx[:, :], srcT[:, bass.ds(c, 2)], ACT.Copy).then_inc(idx_ready, 1)
                act.activation(rel[:, :], dstT[:, bass.ds(c, 2)], ACT.Identity, bias=neg_first[:, bass.ds(t, 1)]).then_inc(rel_ready, 1)

        @block.tensor
        def _(pe):
            steps = step_count(pe)
            pe.wait_ge(ones_ready, 1)
            with pe.Fori(0, steps) as it:
                pe.wait_ge(hot_ready, it + 1)
                for j in range(2):
                    last = pe.transpose(ps_hot[:, j * P:(j + 1) * P], hot[:, j, :], ident[:, :])
                last.then_inc(hot_tr, 1)
                for j in range(2):
                    pe.wait_ge(diag_ready, it * 2 + (j + 1))
                    for q in range(2):
                        last = pe.matmul(ps_all[q][:, :], ones[:, :],
                                         diag[:, q * HEADS // 2:(q + 1) * HEADS // 2, :].rearrange("p h e -> p (h e)"),
                                         start=True, stop=True)
                    last.then_inc(spread, 1)

        @block.vector
        def _(dve):
            link = Chain(dve, dve_chain)
            dve.memset(ones[:, :], 1.0).then_inc(ones_ready, 1)
            steps = step_count(dve)

            def heads(v):
                return v.unsqueeze(1).to_broadcast([P, HEADS // 2, P])

            with dve.Fori(0, steps) as it:
                link.loop(it, 0, 10)
                dve.wait_ge(rel_ready, it + 1)
                dve.tensor_tensor(hot[:, :, :], node_iota[:, :].unsqueeze(1).to_broadcast([P, 2, P]),
                                  rel[:, :].unsqueeze(2).to_broadcast([P, 2, P]), ALU.is_equal).then_inc(hot_ready, 1)
                dve.wait_ge(hot_tr, it + 1)
                link(dve.tensor_scalar(away[:, :, :].rearrange("p a b -> p (a b)"), ps_hot[:, 0:2 * P], -1.0, FAR,
                                       ALU.add, ALU.mult))
                dve.wait_ge(landed, it * 32 + 32)
                tile = from_list(dve, it, TILE, TILES - 1)
                here = one(seg_max[:, bass.ds(tile, 1), :])
                for j in range(2):
                    link(dve.tensor_tensor(diag[:, :, :], ident[:, :].unsqueeze(1).to_broadcast([P, HEADS, P]),
                                           gat[:, j, D:D + HEADS].unsqueeze(2).to_broadcast([P, HEADS, P]), ALU.mult))
                    dve.memset(spare[:, 0:1], 0.0).then_inc(diag_ready, 1)
                    dve.wait_ge(spread, it * 2 + (j + 1))
                    for q in range(2):
                        last = dve.tensor_tensor(masked[:, q * HEADS // 2:(q + 1) * HEADS // 2, :],
                                                 ps_all[q][:, :].rearrange("p (h e) -> p h e", e=P),
                                                 heads(away[:, j, :]), ALU.add)
                    link(last)
                    link(dve.tensor_reduce(cur[:, :], masked[:, :, :], AX.X, ALU.max))
                    link(dve.tensor_tensor(here, here, cur[:, :], ALU.max))
                link(dve.memset(spare[:, 1:2], 0.0))
                dve.memset(spare[:, 2:3], 0.0).then_inc(step_done, 1)
            link.end(steps)
            link(dve.tensor_tensor(leak[:, :, :], dst_tab[:, :, 0:HEADS], seg_max[:, :, :], ALU.add))
            link(dve.scalar_tensor_tensor(leak[:, :, :], leak[:, :, :], SLOPE, leak[:, :, :], ALU.mult, ALU.max))
            link(dve.scalar_tensor_tensor(dst_tab[:, :, HEADS:2 * HEADS], dst_tab[:, :, 0:HEADS], SLOPE, leak[:, :, :],
                                          ALU.mult, ALU.subtract))
            link(dve.tensor_tensor(dst_tab[:, :, 0:HEADS], dst_tab[:, :, 0:HEADS], leak[:, :, :], ALU.subtract))
            dve.memset(spare[:, 3:4], 0.0)


def stage3(nc, table, schedule, acc, ident, node_iota, neg_first, dst_tab, srcT,
           dstT, counts):
    with ExitStack() as ctx:
        def sb(name, shape, dt=F32):
            return ctx.enter_context(nc.sbuf_tensor(name, shape, dt))

        def pb(name, shape, dt=F32):
            return ctx.enter_context(nc.psum_tensor(name, shape, dt))

        def sem(name):
            return ctx.enter_context(nc.semaphore(name))

        MSGS = 4
        MAXBODY = (MAXSTEPS + JOIN + BODY - 1) // BODY
        gat = sb("gat", [P, BODY, 2, ROW])
        idx = sb("idx", [P, BODY, 2], I32)
        rel = sb("rel", [P, BODY, 2])
        lists = sb("lists", [1, RING, LISTS, BODY], I32)
        hot = sb("hot", [P, BODY, 2, P])
        hotT = sb("hotT", [P, 2, 2, P])
        both = sb("both", [P, 2, 2, 2 * HEADS])
        score = sb("score", [P, 2, 2, HEADS])
        msg = sb("msg", [P, MSGS, 2, SUM])
        ps_hot = [pb(f"ps_hot{i}", [P, 512]) for i in range(2)]
        ps_look = [pb(f"ps_look{i}", [P, 512]) for i in range(2)]
        ps_sum = [pb(f"ps_sum{i}", [P, 512]) for i in range(2)]
        landed = [sem(f"landed{k}") for k in range(BODY)]
        lists_in = sem("lists_in")
        rows_landed = sem("rows_landed")
        idx_ready = sem("idx_ready")
        rel_ready = sem("rel_ready")
        pool_turn = sem("pool_turn")
        sp_turn = sem("sp_turn")
        hot_ready = sem("hot_ready")
        hot_tr = sem("hot_tr")
        hotT_ready = sem("hotT_ready")
        look_done = sem("look_done")
        both_ready = sem("both_ready")
        score_ready = sem("score_ready")
        weight_ready = sem("weight_ready")
        msg_ready = sem("msg_ready")
        sum_done = sem("sum_done")
        added = sem("added")
        block = ctx.enter_context(nc.Block())

        def registers(eng, name):
            return [eng.alloc_register(f"{name}{k}") for k in range(BODY)]

        def load_list(eng, regs, which, it):
            at = (it & (RING - 1)) * (LISTS * BODY) + which * BODY
            flat = lists[:, :, :, :].rearrange("o r l k -> o (r l k)")
            for k in range(0, BODY, 4):
                eng.load(regs[k:k + 4], flat[0:1, bass.ds(at + k, 4)])

        def chunk_of(eng, reg):
            return eng.snap(reg, min_val=0, max_val=PADC + 4)

        def tile_of(eng, reg):
            return eng.snap(reg, min_val=0, max_val=TILES - 1)

        def body_count(eng):
            return eng.value_load(counts[0:1, 0:1], min_val=2, max_val=MAXBODY)

        @block.gpsimd
        def _(pool):
            bodies = body_count(pool)

            def step(k, g, head):
                if not head:
                    pool.wait_ge(msg_ready, g - (BODY - 1))
                pool.wait_ge(idx_ready, g + 1)
                pool.sem_inc(pool_turn, 1)
                for j in range(2):
                    pool.indirect_dma_start(gat[:, k, j, :], None, table,
                                            bass.IndirectOffsetOnAxis(ap=idx[:, k, j:j + 1], axis=0)).then_inc(landed[k], 16)

            for k in range(BODY):
                step(k, k, True)
            with pool.Fori(1, bodies) as it:
                for k in range(BODY):
                    step(k, it * BODY + k, False)

        @block.sync
        def _(sp):
            bodies = body_count(sp)
            sp.dma_start(lists[0:1, 0:2, :, :].rearrange("o r l k -> o (r l k)"),
                         schedule[0:2, :].rearrange("(o r) n -> o (r n)", o=1)).then_inc(lists_in, 32)
            with sp.Fori(0, bodies) as it:
                sp.wait_ge(lists_in, it * 16 + 32)
                sp.sem_inc(sp_turn, 1)
                sp.dma_start(lists[:, :, :, :].rearrange("o r l k -> o r (l k)")[0:1, bass.ds((it + 2) & (RING - 1), 1), :],
                             schedule[bass.ds(it + 2, 1), :].unsqueeze(0)).then_inc(lists_in, 16)
                for k in range(BODY):
                    sp.wait_ge(landed[k], it * 32 + 32)
                    sp.sem_inc(rows_landed, 1)
            sp.wait_ge(lists_in, bodies * 16 + 32)
            sp.sem_inc(sp_turn, 1)

        @block.scalar
        def _(act):
            act.preload_act_table(ACT.Exp)
            chunks, tiles = registers(act, "next_chunk"), registers(act, "next_tile")
            bodies = body_count(act)
            act.wait_ge(lists_in, 32)

            def lay_out(slot, chunk, tile):
                c, t = chunk_of(act, chunk), tile_of(act, tile)
                act.activation(idx[:, slot, :], srcT[:, bass.ds(c, 2)], ACT.Copy).then_inc(idx_ready, 1)
                act.activation(rel[:, slot, :], dstT[:, bass.ds(c, 2)], ACT.Identity, bias=neg_first[:, bass.ds(t, 1)]).then_inc(rel_ready, 1)

            load_list(act, chunks, CHUNK, 0)
            load_list(act, tiles, TILE, 0)
            for k in range(AHEAD):
                lay_out(k, chunks[k], tiles[k])

            def step(k, g, head):
                if not (head and k < WEIGH):
                    act.wait_ge(score_ready, g - WEIGH + 1)
                    if not (head and k < WEIGH + MSGS):
                        act.wait_ge(sum_done, g - WEIGH - MSGS + 1)
                    m = (k - WEIGH) % MSGS
                    act.activation(msg[:, m, :, D:SUM], score[:, m % 2, :, :], ACT.Exp).then_inc(weight_ready, 1)
                act.wait_ge(hot_tr, g + 1)
                if not (head and k < 2):
                    act.wait_ge(look_done, g - 1)
                act.activation(hotT[:, k % 2, :, :].rearrange("p a b -> p (a b)"), ps_hot[k % 2][:, 0:2 * P],
                               ACT.Copy).then_inc(hotT_ready, 1)
                if not (head and k < BODY - AHEAD):
                    act.wait_ge(rows_landed, g - (BODY - AHEAD) + 1)
                lay_out((k + AHEAD) % BODY, chunks[k], tiles[k])

            def body(it, head):
                load_list(act, chunks, NEXT_CHUNK, it)
                load_list(act, tiles, NEXT_TILE, it)
                for k in range(BODY):
                    step(k, it * BODY + k, head)

            body(0, True)
            with act.Fori(1, bodies) as it:
                act.wait_ge(lists_in, it * 16 + 16)
                body(it, False)

        @block.tensor
        def _(pe):
            tiles = registers(pe, "tile")
            bodies = body_count(pe)
            pe.wait_ge(lists_in, 32)

            def look(k, g, head, tile):
                pe.wait_ge(hotT_ready, g + 1)
                if not (head and k < 2):
                    pe.wait_ge(both_ready, g - 1)
                for j in range(2):
                    last = pe.matmul(ps_look[k % 2][:, j * 2 * HEADS:(j + 1) * 2 * HEADS], hotT[:, k % 2, j, :],
                                     dst_tab[:, bass.ds(tile_of(pe, tile), 1), :].rearrange("p a b -> p (a b)"),
                                     start=True, stop=True)
                last.then_inc(look_done, 1)

            def step(k, g, head):
                pe.wait_ge(hot_ready, g + 1)
                if not (head and k < 2):
                    pe.wait_ge(hotT_ready, g - 1)
                for j in range(2):
                    last = pe.transpose(ps_hot[k % 2][:, j * P:(j + 1) * P], hot[:, k, j, :], ident[:, :])
                last.then_inc(hot_tr, 1)
                if not (head and k < 1):
                    look((k - 1) % BODY, g - 1, head, tiles[k])
                if not (head and k < SUMS):
                    pe.wait_ge(msg_ready, g - SUMS + 1)
                    if not (head and k < SUMS + 2):
                        pe.wait_ge(added, g - SUMS - 1)
                    for j in range(2):
                        last = pe.matmul(ps_sum[(k - SUMS) % 2][:, 0:SUM], hot[:, (k - SUMS) % BODY, j, :],
                                         msg[:, (k - SUMS) % MSGS, j, :], start=(j == 0), stop=(j == 1))
                    last.then_inc(sum_done, 1)

            def body(it, head):
                load_list(pe, tiles, LOOK_TILE, it)
                for k in range(BODY):
                    step(k, it * BODY + k, head)

            body(0, True)
            with pe.Fori(1, bodies) as it:
                pe.wait_ge(lists_in, it * 16 + 16)
                body(it, False)

        @block.vector
        def _(dve):
            olds = registers(dve, "old_tile")
            bodies = body_count(dve)
            dve.wait_ge(lists_in, 32)

            def step(k, g, head):
                m = (k - WEIGH) % MSGS
                if not (head and k < WEIGH):
                    dve.wait_ge(rows_landed, g - WEIGH + 1)
                    dve.wait_ge(look_done, g - WEIGH + 1)
                    dve.tensor_tensor(both[:, m % 2, :, :], gat[:, (k - WEIGH) % BODY, :, D:ROW],
                                      ps_look[m % 2][:, 0:4 * HEADS].rearrange("p (j s) -> p j s", j=2),
                                      ALU.add).then_inc(both_ready, 1)
                dve.wait_ge(rel_ready, g + 1)
                if not (head and k < BODY):
                    dve.wait_ge(sum_done, g - BODY + 1)
                dve.tensor_tensor(hot[:, k, :, :], node_iota[:, :].unsqueeze(1).to_broadcast([P, 2, P]),
                                  rel[:, k, :].unsqueeze(2).to_broadcast([P, 2, P]), ALU.is_equal).then_inc(hot_ready, 1)
                if head and k < WEIGH:
                    return
                dve.wait_ge(both_ready, g - WEIGH + 1)
                dve.tensor_tensor(score[:, m % 2, :, :], both[:, m % 2, :, 0:HEADS], both[:, m % 2, :, HEADS:2 * HEADS],
                                  ALU.max).then_inc(score_ready, 1)
                if not (head and k < JOIN):
                    o = tile_of(dve, olds[k])
                    dve.wait_ge(sum_done, g - JOIN + 1)
                    if not (head and k < JOIN + 1):
                        dve.wait_ge(added, g - JOIN)
                    to = acc[:, bass.ds(o, 1), :].rearrange("p a b -> p (a b)")
                    dve.tensor_tensor(to, to, ps_sum[(k - JOIN) % 2][:, 0:SUM], ALU.add).then_inc(added, 1)
                dve.wait_ge(weight_ready, g - WEIGH + 1)
                dve.tensor_tensor(msg[:, m, :, 0:D].rearrange("p j (h d) -> p j h d", d=HD),
                                  gat[:, (k - WEIGH) % BODY, :, 0:D].rearrange("p j (h d) -> p j h d", d=HD),
                                  msg[:, m, :, D:SUM].unsqueeze(3).to_broadcast([P, 2, HEADS, HD]),
                                  ALU.mult).then_inc(msg_ready, 1)

            def body(it, head):
                load_list(dve, olds, OLD_TILE, it)
                for k in range(BODY):
                    step(k, it * BODY + k, head)

            body(0, True)
            with dve.Fori(1, bodies) as it:
                dve.wait_ge(lists_in, it * 16 + 16)
                body(it, False)


def spread_tiles(v, n=GRP):
    return v.unsqueeze(1).to_broadcast([P, n, D])


def group_stats(dve, link, source, stats, mv, spare, mean_var, it):
    dve.memset(spare[:, 1:2], 0.0)
    for k in range(GRP):
        last = dve.bn_stats(stats[:, k, :], source(k))
    link(last)
    dve.memset(spare[:, 1:2], 0.0)
    for k in range(GRP):
        last = dve.bn_aggr(mv[:, k, :], stats[:, k, :])
    link(last)
    link(dve.tensor_copy(mean_var[:, bass.ds(it * GRP, GRP), :], mv[:, :, :]))


def one(v):
    return v.rearrange("p a d -> p (a d)")


def stage4(nc, gamma, beta, w1, w1_sb, w1_in, x_all, acc, mean_var, rstd, nmr):
    with ExitStack() as ctx:
        def sb(name, shape, dt=F32):
            return ctx.enter_context(nc.sbuf_tensor(name, shape, dt))

        def sem(name):
            return ctx.enter_context(nc.semaphore(name))

        gam = sb("gam", [P, D])
        bet = sb("bet", [P, D])
        stats = sb("stats4", [P, GRP, 6])
        mv = sb("mv4", [P, GRP, 2])
        spare = sb("spare4", [P, 2])
        rden = sb("rden", [P, GRP, HEADS])
        grp_a = sb("grp_a", [P, GRP, D])
        grp_b = sb("grp_b", [P, GRP, D])

        par_in = sem("par_in")
        dve_chain = sem("dve_chain4")
        norm_a = sem("norm_a")
        norm_a_used = sem("norm_a_used")
        var2 = sem("var2")
        std2 = sem("std2")
        scale2 = sem("scale2")
        norm_b = sem("norm_b")
        low_ready = sem("low_ready")
        exp_ready = sem("exp_ready")
        norm_b_used = sem("norm_b_used")
        var3 = sem("var3")
        std3 = sem("std3")
        scale3 = sem("scale3")
        block = ctx.enter_context(nc.Block())

        def tile(k, it):
            return bass.ds(it * GRP + k, 1)

        def group(it):
            return bass.ds(it * GRP, GRP)

        @block.sync
        def _(sp):
            sp.dma_start(gam[:, :], gamma.unsqueeze(0).to_broadcast([P, D])).then_inc(par_in, 16)
            sp.dma_start(bet[:, :], beta.unsqueeze(0).to_broadcast([P, D])).then_inc(par_in, 16)
            for q in range(4):
                e = slice(EXPERTS // 4 * q, EXPERTS // 4 * (q + 1))
                sp.dma_start(w1_sb[:, e, :, :].rearrange("p e a f -> p (e a) f"),
                             w1[e, :, :].rearrange("e (a p) f -> p (e a) f", p=P)).then_inc(w1_in, 16)

        @block.scalar
        def _(act):
            with act.Fori(0, NGRP) as it:
                for k in range(GRP):
                    act.wait_ge(norm_a_used, it + 1)
                    act.activation(grp_a[:, k, :], one(x_all[:, tile(k, it), :]), ACT.Identity,
                                   bias=nmr[:, tile(k, it)], scale=rstd[:, tile(k, it)]).then_inc(norm_a, 1)
            act.wait_ge(var2, 1)
            act.activation(rstd[:, :], nmr[:, :], ACT.Sqrt).then_inc(std2, 1)
            act.wait_ge(scale2, 1)
            act.preload_act_table(ACT.Exp)
            with act.Fori(0, NGRP) as it:
                for k in range(GRP):
                    act.wait_ge(norm_b_used, it + 1)
                    act.activation(grp_a[:, k, :], acc[:, tile(k, it), 0:D].rearrange("p a d -> p (a d)"), ACT.Identity,
                                   bias=nmr[:, tile(k, it)], scale=rstd[:, tile(k, it)]).then_inc(norm_b, 1)
                act.wait_ge(low_ready, it + 1)
                act.activation(grp_b[:, :, :], grp_b[:, :, :], ACT.Exp).then_inc(exp_ready, 1)
            act.wait_ge(var3, 1)
            act.activation(rstd[:, :], nmr[:, :], ACT.Sqrt).then_inc(std3, 1)

        @block.vector
        def _(dve):
            link = Chain(dve, dve_chain)
            dve.memset(spare[:, 0:1], 0.0).then_inc(norm_a_used, 1)
            with dve.Fori(0, NGRP) as it:
                link.loop(it, 0, 8)
                link(dve.tensor_scalar(rden[:, :, :], acc[:, group(it), D:SUM], 1e-30, None, ALU.max))
                link(dve.reciprocal(rden[:, :, :], rden[:, :, :]))
                num = acc[:, group(it), 0:D].rearrange("p k (h d) -> p k h d", d=HD)
                link(dve.tensor_tensor(num, num, rden[:, :, :].unsqueeze(3).to_broadcast([P, GRP, HEADS, HD]), ALU.mult))
                dve.wait_ge(norm_a, it * GRP + GRP)
                rows = acc[:, group(it), 0:D]
                link(dve.tensor_tensor(rows, rows, grp_a[:, :, :], ALU.add))
                link(dve.memset(spare[:, 0:1], 0.0))
                dve.memset(spare[:, 0:1], 0.0).then_inc(norm_a_used, 1)
                group_stats(dve, link, lambda k: one(acc[:, tile(k, it), 0:D]), stats, mv, spare, mean_var, it)
            link.end(NGRP)
            scales(dve, link, mean_var, rstd, nmr, var2, std2, scale2)
            dve.wait_ge(par_in, 32)
            dve.memset(spare[:, 0:1], 0.0).then_inc(norm_b_used, 1)
            with dve.Fori(0, NGRP) as it:
                link.loop(it, 0, 7)
                dve.wait_ge(norm_b, it * GRP + GRP)
                link(dve.tensor_tensor(grp_a[:, :, :], grp_a[:, :, :], spread_tiles(gam[:, :]), ALU.mult))
                link(dve.tensor_tensor(grp_a[:, :, :], grp_a[:, :, :], spread_tiles(bet[:, :]), ALU.add))
                dve.tensor_scalar(grp_b[:, :, :], grp_a[:, :, :], 0.0, None, ALU.min).then_inc(low_ready, 1)
                dve.wait_ge(exp_ready, it + 1)
                link(dve.scalar_tensor_tensor(grp_b[:, :, :], grp_a[:, :, :], 0.0, grp_b[:, :, :], ALU.max, ALU.add))
                dve.memset(spare[:, 0:1], 0.0).then_inc(norm_b_used, 1)
                rows = x_all[:, group(it), :]
                link(dve.scalar_tensor_tensor(rows, grp_b[:, :, :], -1.0, rows, ALU.add, ALU.add))
                group_stats(dve, link, lambda k: one(x_all[:, tile(k, it), :]), stats, mv, spare, mean_var, it)
            link.end(NGRP)
            scales(dve, link, mean_var, rstd, nmr, var3, std3, scale3)


def route(nc, gate_w, gate_b, w2, w2_sb, w2_in, dispatched, x_all, ident, rstd, nmr, slots, gates, taken):
    with ExitStack() as ctx:
        def sb(name, shape, dt=F32):
            return ctx.enter_context(nc.sbuf_tensor(name, shape, dt))

        def pb(name, shape, dt=F32):
            return ctx.enter_context(nc.psum_tensor(name, shape, dt))

        def sem(name):
            return ctx.enter_context(nc.semaphore(name))

        gw = sb("gw", [P, KD, EXPERTS])
        gb = sb("gb", [1, EXPERTS])
        ones_row = sb("ones_row", [1, P])
        ones_sq = sb("ones_sq", [P, P], BF16)
        before = sb("before", [P, P], BF16)
        expert_no = sb("expert_no", [P, EXPERTS])
        expert_row = sb("expert_row", [P, EXPERTS])
        valid = sb("valid", [P, TILES])
        pads = sb("pads", [P, TILES, 2])
        spare = sb("spare_r", [P, 1])
        y = sb("y", [P, 2, GRP, D])
        yT = sb("yT", [P, GRP, D])
        top = sb("top", [P, GRP, 8])
        top_i = sb("top_i", [P, GRP, 8], U32)
        top_f = sb("top_f", [P, GRP, 2])
        logits = sb("logits", [P, GRP, EXPERTS])
        diff = sb("diff", [P, GRP])
        ediff = sb("ediff", [P, GRP])
        rsum = sb("rsum", [P, GRP])
        pick = sb("pick", [P, 2, GRP, EXPERTS])
        both = sb("both4", [P, GRP, EXPERTS])
        both_h = sb("both_h", [P, GRP, EXPERTS], BF16)
        base = sb("base", [P, GRP + 1, EXPERTS])
        place = sb("place", [P, GRP, EXPERTS])
        hit = sb("hit", [P, 2, GRP, EXPERTS])
        slot_f = sb("slot_f", [P, 2, GRP])
        slot_g = sb("slot_g", [P, 2, 2, GRP], I32)
        ps_t = [pb(f"ps4_t{i}", [P, 512]) for i in range(2)]
        ps_l = pb("ps4_l", [P, 512])
        ps_before = pb("ps4_before", [P, 512])
        ps_total = pb("ps4_total", [P, 512])

        par_in = sem("par_in_r")
        consts = sem("consts4")
        dve_chain = sem("dve_chain_r")
        y_ready = sem("y_ready")
        y_tr = sem("y_tr")
        yT_ready = sem("yT_ready")
        logits_done = sem("logits_done")
        logits_read = sem("logits_read")
        diff_ready = sem("diff_ready")
        ediff_ready = sem("ediff_ready")
        both_ready = sem("both_ready4")
        ranks_done = sem("ranks_done")
        slots_ready = sem("slots_ready")
        pool_turn = sem("pool_turn4")
        sent = [sem(f"sent{i}") for i in range(2)]
        SENT = 16 * 2 * GRP
        block = ctx.enter_context(nc.Block())

        def tile(k, g):
            return bass.ds(g * GRP + k, 1)

        def group(g):
            return bass.ds(g * GRP, GRP)

        def over_groups(eng, body):
            body(0, 0, None)
            body(1, 1, None)
            with eng.Fori(1, NGRP // 2) as it:
                body(it * 2, 0, it)
                body(it * 2 + 1, 1, it)
            body(NGRP - 1, 0, NGRP // 2)

        @block.sync
        def _(sp):
            sp.dma_start(gw[:, :, :], gate_w.rearrange("(a p) e -> p a e", p=P)).then_inc(par_in, 16)
            sp.dma_start(gb[:, :], gate_b.unsqueeze(0)).then_inc(par_in, 16)
            for q in range(4):
                e = slice(EXPERTS // 4 * q, EXPERTS // 4 * (q + 1))
                sp.dma_start(w2_sb[:, e, :, :].rearrange("p e a f -> p (e a) f"),
                             w2[e, :, :].rearrange("e (a p) f -> p (e a) f", p=P)).then_inc(w2_in, 16)

        @block.gpsimd
        def _(pool):
            pool.memset(ones_row[:, :], 1.0).then_inc(consts, 1)
            pool.memset(ones_sq[:, :], 1.0).then_inc(consts, 1)
            pool.memset(before[:, :], 1.0).then_inc(consts, 1)
            pool.memset(valid[:, :], 1.0).then_inc(consts, 1)
            pool.memset(pads[:, :, :], 0.0).then_inc(consts, 1)
            pool.memset(base[:, 0, :], 0.0).then_inc(consts, 1)
            pool.iota(expert_no[:, :], pattern=[[1, EXPERTS]], base=0, channel_multiplier=0,
                      allow_small_or_imprecise_dtypes=True).then_inc(consts, 1)
            pool.iota(expert_row[:, :], pattern=[[CAP, EXPERTS]], base=0, channel_multiplier=0,
                      allow_small_or_imprecise_dtypes=True).then_inc(consts, 1)
            pool.wait_ge(consts, 8)
            pool.affine_select(out=before[:, :], in_=before[:, :], compare_op=ALU.is_gt, fill=0.0, base=0,
                               pattern=[[1, P]], channel_multiplier=-1).then_inc(consts, 1)
            pool.affine_select(out=valid[:, FULL:TILES], in_=valid[:, FULL:TILES], compare_op=ALU.is_gt, fill=0.0,
                               base=LAST, pattern=[[0, 1]], channel_multiplier=-1).then_inc(consts, 1)
            pool.iota(pads[:, FULL, :], pattern=[[P, 2]], base=PADROWS, channel_multiplier=1,
                      allow_small_or_imprecise_dtypes=True).then_inc(consts, 1)
            pool.wait_ge(consts, 11)
            pool.affine_select(out=pads[:, FULL, :], in_=pads[:, FULL, :], compare_op=ALU.is_ge, fill=0.0,
                               base=-LAST, pattern=[[0, 2]], channel_multiplier=1).then_inc(consts, 1)
            pool.wait_ge(consts, 12)

            def send(g, s, n):
                pool.wait_ge(slots_ready, g + 1)
                pool.sem_inc(pool_turn, 1)
                for k in range(GRP):
                    for c in range(2):
                        pool.indirect_dma_start(dispatched, bass.IndirectOffsetOnAxis(ap=slot_g[:, s, c, k:k + 1], axis=0),
                                                y[:, s, k, :], None).then_inc(sent[s], 16)

            over_groups(pool, send)
            pool.wait_ge(sent[0], SENT * ((NGRP + 1) // 2))
            pool.wait_ge(sent[1], SENT * (NGRP // 2))

        @block.scalar
        def _(act):
            act.preload_act_table(ACT.Exp)

            def norm(g, s, k):
                act.activation(y[:, s, k, :], one(x_all[:, tile(k, g), :]), ACT.Identity,
                               bias=nmr[:, tile(k, g)], scale=rstd[:, tile(k, g)]).then_inc(y_ready, 1)

            def router(g, s, n):
                if n is not None:
                    act.wait_ge(sent[s], n * SENT)
                norm(g, s, 0)
                for k in range(GRP):
                    if k < GRP - 1:
                        norm(g, s, k + 1)
                    act.wait_ge(y_tr, g * GRP + k + 1)
                    if not (n is None and s == 0):
                        act.wait_ge(logits_done, g)
                    act.activation(yT[:, k, :], ps_t[k % 2][:, 0:D], ACT.Copy).then_inc(yT_ready, 1)
                act.wait_ge(diff_ready, g + 1)
                act.activation(ediff[:, :], diff[:, :], ACT.Exp).then_inc(ediff_ready, 1)

            over_groups(act, router)

        @block.tensor
        def _(pe):
            pe.wait_ge(par_in, 32)
            pe.wait_ge(consts, 12)

            def router(g, s, n):
                first = n is None and s == 0
                if not first:
                    pe.wait_ge(logits_read, g)

                def turn(k):
                    pe.wait_ge(y_ready, g * GRP + k + 1)
                    if not (first and k < 2):
                        pe.wait_ge(yT_ready, g * GRP + k - (1 if k else 0))
                    for a in range(KD):
                        last = pe.transpose(ps_t[k % 2][:, a * P:(a + 1) * P], y[:, s, k, a * P:(a + 1) * P], ident[:, :])
                    last.then_inc(y_tr, 1)

                turn(0)
                for k in range(GRP):
                    if k < GRP - 1:
                        turn(k + 1)
                    pe.wait_ge(yT_ready, g * GRP + k + 1)
                    to = ps_l[:, k * EXPERTS:(k + 1) * EXPERTS]
                    for a in range(KD):
                        pe.matmul(to, yT[:, k, a * P:(a + 1) * P], gw[:, a, :], start=(a == 0), stop=False)
                    last = pe.matmul(to, ones_row[:, :], gb[:, :], start=False, stop=True)
                last.then_inc(logits_done, 1)
                pe.wait_ge(both_ready, g + 1)
                flat = both_h[:, :, :].rearrange("p k e -> p (k e)")
                pe.matmul(ps_before[:, 0:GRP * EXPERTS], before[:, :], flat, start=True, stop=True)
                pe.matmul(ps_total[:, 0:GRP * EXPERTS], ones_sq[:, :], flat, start=True, stop=True).then_inc(ranks_done, 1)

            over_groups(pe, router)

        @block.vector
        def _(dve):
            link = Chain(dve, dve_chain)
            dve.wait_ge(consts, 12)

            def experts(v):
                return v.unsqueeze(1).to_broadcast([P, GRP, EXPERTS])

            def per_tile(v):
                return v.unsqueeze(2).to_broadcast([P, GRP, EXPERTS])

            def router(it, s, n):
                dve.wait_ge(logits_done, it + 1)
                link(dve.tensor_copy(logits[:, :, :].rearrange("p k e -> p (k e)"), ps_l[:, 0:GRP * EXPERTS]))
                dve.memset(spare[:, :], 0.0).then_inc(logits_read, 1)
                for k in range(GRP):
                    last = dve.max(top[:, k, :], logits[:, k, :])
                link(last)
                dve.memset(spare[:, :], 0.0)
                for k in range(GRP):
                    last = dve.max_index(top_i[:, k, :], top[:, k, :], logits[:, k, :])
                link(last)
                dve.tensor_tensor(diff[:, :], top[:, :, 1], top[:, :, 0], ALU.subtract).then_inc(diff_ready, 1)
                link(dve.tensor_copy(top_f[:, :, :], top_i[:, :, 0:2]))
                for c in range(2):
                    last = dve.tensor_tensor(pick[:, c, :, :], experts(expert_no[:, :]), per_tile(top_f[:, :, c]), ALU.is_equal)
                link(last)
                link(dve.tensor_tensor(both[:, :, :], pick[:, 0, :, :], pick[:, 1, :, :], ALU.add))
                dve.tensor_tensor(both_h[:, :, :], both[:, :, :], per_tile(valid[:, group(it)]), ALU.mult).then_inc(both_ready, 1)
                dve.wait_ge(ediff_ready, it + 1)
                link(dve.tensor_scalar(rsum[:, :], ediff[:, :], 1.0, None, ALU.add))
                link(dve.reciprocal(rsum[:, :], rsum[:, :]))
                dve.tensor_copy(gates[:, group(it), 0], rsum[:, :])
                dve.tensor_tensor(gates[:, group(it), 1], rsum[:, :], ediff[:, :], ALU.mult)
                dve.wait_ge(ranks_done, it + 1)
                for k in range(GRP):
                    link(dve.tensor_tensor(base[:, k + 1, :], base[:, k, :], ps_total[:, k * EXPERTS:(k + 1) * EXPERTS], ALU.add))
                link(dve.tensor_tensor(place[:, :, :], base[:, 0:GRP, :],
                                       ps_before[:, 0:GRP * EXPERTS].rearrange("p (k e) -> p k e", k=GRP), ALU.add))
                link(dve.tensor_tensor(place[:, :, :], place[:, :, :], experts(expert_row[:, :]), ALU.add))
                for c in range(2):
                    last = dve.tensor_tensor(hit[:, c, :, :], place[:, :, :], pick[:, c, :, :], ALU.mult)
                link(last)
                link(dve.tensor_reduce(slot_f[:, :, :], hit[:, :, :, :], AX.X, ALU.add))
                v2 = valid[:, group(it)].unsqueeze(1).to_broadcast([P, 2, GRP])
                link(dve.tensor_tensor(slot_f[:, :, :], slot_f[:, :, :], v2, ALU.mult))
                link(dve.tensor_tensor(slot_f[:, :, :], slot_f[:, :, :], pads[:, group(it), :].rearrange("p k c -> p c k"), ALU.add))
                if n is not None:
                    dve.wait_ge(sent[s], n * SENT)
                dve.tensor_copy(slots[:, group(it), :].rearrange("p k c -> p c k"), slot_f[:, :, :])
                dve.tensor_copy(slot_g[:, s, :, :], slot_f[:, :, :]).then_inc(slots_ready, 1)
                link(dve.tensor_copy(base[:, 0, :], base[:, GRP, :]))

            ROUTER_LINKS = 22
            router(0, 0, None)
            router(1, 1, None)
            with dve.Fori(1, NGRP // 2) as it:
                link.loop(it, 1, 2 * ROUTER_LINKS)
                router(it * 2, 0, it)
                router(it * 2 + 1, 1, it)
            link.end(NGRP // 2 - 1)
            router(NGRP - 1, 0, NGRP // 2)
            link(dve.tensor_copy(taken[:, :], base[:, 0, :]))


def scales(dve, link, mean_var, rstd, nmr, var, std, scale):
    dve.tensor_scalar(nmr[:, :], mean_var[:, :, 1], EPS, None, ALU.add).then_inc(var, 1)
    dve.wait_ge(std, 1)
    link(dve.reciprocal(rstd[:, :], rstd[:, :]))
    dve.scalar_tensor_tensor(nmr[:, :], mean_var[:, :, 0], -1.0, rstd[:, :], ALU.mult, ALU.mult).then_inc(scale, 1)


def stage5(nc, dispatched, taken, slots, rows_l, expert_l, passes_i):
    with ExitStack() as ctx:
        def sb(name, shape, dt=F32):
            return ctx.enter_context(nc.sbuf_tensor(name, shape, dt))

        def sem(name):
            return ctx.enter_context(nc.semaphore(name))

        X1 = EXPERTS + 1
        L = FFN_LIST
        zeros = sb("zeros", [P, D])
        need_i = sb("need_i", [P, EXPERTS], I32)
        need = sb("need", [P, EXPERTS])
        ones = sb("ones5", [P, EXPERTS])
        begin = sb("begin", [P, X1])
        key = sb("key5", [P, X1])
        delta = sb("delta5", [P, X1])
        region = sb("region", [P, X1])
        tile_no = sb("tile_no", [P, L])
        ge = sb("ge5", [P, L, X1])
        slot_f = sb("slot_f5", [P, TILES * 2])
        shift_by = sb("shift_by", [P, TILES * 2])
        over = sb("over5", [P, TILES * 2, X1])
        res = sb("res5", [P, L])
        row_end = sb("row_end", [P, EXPERTS])
        row_end_i = sb("row_end_i", [P, EXPERTS], I32)
        passes_f = sb("passes_f", [P, 1])
        consts = sem("consts5")
        dve_chain = sem("dve_chain5")
        ends_ready = sem("ends_ready")
        zeros_out = sem("zeros_out")
        block = ctx.enter_context(nc.Block())

        @block.gpsimd
        def _(pool):
            pool.memset(zeros[:, :], 0.0).then_inc(consts, 1)
            pool.iota(tile_no[:, :], pattern=[[1, L]], base=0, channel_multiplier=0,
                      allow_small_or_imprecise_dtypes=True).then_inc(consts, 1)
            pool.iota(region[:, :], pattern=[[CAP, X1]], base=0, channel_multiplier=0,
                      allow_small_or_imprecise_dtypes=True).then_inc(consts, 1)

        @block.sync
        def _(sp):
            sp.wait_ge(consts, 3)
            for j in range(FFN_SPARE):
                sp.dma_start(dispatched[PADFFN + j * P:PADFFN + (j + 1) * P, :], zeros[:, :]).then_inc(zeros_out, 16)
            sp.wait_ge(ends_ready, 1)
            for e in range(EXPERTS):
                end = sp.value_load(row_end_i[0:1, e:e + 1], min_val=0, max_val=DROWS - P)
                sp.dma_start(dispatched[bass.ds(end, P), :], zeros[:, :]).then_inc(zeros_out, 16)
            sp.wait_ge(zeros_out, 16 * (EXPERTS + FFN_SPARE))

        @block.vector
        def _(dve):
            link = Chain(dve, dve_chain)
            dve.wait_ge(consts, 3)
            link(dve.tensor_tensor(row_end[:, :], taken[:, :], region[:, 0:EXPERTS], ALU.add))
            dve.tensor_copy(row_end_i[:, :], row_end[:, :]).then_inc(ends_ready, 1)
            link(dve.tensor_scalar(need[:, :], taken[:, :], float(P - 1), None, ALU.add))
            link(dve.tensor_copy(need_i[:, :], need[:, :]))
            link(dve.tensor_scalar(need_i[:, :], need_i[:, :], P.bit_length() - 1, None, ALU.arith_shift_right))
            link(dve.tensor_copy(need[:, :], need_i[:, :]))
            dve.memset(ones[:, :], 1.0)
            link(dve.memset(begin[:, 0:1], 0.0))
            link(dve.tensor_tensor_scan(begin[:, 1:X1], ones[:, :], need[:, :], 0.0, ALU.mult, ALU.add))
            link(dve.scalar_tensor_tensor(key[:, :], begin[:, :], -float(P), region[:, :], ALU.mult, ALU.add))
            link(dve.tensor_scalar(key[:, EXPERTS:X1], key[:, EXPERTS:X1], float(PADFFN - PADROWS), None, ALU.add))
            link(dve.tensor_copy(delta[:, 0:1], key[:, 0:1]))
            link(dve.tensor_tensor(delta[:, 1:X1], key[:, 1:X1], key[:, 0:EXPERTS], ALU.subtract))
            link(dve.tensor_tensor(ge[:, :, :], tile_no[:, :].unsqueeze(2).to_broadcast([P, L, X1]),
                                   begin[:, :].unsqueeze(1).to_broadcast([P, L, X1]), ALU.is_ge))
            link(dve.tensor_reduce(res[:, :], ge[:, :, 1:X1], AX.X, ALU.add))
            dve.memset(expert_l[:, 0:4], 0)
            link(dve.tensor_scalar(expert_l[:, 4:L + 4], res[:, :], float(EXPERTS - 1), None, ALU.min))
            link(dve.tensor_tensor(ge[:, :, :], ge[:, :, :], delta[:, :].unsqueeze(1).to_broadcast([P, L, X1]), ALU.mult))
            link(dve.tensor_reduce(res[:, :], ge[:, :, :], AX.X, ALU.add))
            link(dve.scalar_tensor_tensor(res[:, :], tile_no[:, :], float(P), res[:, :], ALU.mult, ALU.add))
            link(dve.tensor_scalar(rows_l[:, :], res[:, :], float(DROWS - P), None, ALU.min))
            flat = slots[:, :, :].rearrange("p t c -> p (t c)")
            link(dve.tensor_copy(slot_f[:, :], flat))
            link(dve.tensor_tensor(over[:, :, :], slot_f[:, :].unsqueeze(2).to_broadcast([P, TILES * 2, X1]),
                                   region[:, :].unsqueeze(1).to_broadcast([P, TILES * 2, X1]), ALU.is_ge))
            link(dve.tensor_tensor(over[:, :, :], over[:, :, :], delta[:, :].unsqueeze(1).to_broadcast([P, TILES * 2, X1]), ALU.mult))
            link(dve.tensor_reduce(shift_by[:, :], over[:, :, :], AX.X, ALU.add))
            link(dve.tensor_tensor(flat, slot_f[:, :], shift_by[:, :], ALU.subtract))
            link(dve.tensor_scalar(passes_f[:, :], begin[:, EXPERTS:X1], float(FFN_LAG + FFN_BODY - 1), None, ALU.add))
            link(dve.tensor_copy(passes_i[:, :], passes_f[:, :]))
            link(dve.tensor_scalar(passes_i[:, :], passes_i[:, :], FFN_BODY.bit_length() - 1, None, ALU.arith_shift_right))


def stage6(nc, b1, b2, w1_sb, w2_sb, w1_in, w2_in, dispatched, expert_out, ident, rows_l, expert_l, passes_i):
    with ExitStack() as ctx:
        def sb(name, shape, dt=F32):
            return ctx.enter_context(nc.sbuf_tensor(name, shape, dt))

        def pb(name, shape, dt=F32):
            return ctx.enter_context(nc.psum_tensor(name, shape, dt))

        def sem(name):
            return ctx.enter_context(nc.semaphore(name))

        B = FFN_BODY
        b1T = sb("b1T", [P, EXPERTS, KF])
        b2_t = sb("b2_t", [P, B, D])
        xt = sb("xt", [P, B, D])
        xT = sb("xT", [P, 2, D])
        hid = sb("hid", [P, 2, FF])
        hidT = sb("hidT", [P, 2, FF])
        o_sb = sb("o_sb", [P, 2, D])
        ps_x = [pb(f"ps_x{i}", [P, 512]) for i in range(2)]
        ps_h = [pb(f"ps5_h{i}", [P, 512]) for i in range(2)]
        ps_ht = [pb(f"ps_ht{i}", [P, 512]) for i in range(2)]
        ps_o = [pb(f"ps_o{i}", [P, 512]) for i in range(2)]

        b1_in = sem("b1_in")
        b2_in = [sem(f"b2_in{i}") for i in range(B)]
        x_in = [sem(f"x5_in{i}") for i in range(B)]
        x_tr = sem("x_tr")
        xT_ready = sem("xT_ready")
        h_done = sem("h_done")
        h_copied = sem("h_copied")
        h_tr = sem("h_tr")
        hT_ready = sem("hT_ready")
        o_done = sem("o_done")
        o_ready = sem("o_ready")
        o_out = [sem(f"o_out{i}") for i in range(2)]
        sp_turn = sem("sp_turn5")
        block = ctx.enter_context(nc.Block())
        MAXPASS = (MAXFFN + FFN_LAG + B - 1) // B

        def pass_count(eng):
            return eng.value_load(passes_i[0:1, 0:1], min_val=3, max_val=MAXPASS)

        def expert(eng, i, back):
            return eng.value_load(expert_l[0:1, bass.ds(i + (4 - back), 1)], min_val=0, max_val=EXPERTS - 1)

        def row(eng, i):
            return eng.value_load(rows_l[0:1, bass.ds(i, 1)], min_val=0, max_val=DROWS - P)

        @block.sync
        def _(sp):
            passes = pass_count(sp)

            def load(s, i, head):
                r = row(sp, i)
                if not head:
                    sp.wait_ge(x_tr, i - B + 1)
                    sp.sem_inc(sp_turn, 1)
                sp.dma_start(xt[:, s, :], dispatched[bass.ds(r, P), :]).then_inc(x_in[s], 16)

            def store(s, i):
                sp.wait_ge(o_ready, i + 1)
                sp.sem_inc(sp_turn, 1)
                sp.dma_start(expert_out[bass.ds(i * P, P), :], o_sb[:, s, :]).then_inc(o_out[s], 16)

            def load_b2(s, i):
                e = expert(sp, i, 0)
                sp.dma_start(b2_t[:, s, :], b2[bass.ds(e, 1), :].to_broadcast([P, D])).then_inc(b2_in[s], 16)

            for i in range(FFN_AHEAD):
                load(i, i, True)
            for i in range(B):
                load_b2(i, i)
            for i in range(B):
                load((i + FFN_AHEAD) % B, i + FFN_AHEAD, i + FFN_AHEAD < B)
                if i >= FFN_LAG:
                    store((i - FFN_LAG) % 2, i - FFN_LAG)
                    load_b2((i + 1) % B, i + 1)
            with sp.Fori(1, passes) as it:
                for k in range(B):
                    load((k + FFN_AHEAD) % B, it * B + k + FFN_AHEAD, False)
                    store((k - FFN_LAG) % 2, it * B + (k - FFN_LAG))
                    load_b2((k + 1) % B, it * B + (k + 1))
            sp.sem_inc(o_out[0], 16)
            sp.sem_inc(o_out[1], 32)
            for q in range(2):
                sp.wait_ge(o_out[q], passes * (16 * B // 2))
            for k in range(B):
                sp.wait_ge(b2_in[k], passes * 16 + (16 if k == 0 else 0))
            sp.sem_inc(sp_turn, 1)

        @block.scalar
        def _(act):
            act.dma_start(b1T[:, :, :].rearrange("p e a -> p (e a)"), b1.rearrange("e (a p) -> p (e a)", p=P)).then_inc(b1_in, 16)
            act.preload_act_table(ACT.Relu)
            act.wait_ge(b1_in, 16)
            passes = pass_count(act)

            def step(k, i, head):
                s = k % 2
                act.wait_ge(x_tr, i + 1)
                if not (head and i < 2):
                    act.wait_ge(h_done, i - 1)
                act.activation(xT[:, s, :], ps_x[s][:, 0:D], ACT.Copy).then_inc(xT_ready, 1)
                if not (head and i < 2):
                    e = expert(act, i, 2)
                    act.wait_ge(h_tr, i - 1)
                    if not (head and i < 4):
                        act.wait_ge(o_done, i - 3)
                    for j in range(KF):
                        last = act.activation(hidT[:, s, j * P:(j + 1) * P], ps_ht[s][:, j * P:(j + 1) * P], ACT.Relu,
                                              bias=b1T[:, bass.ds(e, 1), j:j + 1].rearrange("p a b -> p (a b)"))
                    last.then_inc(hT_ready, 1)

            for i in range(2 * B):
                step(i % B, i, True)
            with act.Fori(2, passes) as it:
                for k in range(B):
                    step(k, it * B + k, False)

        @block.tensor
        def _(pe):
            pe.wait_ge(w1_in, 64)
            pe.wait_ge(w2_in, 64)
            passes = pass_count(pe)

            def step(k, i, head):
                s, o = k % 2, 1 - k % 2
                pe.wait_ge(x_in[k], 16 * (i // B + 1) if head else (i - k) * (16 // B) + 16)
                if not (head and i < 2):
                    pe.wait_ge(xT_ready, i - 1)
                for a in range(KD):
                    last = pe.transpose(ps_x[s][:, a * P:(a + 1) * P], xt[:, k, a * P:(a + 1) * P], ident[:, :])
                last.then_inc(x_tr, 1)
                if not (head and i < 1):
                    e = expert(pe, i, 1)
                    pe.wait_ge(xT_ready, i)
                    if not (head and i < 3):
                        pe.wait_ge(h_copied, i - 2)
                    for a in range(KD):
                        last = pe.matmul(ps_h[o][:, :], xT[:, o, a * P:(a + 1) * P],
                                         w1_sb[:, bass.ds(e, 1), a, :].rearrange("p a b -> p (a b)"),
                                         start=(a == 0), stop=(a == KD - 1))
                    last.then_inc(h_done, 1)
                if not (head and i < 2):
                    pe.wait_ge(h_copied, i - 1)
                    if not (head and i < 4):
                        pe.wait_ge(hT_ready, i - 3)
                    for j in range(KF):
                        last = pe.transpose(ps_ht[s][:, j * P:(j + 1) * P], hid[:, s, j * P:(j + 1) * P], ident[:, :])
                    last.then_inc(h_tr, 1)
                if not (head and i < 3):
                    e = expert(pe, i, 3)
                    pe.wait_ge(hT_ready, i - 2)
                    if not (head and i < 5):
                        pe.wait_ge(o_ready, i - 4)
                    for j in range(KF):
                        last = pe.matmul(ps_o[o][:, 0:D], hidT[:, o, j * P:(j + 1) * P],
                                         w2_sb[:, bass.ds(e, 1), j, :].rearrange("p a b -> p (a b)"),
                                         start=(j == 0), stop=(j == KF - 1))
                    last.then_inc(o_done, 1)

            for i in range(2 * B):
                step(i % B, i, True)
            with pe.Fori(2, passes) as it:
                for k in range(B):
                    step(k, it * B + k, False)

        @block.vector
        def _(dve):
            passes = pass_count(dve)

            def step(k, i, head):
                o = 1 - k % 2
                if not (head and i < 1):
                    dve.wait_ge(h_done, i)
                    if not (head and i < 3):
                        dve.wait_ge(h_tr, i - 2)
                    dve.tensor_copy(hid[:, o, :], ps_h[o][:, :]).then_inc(h_copied, 1)
                if not (head and i < 3):
                    dve.wait_ge(b2_in[(k - 3) % B], 16 * ((i - 3) // B + 1) if head else (i - 3 - (k - 3) % B) * (16 // B) + 16)
                    dve.wait_ge(o_done, i - 2)
                    if not (head and i < 5):
                        dve.wait_ge(o_out[o], ((i - 3) // 2) * 16 if head else (i - 3 - o) * 8)
                    dve.tensor_tensor(o_sb[:, o, :], ps_o[o][:, 0:D], b2_t[:, (k - 3) % B, :], ALU.add).then_inc(o_ready, 1)

            for i in range(2 * B):
                step(i % B, i, True)
            with dve.Fori(2, passes) as it:
                for k in range(B):
                    step(k, it * B + k, False)


def stage7(nc, fgamma, fbeta, expert_out, out, x_all, mean_var, rstd, nmr, slots, gates):
    with ExitStack() as ctx:
        def sb(name, shape, dt=F32):
            return ctx.enter_context(nc.sbuf_tensor(name, shape, dt))

        def sem(name):
            return ctx.enter_context(nc.semaphore(name))

        gam = sb("fgam", [P, D])
        bet = sb("fbet", [P, D])
        slot_g = sb("slot_g7", [P, 2, GRP, 2], I32)
        gate_g = sb("gate_g7", [P, GRP, 2])
        back = sb("back", [P, 2, GRP, 2, D])
        y = sb("y7", [P, GRP, D])
        part = sb("part", [P, GRP, D])
        moe = sb("moe", [P, TILES, D])
        stats = sb("stats7", [P, GRP, 6])
        mv = sb("mv7", [P, GRP, 2])
        spare = sb("spare7", [P, 2])
        normed = sb("normed", [P, 2, GRP, D])

        par_in = sem("par_in7")
        dve_chain = sem("dve_chain7")
        slots_staged = sem("slots_staged")
        pool_turn = sem("pool_turn7")
        came = [sem(f"came{i}") for i in range(2)]
        y_ready = sem("y_ready7")
        group_used = sem("group_used7")
        var4 = sem("var4")
        std4 = sem("std4")
        scale4 = sem("scale4")
        norm_ready = sem("norm_ready7")
        out_ready = sem("out_ready")
        out_sent = [sem(f"out_sent{i}") for i in range(2)]
        block = ctx.enter_context(nc.Block())

        def tile(k, it):
            return bass.ds(it * GRP + k, 1)

        def group(it):
            return bass.ds(it * GRP, GRP)

        def over_groups(eng, body):
            body(0, 0, 0)
            with eng.Fori(0, (NGRP - 3) // 2) as it:
                body(it * 2 + 1, 1, it)
                body(it * 2 + 2, 0, it + 1)

        @block.gpsimd
        def _(pool):
            def fetch(g, s, n, last=False):
                pool.wait_ge(slots_staged, g + 1)
                pool.sem_inc(pool_turn, 1)
                for k in range(GRP):
                    m = LAST if last and k == GRP - 1 else P
                    for c in range(2):
                        pool.indirect_dma_start(back[0:m, s, k, c, :], None, expert_out,
                                                bass.IndirectOffsetOnAxis(ap=slot_g[0:m, s, k, c:c + 1], axis=0)).then_inc(came[s], 16)

            over_groups(pool, fetch)
            fetch(NGRP - 2, 1, NGRP // 2 - 1)
            fetch(NGRP - 1, 0, NGRP // 2, last=True)

        @block.scalar
        def _(act):
            def norm_x(it, head):
                for k in range(GRP):
                    if not head:
                        act.wait_ge(group_used, it)
                    act.activation(y[:, k, :], one(x_all[:, tile(k, it), :]), ACT.Identity,
                                   bias=nmr[:, tile(k, it)], scale=rstd[:, tile(k, it)]).then_inc(y_ready, 1)

            act.preload_act_table(ACT.Identity)
            norm_x(0, True)
            with act.Fori(1, NGRP) as it:
                norm_x(it, False)
            act.wait_ge(var4, 1)
            act.activation(rstd[:, :], nmr[:, :], ACT.Sqrt).then_inc(std4, 1)
            act.wait_ge(scale4, 1)
            act.preload_act_table(ACT.Identity)
            for it in range(NGRP):
                for k in range(GRP):
                    if it >= 2:
                        act.wait_ge(out_sent[it % 2], 16 * (it // 2))
                    t = it * GRP + k
                    act.activation(normed[:, it % 2, k, :], moe[:, t, :], ACT.Identity,
                                   bias=nmr[:, t:t + 1], scale=rstd[:, t:t + 1]).then_inc(norm_ready, 1)

        @block.vector
        def _(dve):
            link = Chain(dve, dve_chain)
            dve.memset(back[:, 0, GRP - 1, :, :], 0.0)

            def stage_slots(g, s):
                link(dve.tensor_copy(slot_g[:, s, :, :], slots[:, bass.ds(g * GRP, GRP), :]))
                dve.memset(spare[:, 0:1], 0.0).then_inc(slots_staged, 1)

            def gather_sum(g, s, n, more=True):
                link(dve.tensor_copy(gate_g[:, :, :], gates[:, group(g), :]))
                dve.wait_ge(came[s], n * (32 * GRP) + 32 * GRP)
                dve.wait_ge(y_ready, g * GRP + GRP)
                for c in range(2):
                    for k in range(GRP):
                        last = dve.scalar_tensor_tensor(part[:, k, :] if c == 0 else one(moe[:, tile(k, g), :]),
                                                        back[:, s, k, c, :], gate_g[:, k, c:c + 1],
                                                        y[:, k, :] if c == 0 else part[:, k, :], ALU.mult, ALU.add)
                    link(last)
                dve.memset(spare[:, 0:1], 0.0).then_inc(group_used, 1)
                group_stats(dve, link, lambda k: one(moe[:, tile(k, g), :]), stats, mv, spare, mean_var, g)
                if more:
                    stage_slots(g + 2, s)

            for g in range(2):
                stage_slots(g, g)
            GATHER_LINKS = 7
            link.loop(0, 0, GATHER_LINKS)
            gather_sum(0, 0, 0)
            link.end(1)
            with dve.Fori(0, (NGRP - 3) // 2) as it:
                link.loop(it, 0, 2 * GATHER_LINKS)
                gather_sum(it * 2 + 1, 1, it)
                gather_sum(it * 2 + 2, 0, it + 1)
            link.end((NGRP - 3) // 2)
            gather_sum(NGRP - 2, 1, NGRP // 2 - 1, more=False)
            gather_sum(NGRP - 1, 0, NGRP // 2, more=False)
            scales(dve, link, mean_var, rstd, nmr, var4, std4, scale4)
            dve.wait_ge(par_in, 32)
            for it in range(NGRP):
                z = normed[:, it % 2, :, :]
                dve.wait_ge(norm_ready, it * GRP + GRP)
                link(dve.tensor_tensor(z, z, spread_tiles(gam[:, :]), ALU.mult))
                link(dve.tensor_tensor(z, z, spread_tiles(bet[:, :]), ALU.add))
                dve.tensor_tensor(z, z, x_all[:, it * GRP:(it + 1) * GRP, :], ALU.add).then_inc(out_ready, 1)

        @block.sync
        def _(sp):
            sp.dma_start(gam[:, :], fgamma.unsqueeze(0).to_broadcast([P, D])).then_inc(par_in, 16)
            sp.dma_start(bet[:, :], fbeta.unsqueeze(0).to_broadcast([P, D])).then_inc(par_in, 16)
            for it in range(NGRP):
                sp.wait_ge(out_ready, it + 1)
                t0 = it * GRP
                nt = GRP if it < NGRP - 1 else GRP - 1
                sp.dma_start(out[t0 * P:(t0 + nt) * P, :].rearrange("(t p) d -> p t d", p=P),
                             normed[:, it % 2, 0:nt, :]).then_inc(out_sent[it % 2], 16)
            last = (NGRP - 1) % 2
            sp.dma_start(out[FULL * P:N, :], normed[0:LAST, last, GRP - 1, :]).then_inc(out_sent[last], 16)
            sp.wait_ge(out_sent[last], 16 * ((NGRP + 1) // 2 + 1))
            sp.wait_ge(out_sent[1 - last], 16 * (NGRP // 2))


_INS = ["x", "src", "dst", "L0_gnn_W", "L0_gnn_a_src", "L0_gnn_a_dst", "L0_gnn_gamma", "L0_gnn_beta", "L0_ffn_gate_w",
        "L0_ffn_gate_b", "L0_ffn_w1", "L0_ffn_b1", "L0_ffn_w2", "L0_ffn_b2", "L0_ffn_gamma", "L0_ffn_beta"]


def kernel(**inputs):
    import concourse.bacc as _bacc
    from concourse.bass_utils import run_bass_kernel_spmd as _run

    nc = _bacc.Bacc("TRN2", target_bir_lowering=False, num_devices=1)
    arrays, args = {}, []
    for name in _INS:
        a = np.ascontiguousarray(inputs[name])
        arrays[f"in_{name}_dram"] = a
        args.append(nc.dram_tensor(f"in_{name}_dram", a.shape, mybir.dt.from_np(a.dtype), kind="ExternalInput").ap())
    args.append(nc.dram_tensor("out_0_dram", (N, D), F32, kind="ExternalOutput").ap())
    build(nc, *args)
    r = _run(nc, [arrays], core_ids=[0])
    return r.results[0]["out_0_dram"]
```

```python
from contextlib import ExitStack

import concourse.bass as bass
import numpy as np
from concourse import mybir

F32 = mybir.dt.float32
BF16 = mybir.dt.bfloat16
I32 = mybir.dt.int32
U32 = mybir.dt.uint32
ALU = mybir.AluOpType
ACT = mybir.ActivationFunctionType
AX = mybir.AxisListType

P = 128
N, D = 6250, 256
E = 206250
HEADS, HD = 8, 32
TILES = (N + P - 1) // P
LAST = N - (TILES - 1) * P
FULL = TILES - 1
ROW = D + 2 * HEADS
SUM = D + HEADS
PROJ = D + 2 * HEADS
GRP = 7
NGRP = TILES // GRP
CHUNKS = (E + P - 1) // P
CB = (CHUNKS + P - 1) // P
CFULL = E // P
CREST = E - CFULL * P
PADC = CB * P
COLS = PADC + 8
NODST = 9999.0
BODY = 8
WEIGH, SUMS, JOIN = 2, 3, 4
AHEAD = 5
RING = 4
SLOPE = 0.2
IBLK = 1024
MAXSTEPS = TILES * ((CHUNKS + 1) // 2 + 1)
SLACK = (RING + 1) * BODY
IBLKS = (MAXSTEPS + SLACK) // IBLK + 1
EPS = 1e-5
EXPERTS, FF = 16, 512
KD, KF = D // P, FF // P
CAP = (N + P - 1) // P * P + P
PADROWS = EXPERTS * CAP
PADFFN = PADROWS + 2 * P
MAXFFN = 2 * N // P + EXPERTS
FFN_BODY = 4
FFN_LAG = 3
FFN_AHEAD = 3
FFN_SPARE = FFN_LAG + FFN_BODY + FFN_AHEAD
DROWS = PADFFN + FFN_SPARE * P
FFN_LIST = 128
FFN_TILES = MAXFFN + FFN_LAG + FFN_BODY
MINFFN = 2 * N // P
SAFE = 60.0
FAR = 1e30


LIST_OF = ((AHEAD, True), (AHEAD, False), (0, True), (0, False), (-1, False), (-JOIN, False))
LISTS = len(LIST_OF)
NEXT_CHUNK, NEXT_TILE, CHUNK, TILE, LOOK_TILE, OLD_TILE = range(LISTS)


class Chain:

    def __init__(self, eng, sem):
        self.eng, self.sem, self.n, self.base = eng, sem, 0, 0

    def __call__(self, ins):
        self.n += 1
        ins.then_inc(self.sem, 1)
        self.eng.wait_ge(self.sem, self.base + self.n)

    def loop(self, it, first, per):
        self.start, self.per = self.n, per
        self.base = (it - first) * per

    def end(self, passes):
        assert self.n == self.start + self.per, (self.n, self.start, self.per)
        self.n, self.base = self.start + self.per * passes, 0


class Norms:

    def __init__(self, sem):
        self.var_ready, self.std_ready, self.scale_ready = sem("var_ready"), sem("std_ready"), sem("scale_ready")


def build(nc, x, src, dst, W, a_src, a_dst, gamma, beta, gate_w, gate_b, w1, b1, w2, b2, fgamma, fbeta, out, stage=9):
    ctx = ExitStack()
    with ctx:
        def sb(name, shape, dt=F32):
            return ctx.enter_context(nc.sbuf_tensor(name, shape, dt))

        def sem(name):
            return ctx.enter_context(nc.semaphore(name))

        ctx.enter_context(nc.allow_non_contiguous_dma(reason="small constants"))
        table = nc.dram_tensor("table", [TILES * P, ROW], F32).ap()
        schedule = nc.dram_tensor("schedule", [IBLKS * IBLK // BODY, LISTS * BODY], I32).ap()

        dispatched = nc.dram_tensor("dispatched", [DROWS, D], F32).ap()
        expert_out = nc.dram_tensor("expert_out", [FFN_TILES * P, D], F32).ap()

        x_all = sb("x_all", [P, TILES, D])
        ident = sb("ident", [P, P])
        mean_var = sb("mean_var", [P, TILES, 2])
        rstd = sb("rstd", [P, TILES])
        nmr = sb("nmr", [P, TILES])
        slots = sb("slots", [P, TILES, 2], I32)
        gates = sb("gates", [P, TILES, 2])
        taken = sb("taken", [P, EXPERTS])
        gw = sb("gw", [P, KD, EXPERTS])
        gb = sb("gb", [1, EXPERTS])
        zeroed = sem("zeroed")
        norms = Norms(sem)
        w1_in = sem("w1_in")
        gate_in = sem("gate_in")
        w2_in = sem("w2_in")
        weights = ctx.enter_context(ExitStack())

        def right(name, shape):
            return weights.enter_context(nc.sbuf_tensor(name, shape, F32, side="right"))

        with ExitStack() as graph:
            def gsb(name, shape, dt=F32):
                return graph.enter_context(nc.sbuf_tensor(name, shape, dt))

            acc = gsb("acc", [P, TILES, SUM])
            with ExitStack() as edge:
                def esb(name, shape, dt=F32):
                    return edge.enter_context(nc.sbuf_tensor(name, shape, dt))

                node_iota = esb("node_iota", [P, P])
                neg_first = esb("neg_first", [P, TILES])
                dst_tab = esb("dst_tab", [P, TILES, 2 * HEADS])
                src_sc = esb("src_sc", [P, TILES, HEADS])
                srcT = esb("srcT", [P, COLS], I32)
                dstT = esb("dstT", [P, COLS])
                tile_lo = esb("tile_lo", [P, TILES])
                tile_n = esb("tile_n", [P, TILES])
                counts = esb("counts", [P, 4], I32)
                seg_max = esb("seg_max", [P, TILES, HEADS])
                stage1(nc, x, src, dst, W, a_src, a_dst, table, x_all, acc, ident, node_iota, neg_first, mean_var,
                       rstd, nmr, norms, dst_tab, src_sc, srcT, dstT, tile_lo, tile_n, expert_out, zeroed)
                stage2(nc, table, schedule, zeroed, src_sc, dst_tab, tile_lo, tile_n, counts, seg_max)
                bounds(nc, table, schedule, ident, node_iota, neg_first, dst_tab, srcT, dstT, counts, seg_max)
                stage3(nc, table, schedule, acc, ident, node_iota, neg_first, dst_tab, srcT, dstT, counts)
            w1_sb = right("w1_sb", [P, EXPERTS, KD, FF])
            stage4(nc, gamma, beta, gate_w, gate_b, gw, gb, gate_in, w1, w1_sb, w1_in, x_all, acc, mean_var, rstd, nmr, norms)
        w2_sb = right("w2_sb", [P, EXPERTS, KF, D])
        route(nc, gw, gb, gate_in, w2, w2_sb, w2_in, dispatched, x_all, ident, rstd, nmr, slots, gates, taken)
        rows_l = sb("rows_l", [P, FFN_LIST], I32)
        expert_l = sb("expert_l", [P, FFN_LIST + 4], I32)
        passes_i = sb("passes_i", [P, 1], I32)
        stage5(nc, dispatched, taken, slots, rows_l, expert_l, passes_i)
        stage6(nc, b1, b2, w1_sb, w2_sb, w1_in, w2_in, dispatched, expert_out, ident, rows_l, expert_l, passes_i)
        weights.close()
        stage7(nc, fgamma, fbeta, expert_out, out, x_all, rstd, nmr, slots, gates)


def stage1(nc, x, src, dst, W, a_src, a_dst, table, x_all, acc, ident, node_iota, neg_first, mean_var, rstd, nmr,
           norms, dst_tab, src_sc, srcT, dstT, tile_lo, tile_n, expert_out, zeroed):
    with ExitStack() as ctx:
        def sb(name, shape, dt=F32):
            return ctx.enter_context(nc.sbuf_tensor(name, shape, dt))

        def pb(name, shape, dt=F32):
            return ctx.enter_context(nc.psum_tensor(name, shape, dt))

        def sem(name):
            return ctx.enter_context(nc.semaphore(name))

        w_ext = sb("w_ext", [P, 2, PROJ])
        w_T = sb("w_T", [P, 2, D])
        a_col = sb("a_col", [P, 2, 2])
        a_blk = sb("a_blk", [P, 2, 2 * HEADS])
        stats = sb("stats", [P, GRP, 6])
        mv = sb("mv", [P, GRP, 2])
        spare = sb("spare", [P, 2])
        edges_i = sb("edges_i", [P, 2, CB, P], I32)
        edges_f = sb("edges_f", [P, 2, CB, P])
        real_dst = sb("real_dst", [P, P])
        chunk_min = sb("chunk_min", [P, CB])
        chunk_max = sb("chunk_max", [P, CB])
        chunk_no = sb("chunk_no", [P, CB])
        tile_first = sb("tile_first", [P, TILES])
        over_a = sb("over_a", [P, TILES, CB])
        over_b = sb("over_b", [P, TILES, CB])
        lohi = sb("lohi", [P, 2, TILES])
        lohi_r = sb("lohi_r", [P, 2, TILES])
        span_i = sb("span_i", [P, TILES], I32)
        odd_i = sb("odd_i", [P, TILES], I32)
        span = sb("span", [P, TILES])
        odd = sb("odd", [P, TILES])
        xn = sb("xn", [P, GRP, D])
        xnT = sb("xnT", [P, GRP, D])
        rows = sb("rows", [P, GRP, D])
        ps_t = [pb(f"ps_t{i}", [P, 512]) for i in range(2)]
        ps_h = [pb(f"ps_h{i}", [P, 512]) for i in range(2)]
        ps_e = [pb(f"ps_e{i}", [P, 512]) for i in range(2)]

        x_in = [sem(f"x_in{i}") for i in range(NGRP)]
        w_in = sem("w_in")
        edges_in = sem("edges_in")
        consts = sem("consts")
        acc_zero = sem("acc_zero")
        dve_chain = sem("dve_chain")
        edges_clear = sem("edges_clear")
        x_clear = sem("x_clear")
        w_tr = sem("w_tr")
        w_tr_copied = sem("w_tr_copied")
        wa_done = sem("wa_done")
        wext_ready = sem("wext_ready")
        xn_ready = sem("xn_ready")
        xn_tr = sem("xn_tr")
        xnT_ready = sem("xnT_ready")
        proj_done = sem("proj_done")
        rows_ready = sem("rows_ready")
        rows_out = [sem(f"rows_out{k}") for k in range(GRP)]
        edges_f_ready = sem("edges_f_ready")
        edge_tr = sem("edge_tr")
        edge_tr_copied = sem("edge_tr_copied")
        lohi_ready = sem("lohi_ready")
        lohi_all = sem("lohi_all")

        block = ctx.enter_context(nc.Block())
        EG = (2 * CB + 3) // 4

        @block.sync
        def _(sp):
            sp.wait_ge(edges_clear, 1)
            for i, e in enumerate((src, dst)):
                sp.dma_start(edges_i[:, i, 0:CB - 1, :],
                              e[0:(CB - 1) * P * P].rearrange("(b p e) -> p b e", p=P, e=P)).then_inc(edges_in, 16)
                lo = (CB - 1) * P * P
                sp.dma_start(edges_i[0:CFULL % P, i, CB - 1, :],
                              e[lo:CFULL * P].rearrange("(p e) -> p e", e=P)).then_inc(edges_in, 16)
                sp.dma_start(edges_i[CFULL % P:CFULL % P + 1, i, CB - 1, 0:CREST],
                              e[CFULL * P:E].rearrange("(p e) -> p e", p=1)).then_inc(edges_in, 16)
            sp.wait_ge(x_clear, 1)
            for g in range(NGRP):
                t0 = g * GRP
                nt = GRP if g < NGRP - 1 else GRP - 1
                sp.dma_start(x_all[:, t0:t0 + nt, :],
                             x[t0 * P:(t0 + nt) * P, :].rearrange("(t p) d -> p t d", p=P)).then_inc(x_in[g], 16)
            sp.dma_start(x_all[0:LAST, FULL, :], x[FULL * P:N, :]).then_inc(x_in[NGRP - 1], 16)
            for it in range(1):
                for k in range(GRP):
                    sp.wait_ge(rows_ready, k + 1)
                    sp.dma_start(table[k * P:(k + 1) * P, 0:D], rows[:, k, :]).then_inc(rows_out[k], 16)
            with sp.Fori(1, NGRP) as it:
                for k in range(GRP):
                    sp.wait_ge(rows_ready, it * GRP + (k + 1))
                    sp.dma_start(table[bass.ds(it * (GRP * P) + k * P, P), 0:D], rows[:, k, :]).then_inc(rows_out[k], 16)
            sp.wait_ge(acc_zero, 1)
            sp.dma_start(expert_out[MINFFN * P:FFN_TILES * P, :].rearrange("(t p) d -> p t d", p=P),
                         acc[:, 0:FFN_TILES - MINFFN, 0:D]).then_inc(zeroed, 16)
            for k in range(GRP):
                sp.wait_ge(rows_out[k], 16 * NGRP)

        @block.gpsimd
        def _(pool):
            pool.memset(ident[:, :], 0.0).then_inc(consts, 1)
            pool.memset(a_blk[:, :, :], 0.0).then_inc(consts, 1)
            pool.wait_ge(consts, 2)
            pool.affine_select(out=ident[:, :], in_=ident[:, :], compare_op=ALU.not_equal, fill=1.0, base=0,
                               pattern=[[-1, P]], channel_multiplier=1).then_inc(consts, 1)
            pool.iota(chunk_no[:, :], pattern=[[P, CB]], base=0, channel_multiplier=1,
                      allow_small_or_imprecise_dtypes=True).then_inc(consts, 1)
            pool.iota(tile_first[:, :], pattern=[[P, TILES]], base=0, channel_multiplier=0,
                      allow_small_or_imprecise_dtypes=True).then_inc(consts, 1)
            pool.iota(neg_first[:, :], pattern=[[-P, TILES]], base=0, channel_multiplier=0,
                      allow_small_or_imprecise_dtypes=True).then_inc(consts, 1)
            pool.iota(node_iota[:, :], pattern=[[1, P]], base=0, channel_multiplier=0,
                      allow_small_or_imprecise_dtypes=True).then_inc(consts, 1)
            pool.memset(acc[:, :, :], 0.0).then_inc(acc_zero, 1)
            pool.wait_ge(acc_zero, 1)
            pool.wait_ge(lohi_ready, 2)
            pool.partition_all_reduce(lohi_r[:, :, :], lohi[:, :, :], P, bass.bass_isa.ReduceOp.max).then_inc(lohi_all, 1)
            pool.wait_ge(lohi_all, 1)

        @block.scalar
        def _(act):
            act.dma_start(w_ext[:, :, 0:D], W.rearrange("(a p) n -> p a n", p=P)).then_inc(w_in, 16)
            act.dma_start(a_col[:, 0, :], a_src.rearrange("(a h) d -> (h d) a", a=2)).then_inc(w_in, 16)
            act.dma_start(a_col[:, 1, :], a_dst.rearrange("(a h) d -> (h d) a", a=2)).then_inc(w_in, 16)
            for a in range(2):
                act.wait_ge(w_tr, a + 1)
                act.activation(w_T[:, a, :], ps_t[a][:, 0:D], ACT.Copy).then_inc(w_tr_copied, 1)
            for a in range(2):
                act.wait_ge(wa_done, a + 1)
                act.activation(w_ext[:, a, D:PROJ], ps_h[a][:, 0:2 * HEADS], ACT.Copy).then_inc(wext_ready, 1)
            for q in range(EG):
                act.wait_ge(edge_tr, min(4 * q + 4, 2 * CB))
                for j in range(4 * q, min(4 * q + 4, 2 * CB)):
                    to = (srcT if j < CB else dstT)[:, (j % CB) * P:(j % CB + 1) * P]
                    last = act.activation(to, ps_e[q % 2][:, (j % 4) * P:(j % 4 + 1) * P], ACT.Copy)
                last.then_inc(edge_tr_copied, 1)
            act.wait_ge(norms.var_ready, 1)
            act.activation(rstd[:, :], nmr[:, :], ACT.Sqrt).then_inc(norms.std_ready, 1)
            act.wait_ge(norms.scale_ready, 1)
            act.preload_act_table(ACT.Exp)

            def norm(k, g, first):
                if not first:
                    act.wait_ge(xn_tr, g - (GRP - 1))
                act.activation(xn[:, k, :], one(x_all[:, bass.ds(g, 1), :]), ACT.Identity,
                               bias=nmr[:, bass.ds(g, 1)], scale=rstd[:, bass.ds(g, 1)]).then_inc(xn_ready, 1)

            def group(g0, first):
                norm(0, g0, first)
                for k in range(GRP):
                    if k < GRP - 1:
                        norm(k + 1, g0 + (k + 1), first)
                    act.wait_ge(xn_tr, g0 + (k + 1))
                    if not first:
                        act.wait_ge(proj_done, g0 + (k - (GRP - 1)))
                    act.activation(xnT[:, k, :], ps_t[k % 2][:, 0:D], ACT.Copy).then_inc(xnT_ready, 1)

            group(0, True)
            with act.Fori(1, NGRP) as it:
                group(it * GRP, False)

        @block.vector
        def _(dve):
            link = Chain(dve, dve_chain)
            dve.memset(x_all[:, FULL, :], 0.0).then_inc(x_clear, 1)
            dve.memset(edges_i[:, 0, CB - 1, :], 0)
            dve.memset(edges_i[:, 1, CB - 1, :], int(NODST)).then_inc(edges_clear, 1)
            dve.memset(srcT[:, PADC:COLS], 0)
            dve.memset(dstT[:, PADC:COLS], NODST)
            dve.wait_ge(w_in, 48)
            dve.wait_ge(consts, 2)
            for a in range(2):
                for q in range(4):
                    for s in range(2):
                        dve.tensor_copy(a_blk[q * HD:(q + 1) * HD, a, s * HEADS + 4 * a + q:s * HEADS + 4 * a + q + 1],
                                        a_col[q * HD:(q + 1) * HD, s, a:a + 1]).then_inc(edges_f_ready, 1)
            dve.wait_ge(edges_in, 96)
            for i in range(2):
                dve.tensor_copy(edges_f[:, i, :, :], edges_i[:, i, :, :]).then_inc(edges_f_ready, 1)
            dve.wait_ge(edges_f_ready, 18)
            dve.tensor_reduce(chunk_min[:, :], edges_f[:, 1, :, :], AX.X, ALU.min)
            link(dve.tensor_scalar(real_dst[:, :], edges_f[:, 1, CB - 1, :], NODST, -NODST - 1, ALU.is_ge, ALU.mult))
            link(dve.tensor_tensor(real_dst[:, :], real_dst[:, :], edges_f[:, 1, CB - 1, :], ALU.add))
            dve.tensor_reduce(chunk_max[:, 0:CB - 1], edges_f[:, 1, 0:CB - 1, :], AX.X, ALU.max)
            link(dve.tensor_reduce(chunk_max[:, CB - 1:CB], real_dst[:, :], AX.X, ALU.max))

            def per_tile(v):
                return v.unsqueeze(2).to_broadcast([P, TILES, CB])

            def per_chunk(v):
                return v.unsqueeze(1).to_broadcast([P, TILES, CB])

            def seg_steps():
                dve.wait_ge(consts, 7)
                dve.tensor_tensor(over_a[:, :, :], per_chunk(chunk_max[:, :]), per_tile(tile_first[:, :]), ALU.is_ge)
                link(dve.tensor_scalar(span[:, :], tile_first[:, :], float(P - 1), None, ALU.add))
                link(dve.tensor_tensor(over_b[:, :, :], per_chunk(chunk_min[:, :]), per_tile(span[:, :]), ALU.is_le))
                link(dve.tensor_tensor(over_a[:, :, :], over_a[:, :, :], over_b[:, :, :], ALU.mult))
                link(dve.tensor_scalar(chunk_max[:, :], chunk_no[:, :], 1.0, None, ALU.add))
                link(dve.tensor_tensor(over_b[:, :, :], over_a[:, :, :], per_chunk(chunk_max[:, :]), ALU.mult))
                link(dve.tensor_reduce(lohi[:, 1, :], over_b[:, :, :], AX.X, ALU.max))
                link(dve.tensor_scalar(chunk_max[:, :], chunk_no[:, :], -1.0, 4096.0, ALU.mult, ALU.add))
                link(dve.tensor_tensor(over_b[:, :, :], over_a[:, :, :], per_chunk(chunk_max[:, :]), ALU.mult))
                dve.tensor_reduce(lohi[:, 0, :], over_b[:, :, :], AX.X, ALU.max).then_inc(lohi_ready, 2)

            seg_steps()
            for g in range(NGRP):
                dve.wait_ge(x_in[g], 16 if g < NGRP - 1 else 32)
                group_stats(dve, link, lambda k: x_all[:, g * GRP + k, :], stats, mv, spare, mean_var, g)
            dve.tensor_scalar(nmr[:, :], mean_var[:, :, 1], EPS, None, ALU.add).then_inc(norms.var_ready, 1)
            dve.wait_ge(lohi_all, 1)
            link(dve.tensor_scalar(tile_lo[:, :], lohi_r[:, 0, :], -1.0, 4096.0, ALU.mult, ALU.add))
            link(dve.tensor_tensor(span[:, :], lohi_r[:, 1, :], tile_lo[:, :], ALU.subtract))
            link(dve.tensor_scalar(span[:, :], span[:, :], 0.0, None, ALU.max))
            link(dve.tensor_copy(span_i[:, :], span[:, :]))
            link(dve.tensor_scalar(odd_i[:, :], span_i[:, :], 1, None, ALU.bitwise_and))
            link(dve.tensor_copy(odd[:, :], odd_i[:, :]))
            link(dve.tensor_tensor(span[:, :], span[:, :], odd[:, :], ALU.add))
            link(dve.tensor_scalar(tile_n[:, :], span[:, :], 0.5, None, ALU.mult))
            dve.wait_ge(norms.std_ready, 1)
            link(dve.reciprocal(rstd[:, :], rstd[:, :]))
            dve.scalar_tensor_tensor(nmr[:, :], mean_var[:, :, 0], -1.0, rstd[:, :], ALU.mult, ALU.mult).then_inc(norms.scale_ready, 1)

            def tile(k, g, first):
                dve.wait_ge(proj_done, g + 1)
                if not first:
                    dve.wait_ge(rows_out[k], 16 * it)
                dve.tensor_copy(rows[:, k, :], ps_h[k % 2][:, 0:D])
                dve.tensor_copy(src_sc[:, bass.ds(g, 1), :].rearrange("p a d -> p (a d)"), ps_h[k % 2][:, D:SUM])
                dve.tensor_copy(dst_tab[:, bass.ds(g, 1), 0:HEADS].rearrange("p a d -> p (a d)"),
                                ps_h[k % 2][:, SUM:PROJ]).then_inc(rows_ready, 1)

            for k in range(GRP):
                tile(k, k, True)
            with dve.Fori(1, NGRP) as it:
                for k in range(GRP):
                    tile(k, it * GRP + k, False)

        @block.tensor
        def _(pe):
            pe.wait_ge(consts, 3)
            pe.wait_ge(w_in, 48)
            for j in range(2):
                for k in range(2):
                    last = pe.transpose(ps_t[j][:, k * P:(k + 1) * P], w_ext[:, k, j * P:(j + 1) * P], ident[:, :])
                last.then_inc(w_tr, 1)
            pe.wait_ge(w_tr_copied, 2)
            pe.wait_ge(edges_f_ready, 16)
            for k in range(2):
                for j in range(2):
                    last = pe.matmul(ps_h[k][:, 0:2 * HEADS], w_T[:, j, k * P:(k + 1) * P], a_blk[:, j, :],
                                     start=(j == 0), stop=(j == 1))
                last.then_inc(wa_done, 1)
            pe.wait_ge(edges_f_ready, 18)
            for q in range(EG):
                if q >= 2:
                    pe.wait_ge(edge_tr_copied, q - 1)
                for j in range(4 * q, min(4 * q + 4, 2 * CB)):
                    pe.transpose(ps_e[q % 2][:, (j % 4) * P:(j % 4 + 1) * P], edges_f[:, j // CB, j % CB, :],
                                 ident[:, :]).then_inc(edge_tr, 1)
            pe.wait_ge(wext_ready, 2)

            def turn(k, g, first):
                pe.wait_ge(xn_ready, g + 1)
                if not (first and k < 2):
                    pe.wait_ge(xnT_ready, g - 1 if k else g)
                for a in range(2):
                    last = pe.transpose(ps_t[k % 2][:, a * P:(a + 1) * P], xn[:, k, a * P:(a + 1) * P], ident[:, :])
                last.then_inc(xn_tr, 1)

            def project(k, g, first):
                pe.wait_ge(xnT_ready, g + 1)
                if not (first and k < 2):
                    pe.wait_ge(rows_ready, g - 1 if k else g)
                for a in range(2):
                    last = pe.matmul(ps_h[k % 2][:, 0:PROJ], xnT[:, k, a * P:(a + 1) * P], w_ext[:, a, :],
                                     start=(a == 0), stop=(a == 1))
                last.then_inc(proj_done, 1)

            def group(g0, first):
                turn(0, g0, first)
                for k in range(GRP):
                    if k < GRP - 1:
                        turn(k + 1, g0 + (k + 1), first)
                    project(k, g0 + k, first)

            group(0, True)
            with pe.Fori(1, NGRP) as it:
                group(it * GRP, False)


def stage2(nc, table, schedule, zeroed, src_sc, dst_tab, tile_lo, tile_n, counts, seg_max):
    with ExitStack() as ctx:
        def sb(name, shape, dt=F32):
            return ctx.enter_context(nc.sbuf_tensor(name, shape, dt))

        def sem(name):
            return ctx.enter_context(nc.semaphore(name))

        B = TILES + 1
        K = IBLK // P
        assert K == BODY
        first = sb("first", [P, B])
        ones = sb("ones", [P, TILES])
        key = sb("key", [P, B])
        delta = sb("delta", [P, B])
        step_no = sb("step_no", [P, K])
        step_cur = sb("step_cur", [P, K])
        ge = sb("ge", [P, K, B])
        res = sb("res", [P, K])
        res_i = sb("res_i", [P, LISTS, K], I32)
        blk_f = sb("blk_f", [P, 4])
        best = sb("best", [P, 2, HEADS])
        best_all = sb("best_all", [P, 2, HEADS])
        apart = sb("apart", [P, HEADS])
        wide = sb("wide", [P, 1])
        scores = sb("scores", [P, TILES, 2 * HEADS])
        dve_chain = sem("dve_chain2")
        iotas = sem("iotas")
        best_ready = sem("best_ready")
        best_reduced = sem("best_reduced")
        apart_ready = sem("apart_ready")
        scores_ready = sem("scores_ready2")
        scores_out = sem("scores_out")
        counts_ready = sem("counts_ready")
        list_ready = sem("list_ready")
        list_out = sem("list_out")
        list_kept = sem("list_kept")
        block = ctx.enter_context(nc.Block())

        @block.gpsimd
        def _(pool):
            pool.iota(step_no[:, :], pattern=[[1, K]], base=0, channel_multiplier=K,
                      allow_small_or_imprecise_dtypes=True).then_inc(iotas, 1)
            pool.wait_ge(best_ready, 1)
            pool.partition_all_reduce(best_all[:, :, :], best[:, :, :], P, bass.bass_isa.ReduceOp.max).then_inc(best_reduced, 1)

        @block.vector
        def _(dve):
            link = Chain(dve, dve_chain)
            dve.tensor_reduce(best[:, 0, :], src_sc[:, :, :].rearrange("p t h -> p h t"), AX.X, ALU.max)
            link(dve.tensor_reduce(best[:, 1, :], src_sc[:, :, :].rearrange("p t h -> p h t"), AX.X, ALU.min))
            dve.tensor_scalar(best[:, 1, :], best[:, 1, :], -1.0, None, ALU.mult).then_inc(best_ready, 1)
            dve.memset(ones[:, :], 1.0)
            link(dve.memset(first[:, 0:1], 0.0))
            link(dve.tensor_tensor_scan(first[:, 1:B], ones[:, :], tile_n[:, :], 0.0, ALU.mult, ALU.add))
            link(dve.scalar_tensor_tensor(key[:, 0:TILES], first[:, 0:TILES], -2.0, tile_lo[:, :], ALU.mult, ALU.add))
            link(dve.tensor_scalar(key[:, TILES:B], first[:, TILES:B], -2.0, float(PADC), ALU.mult, ALU.add))
            link(dve.tensor_copy(delta[:, 0:1], key[:, 0:1]))
            link(dve.tensor_tensor(delta[:, 1:B], key[:, 1:B], key[:, 0:TILES], ALU.subtract))
            link(dve.tensor_scalar(blk_f[:, 0:1], first[:, TILES:B], 1.0, None, ALU.mult))
            link(dve.tensor_scalar(blk_f[:, 1:2], blk_f[:, 0:1], float(JOIN + BODY - 1), None, ALU.add))
            link(dve.tensor_scalar(blk_f[:, 2:3], blk_f[:, 0:1], float(SLACK + IBLK), None, ALU.add))
            link(dve.tensor_copy(counts[:, 0:2], blk_f[:, 1:3]))
            shift = BODY.bit_length() - 1
            link(dve.tensor_scalar(counts[:, 0:1], counts[:, 0:1], shift, None, ALU.arith_shift_right))
            dve.tensor_scalar(counts[:, 1:2], counts[:, 1:2], 10, None, ALU.arith_shift_right).then_inc(counts_ready, 1)
            dve.wait_ge(counts_ready, 1)
            dve.wait_ge(iotas, 1)
            dve.wait_ge(best_reduced, 1)
            most = best_all[:, 0, :].unsqueeze(1).to_broadcast([P, TILES, HEADS])
            dve.tensor_tensor(dst_tab[:, :, 0:HEADS], dst_tab[:, :, 0:HEADS], most, ALU.add)
            link(dve.tensor_tensor(scores[:, :, 0:HEADS], src_sc[:, :, :], most, ALU.subtract))
            dve.tensor_scalar(scores[:, :, HEADS:2 * HEADS], scores[:, :, 0:HEADS], SLOPE, None, ALU.mult).then_inc(scores_ready, 1)
            dve.tensor_tensor(apart[:, :], best_all[:, 0, :], best_all[:, 1, :], ALU.add).then_inc(apart_ready, 1)
            dve.wait_ge(apart_ready, 1)
            link(dve.tensor_reduce(wide[:, :], apart[:, :], AX.X, ALU.max))
            link(dve.tensor_scalar(wide[:, :], wide[:, :], SAFE, None, ALU.is_gt))
            link(dve.tensor_scalar(apart[:, :], apart[:, :], wide[:, :], -1.0, ALU.mult, ALU.mult))
            link(dve.tensor_copy(seg_max[:, :, :], apart[:, :].unsqueeze(1).to_broadcast([P, TILES, HEADS])))
            blocks = dve.value_load(counts[0:1, 1:2], min_val=1, max_val=IBLKS)

            def tiles(v):
                return v.unsqueeze(1).to_broadcast([P, K, B])

            def steps(v):
                return v.unsqueeze(2).to_broadcast([P, K, B])

            per = 2 + sum(6 if chunk else 4 for _, chunk in LIST_OF)
            with dve.Fori(0, blocks) as b:
                link.loop(b, 0, per)
                for q, (shift, chunk) in enumerate(LIST_OF):
                    link(dve.tensor_scalar(step_cur[:, :], step_no[:, :], float(shift), None, ALU.add))
                    link(dve.tensor_tensor(ge[:, :, :], steps(step_cur[:, :]), tiles(first[:, :]), ALU.is_ge))
                    if chunk:
                        link(dve.tensor_tensor(ge[:, :, :], ge[:, :, :], tiles(delta[:, :]), ALU.mult))
                        link(dve.tensor_reduce(res[:, :], ge[:, :, :], AX.X, ALU.add))
                        link(dve.scalar_tensor_tensor(res[:, :], step_cur[:, :], 2.0, res[:, :], ALU.mult, ALU.add))
                        link(dve.tensor_scalar(res_i[:, q, :], res[:, :], float(PADC + 4), None, ALU.min))
                    else:
                        link(dve.tensor_reduce(res[:, :], ge[:, :, 1:B], AX.X, ALU.add))
                        link(dve.tensor_scalar(res_i[:, q, :], res[:, :], float(TILES - 1), None, ALU.min))
                link(dve.tensor_scalar(step_no[:, :], step_no[:, :], float(IBLK), None, ALU.add))
                dve.memset(blk_f[:, 3:4], 0.0).then_inc(list_ready, 1)
                dve.wait_ge(list_out, 16 * b + 16)
                link(dve.memset(blk_f[:, 2:3], 0.0))
            link.end(blocks)
            link(dve.tensor_tensor(blk_f[:, 0:1], first[:, TILES:B], wide[:, :], ALU.mult))
            link(dve.tensor_copy(counts[:, 2:3], blk_f[:, 0:1]))
            dve.memset(blk_f[:, 3:4], 0.0)

        @block.sync
        def _(sp):
            sp.wait_ge(scores_ready, 1)
            sp.dma_start(table.rearrange("(t p) c -> p t c", p=P)[:, :, D:ROW], scores[:, :, :]).then_inc(scores_out, 16)
            sp.wait_ge(counts_ready, 1)
            blocks = sp.value_load(counts[0:1, 1:2], min_val=1, max_val=IBLKS)
            with sp.Fori(0, blocks) as b:
                sp.wait_ge(list_ready, b + 1)
                sp.dma_start(schedule[bass.ds(b * P, P), :], res_i[:, :, :].rearrange("p q k -> p (q k)")).then_inc(list_out, 16)
            sp.wait_ge(list_out, 16 * blocks)
            sp.sem_inc(list_kept, 1)
            sp.wait_ge(scores_out, 16)
            sp.wait_ge(zeroed, 16)


def bounds(nc, table, schedule, ident, node_iota, neg_first, dst_tab, srcT, dstT, counts, seg_max):
    with ExitStack() as ctx:
        def sb(name, shape, dt=F32):
            return ctx.enter_context(nc.sbuf_tensor(name, shape, dt))

        def pb(name, shape, dt=F32):
            return ctx.enter_context(nc.psum_tensor(name, shape, dt))

        def sem(name):
            return ctx.enter_context(nc.semaphore(name))

        step_row = sb("step_row", [1, LISTS * BODY], I32)
        ones = sb("ones_b", [P, P])
        idx = sb("idx_b", [P, 2], I32)
        rel = sb("rel_b", [P, 2])
        gat = sb("gat_b", [P, 2, ROW])
        hot = sb("hot_b", [P, 2, P])
        away = sb("away", [P, 2, P])
        diag = sb("diag", [P, HEADS, P])
        masked = sb("masked", [P, HEADS, P])
        cur = sb("cur", [P, HEADS])
        spare = sb("spare_b", [P, 4])
        leak = sb("leak", [P, TILES, HEADS])
        ps_hot = pb("ps_hot_b", [P, 512])
        ps_all = [pb(f"ps_all{i}", [P, 512]) for i in range(2)]
        ones_ready = sem("ones_ready")
        row_in = sem("row_in")
        idx_ready = sem("idx_ready_b")
        rel_ready = sem("rel_ready_b")
        landed = sem("landed_b")
        hot_ready = sem("hot_ready_b")
        hot_tr = sem("hot_tr_b")
        diag_ready = sem("diag_ready")
        spread = sem("spread_b")
        step_done = sem("step_done")
        pool_turn = sem("pool_turn_b")
        sp_turn = sem("sp_turn_b")
        dve_chain = sem("dve_chain_b")
        bound_chain = sem("bound_chain")
        block = ctx.enter_context(nc.Block())

        def step_count(eng):
            return eng.value_load(counts[0:1, 2:3], min_val=0, max_val=MAXSTEPS)

        def from_list(eng, it, which, most):
            return eng.value_load(step_row[0:1, bass.ds((it & (BODY - 1)) + which * BODY, 1)], min_val=0, max_val=most)

        @block.sync
        def _(sp):
            steps = step_count(sp)
            with sp.If(steps > 0):
                sp.dma_start(step_row[:, :], schedule[0:1, :]).then_inc(row_in, 16)
                with sp.Fori(0, steps) as it:
                    sp.wait_ge(step_done, it + 1)
                    sp.sem_inc(sp_turn, 1)
                    sp.dma_start(step_row[:, :], schedule[bass.ds((it + 1) >> (BODY.bit_length() - 1), 1), :]).then_inc(row_in, 16)
                sp.wait_ge(row_in, steps * 16 + 16)
                sp.sem_inc(sp_turn, 1)

        @block.gpsimd
        def _(pool):
            steps = step_count(pool)
            with pool.If(steps > 0):
                with pool.Fori(0, steps) as it:
                    pool.wait_ge(idx_ready, it + 1)
                    pool.sem_inc(pool_turn, 1)
                    for j in range(2):
                        pool.indirect_dma_start(gat[:, j, :], None, table,
                                                bass.IndirectOffsetOnAxis(ap=idx[:, j:j + 1], axis=0)).then_inc(landed, 16)

        @block.scalar
        def _(act):
            act.preload_act_table(ACT.Exp)
            steps = step_count(act)
            with act.If(steps > 0):
                with act.Fori(0, steps) as it:
                    act.wait_ge(row_in, it * 16 + 16)
                    c = from_list(act, it, CHUNK, PADC + 4)
                    t = from_list(act, it, TILE, TILES - 1)
                    act.activation(idx[:, :], srcT[:, bass.ds(c, 2)], ACT.Copy).then_inc(idx_ready, 1)
                    act.activation(rel[:, :], dstT[:, bass.ds(c, 2)], ACT.Identity, bias=neg_first[:, bass.ds(t, 1)]).then_inc(rel_ready, 1)

        @block.tensor
        def _(pe):
            steps = step_count(pe)
            with pe.If(steps > 0):
                pe.wait_ge(ones_ready, 1)
                with pe.Fori(0, steps) as it:
                    pe.wait_ge(hot_ready, it + 1)
                    for j in range(2):
                        last = pe.transpose(ps_hot[:, j * P:(j + 1) * P], hot[:, j, :], ident[:, :])
                    last.then_inc(hot_tr, 1)
                    for j in range(2):
                        pe.wait_ge(diag_ready, it * 2 + (j + 1))
                        for q in range(2):
                            last = pe.matmul(ps_all[q][:, :], ones[:, :],
                                             diag[:, q * HEADS // 2:(q + 1) * HEADS // 2, :].rearrange("p h e -> p (h e)"),
                                             start=True, stop=True)
                        last.then_inc(spread, 1)

        @block.vector
        def _(dve):
            link = Chain(dve, dve_chain)
            dve.memset(ones[:, :], 1.0).then_inc(ones_ready, 1)
            steps = step_count(dve)
            with dve.If(steps > 0):

                def heads(v):
                    return v.unsqueeze(1).to_broadcast([P, HEADS // 2, P])

                with dve.Fori(0, steps) as it:
                    link.loop(it, 0, 10)
                    dve.wait_ge(rel_ready, it + 1)
                    dve.tensor_tensor(hot[:, :, :], node_iota[:, :].unsqueeze(1).to_broadcast([P, 2, P]),
                                      rel[:, :].unsqueeze(2).to_broadcast([P, 2, P]), ALU.is_equal).then_inc(hot_ready, 1)
                    dve.wait_ge(hot_tr, it + 1)
                    link(dve.tensor_scalar(away[:, :, :].rearrange("p a b -> p (a b)"), ps_hot[:, 0:2 * P], -1.0, FAR,
                                           ALU.add, ALU.mult))
                    dve.wait_ge(landed, it * 32 + 32)
                    tile = from_list(dve, it, TILE, TILES - 1)
                    here = one(seg_max[:, bass.ds(tile, 1), :])
                    for j in range(2):
                        link(dve.tensor_tensor(diag[:, :, :], ident[:, :].unsqueeze(1).to_broadcast([P, HEADS, P]),
                                               gat[:, j, D:D + HEADS].unsqueeze(2).to_broadcast([P, HEADS, P]), ALU.mult))
                        dve.memset(spare[:, 0:1], 0.0).then_inc(diag_ready, 1)
                        dve.wait_ge(spread, it * 2 + (j + 1))
                        for q in range(2):
                            last = dve.tensor_tensor(masked[:, q * HEADS // 2:(q + 1) * HEADS // 2, :],
                                                     ps_all[q][:, :].rearrange("p (h e) -> p h e", e=P),
                                                     heads(away[:, j, :]), ALU.add)
                        link(last)
                        link(dve.tensor_reduce(cur[:, :], masked[:, :, :], AX.X, ALU.max))
                        link(dve.tensor_tensor(here, here, cur[:, :], ALU.max))
                    link(dve.memset(spare[:, 1:2], 0.0))
                    dve.memset(spare[:, 2:3], 0.0).then_inc(step_done, 1)
            link = Chain(dve, bound_chain)
            link(dve.tensor_tensor(leak[:, :, :], dst_tab[:, :, 0:HEADS], seg_max[:, :, :], ALU.add))
            link(dve.scalar_tensor_tensor(leak[:, :, :], leak[:, :, :], SLOPE, leak[:, :, :], ALU.mult, ALU.max))
            link(dve.scalar_tensor_tensor(dst_tab[:, :, HEADS:2 * HEADS], dst_tab[:, :, 0:HEADS], SLOPE, leak[:, :, :],
                                          ALU.mult, ALU.subtract))
            link(dve.tensor_tensor(dst_tab[:, :, 0:HEADS], dst_tab[:, :, 0:HEADS], leak[:, :, :], ALU.subtract))
            dve.memset(spare[:, 3:4], 0.0)


def stage3(nc, table, schedule, acc, ident, node_iota, neg_first, dst_tab, srcT,
           dstT, counts):
    with ExitStack() as ctx:
        def sb(name, shape, dt=F32):
            return ctx.enter_context(nc.sbuf_tensor(name, shape, dt))

        def pb(name, shape, dt=F32):
            return ctx.enter_context(nc.psum_tensor(name, shape, dt))

        def sem(name):
            return ctx.enter_context(nc.semaphore(name))

        MSGS = 4
        MAXBODY = (MAXSTEPS + JOIN + BODY - 1) // BODY
        gat = sb("gat", [P, BODY, 2, ROW])
        idx = sb("idx", [P, BODY, 2], I32)
        rel = sb("rel", [P, BODY, 2])
        lists = sb("lists", [1, RING, LISTS, BODY], I32)
        hot = sb("hot", [P, BODY, 2, P])
        hotT = sb("hotT", [P, 2, 2, P])
        both = sb("both", [P, 2, 2, 2 * HEADS])
        score = sb("score", [P, 2, 2, HEADS])
        msg = sb("msg", [P, MSGS, 2, SUM])
        ps_hot = [pb(f"ps_hot{i}", [P, 512]) for i in range(2)]
        ps_look = [pb(f"ps_look{i}", [P, 512]) for i in range(2)]
        ps_sum = [pb(f"ps_sum{i}", [P, 512]) for i in range(2)]
        landed = [sem(f"landed{k}") for k in range(BODY)]
        lists_in = sem("lists_in")
        rows_landed = sem("rows_landed")
        idx_ready = sem("idx_ready")
        rel_ready = sem("rel_ready")
        pool_turn = sem("pool_turn")
        sp_turn = sem("sp_turn")
        hot_ready = sem("hot_ready")
        hot_tr = sem("hot_tr")
        hotT_ready = sem("hotT_ready")
        look_done = sem("look_done")
        both_ready = sem("both_ready")
        score_ready = sem("score_ready")
        weight_ready = sem("weight_ready")
        msg_ready = sem("msg_ready")
        sum_done = sem("sum_done")
        added = sem("added")
        block = ctx.enter_context(nc.Block())

        def registers(eng, name):
            return [eng.alloc_register(f"{name}{k}") for k in range(BODY)]

        def load_list(eng, regs, which, it):
            at = (it & (RING - 1)) * (LISTS * BODY) + which * BODY
            flat = lists[:, :, :, :].rearrange("o r l k -> o (r l k)")
            for k in range(0, BODY, 4):
                eng.load(regs[k:k + 4], flat[0:1, bass.ds(at + k, 4)])

        def chunk_of(eng, reg):
            return eng.snap(reg, min_val=0, max_val=PADC + 4)

        def tile_of(eng, reg):
            return eng.snap(reg, min_val=0, max_val=TILES - 1)

        def body_count(eng):
            return eng.value_load(counts[0:1, 0:1], min_val=2, max_val=MAXBODY)

        @block.gpsimd
        def _(pool):
            bodies = body_count(pool)

            def step(k, g, head):
                if not head:
                    pool.wait_ge(msg_ready, g - (BODY - 1))
                pool.wait_ge(idx_ready, g + 1)
                pool.sem_inc(pool_turn, 1)
                for j in range(2):
                    pool.indirect_dma_start(gat[:, k, j, :], None, table,
                                            bass.IndirectOffsetOnAxis(ap=idx[:, k, j:j + 1], axis=0)).then_inc(landed[k], 16)

            for k in range(BODY):
                step(k, k, True)
            with pool.Fori(1, bodies) as it:
                for k in range(BODY):
                    step(k, it * BODY + k, False)

        @block.sync
        def _(sp):
            bodies = body_count(sp)
            sp.dma_start(lists[0:1, 0:2, :, :].rearrange("o r l k -> o (r l k)"),
                         schedule[0:2, :].rearrange("(o r) n -> o (r n)", o=1)).then_inc(lists_in, 32)
            with sp.Fori(0, bodies) as it:
                sp.wait_ge(lists_in, it * 16 + 32)
                sp.sem_inc(sp_turn, 1)
                sp.dma_start(lists[:, :, :, :].rearrange("o r l k -> o r (l k)")[0:1, bass.ds((it + 2) & (RING - 1), 1), :],
                             schedule[bass.ds(it + 2, 1), :].unsqueeze(0)).then_inc(lists_in, 16)
                for k in range(BODY):
                    sp.wait_ge(landed[k], it * 32 + 32)
                    sp.sem_inc(rows_landed, 1)
            sp.wait_ge(lists_in, bodies * 16 + 32)
            sp.sem_inc(sp_turn, 1)

        @block.scalar
        def _(act):
            act.preload_act_table(ACT.Exp)
            chunks, tiles = registers(act, "next_chunk"), registers(act, "next_tile")
            bodies = body_count(act)
            act.wait_ge(lists_in, 32)

            def lay_out(slot, chunk, tile):
                c, t = chunk_of(act, chunk), tile_of(act, tile)
                act.activation(idx[:, slot, :], srcT[:, bass.ds(c, 2)], ACT.Copy).then_inc(idx_ready, 1)
                act.activation(rel[:, slot, :], dstT[:, bass.ds(c, 2)], ACT.Identity, bias=neg_first[:, bass.ds(t, 1)]).then_inc(rel_ready, 1)

            load_list(act, chunks, CHUNK, 0)
            load_list(act, tiles, TILE, 0)
            for k in range(AHEAD):
                lay_out(k, chunks[k], tiles[k])

            def step(k, g, head):
                if not (head and k < WEIGH):
                    act.wait_ge(score_ready, g - WEIGH + 1)
                    if not (head and k < WEIGH + MSGS):
                        act.wait_ge(sum_done, g - WEIGH - MSGS + 1)
                    m = (k - WEIGH) % MSGS
                    act.activation(msg[:, m, :, D:SUM], score[:, m % 2, :, :], ACT.Exp).then_inc(weight_ready, 1)
                act.wait_ge(hot_tr, g + 1)
                if not (head and k < 2):
                    act.wait_ge(look_done, g - 1)
                act.activation(hotT[:, k % 2, :, :].rearrange("p a b -> p (a b)"), ps_hot[k % 2][:, 0:2 * P],
                               ACT.Copy).then_inc(hotT_ready, 1)
                if not (head and k < BODY - AHEAD):
                    act.wait_ge(rows_landed, g - (BODY - AHEAD) + 1)
                lay_out((k + AHEAD) % BODY, chunks[k], tiles[k])

            def body(it, head):
                load_list(act, chunks, NEXT_CHUNK, it)
                load_list(act, tiles, NEXT_TILE, it)
                for k in range(BODY):
                    step(k, it * BODY + k, head)

            body(0, True)
            with act.Fori(1, bodies) as it:
                act.wait_ge(lists_in, it * 16 + 16)
                body(it, False)

        @block.tensor
        def _(pe):
            tiles = registers(pe, "tile")
            bodies = body_count(pe)
            pe.wait_ge(lists_in, 32)

            def look(k, g, head, tile):
                pe.wait_ge(hotT_ready, g + 1)
                if not (head and k < 2):
                    pe.wait_ge(both_ready, g - 1)
                for j in range(2):
                    last = pe.matmul(ps_look[k % 2][:, j * 2 * HEADS:(j + 1) * 2 * HEADS], hotT[:, k % 2, j, :],
                                     dst_tab[:, bass.ds(tile_of(pe, tile), 1), :].rearrange("p a b -> p (a b)"),
                                     start=True, stop=True)
                last.then_inc(look_done, 1)

            def step(k, g, head):
                pe.wait_ge(hot_ready, g + 1)
                if not (head and k < 2):
                    pe.wait_ge(hotT_ready, g - 1)
                for j in range(2):
                    last = pe.transpose(ps_hot[k % 2][:, j * P:(j + 1) * P], hot[:, k, j, :], ident[:, :])
                last.then_inc(hot_tr, 1)
                if not (head and k < 1):
                    look((k - 1) % BODY, g - 1, head, tiles[k])
                if not (head and k < SUMS):
                    pe.wait_ge(msg_ready, g - SUMS + 1)
                    if not (head and k < SUMS + 2):
                        pe.wait_ge(added, g - SUMS - 1)
                    for j in range(2):
                        last = pe.matmul(ps_sum[(k - SUMS) % 2][:, 0:SUM], hot[:, (k - SUMS) % BODY, j, :],
                                         msg[:, (k - SUMS) % MSGS, j, :], start=(j == 0), stop=(j == 1))
                    last.then_inc(sum_done, 1)

            def body(it, head):
                load_list(pe, tiles, LOOK_TILE, it)
                for k in range(BODY):
                    step(k, it * BODY + k, head)

            body(0, True)
            with pe.Fori(1, bodies) as it:
                pe.wait_ge(lists_in, it * 16 + 16)
                body(it, False)

        @block.vector
        def _(dve):
            olds = registers(dve, "old_tile")
            bodies = body_count(dve)
            dve.wait_ge(lists_in, 32)

            def step(k, g, head):
                m = (k - WEIGH) % MSGS
                if not (head and k < WEIGH):
                    dve.wait_ge(rows_landed, g - WEIGH + 1)
                    dve.wait_ge(look_done, g - WEIGH + 1)
                    dve.tensor_tensor(both[:, m % 2, :, :], gat[:, (k - WEIGH) % BODY, :, D:ROW],
                                      ps_look[m % 2][:, 0:4 * HEADS].rearrange("p (j s) -> p j s", j=2),
                                      ALU.add).then_inc(both_ready, 1)
                dve.wait_ge(rel_ready, g + 1)
                if not (head and k < BODY):
                    dve.wait_ge(sum_done, g - BODY + 1)
                dve.tensor_tensor(hot[:, k, :, :], node_iota[:, :].unsqueeze(1).to_broadcast([P, 2, P]),
                                  rel[:, k, :].unsqueeze(2).to_broadcast([P, 2, P]), ALU.is_equal).then_inc(hot_ready, 1)
                if head and k < WEIGH:
                    return
                dve.wait_ge(both_ready, g - WEIGH + 1)
                dve.tensor_tensor(score[:, m % 2, :, :], both[:, m % 2, :, 0:HEADS], both[:, m % 2, :, HEADS:2 * HEADS],
                                  ALU.max).then_inc(score_ready, 1)
                if not (head and k < JOIN):
                    o = tile_of(dve, olds[k])
                    dve.wait_ge(sum_done, g - JOIN + 1)
                    if not (head and k < JOIN + 1):
                        dve.wait_ge(added, g - JOIN)
                    to = acc[:, bass.ds(o, 1), :].rearrange("p a b -> p (a b)")
                    dve.tensor_tensor(to, to, ps_sum[(k - JOIN) % 2][:, 0:SUM], ALU.add).then_inc(added, 1)
                dve.wait_ge(weight_ready, g - WEIGH + 1)
                dve.tensor_tensor(msg[:, m, :, 0:D].rearrange("p j (h d) -> p j h d", d=HD),
                                  gat[:, (k - WEIGH) % BODY, :, 0:D].rearrange("p j (h d) -> p j h d", d=HD),
                                  msg[:, m, :, D:SUM].unsqueeze(3).to_broadcast([P, 2, HEADS, HD]),
                                  ALU.mult).then_inc(msg_ready, 1)

            def body(it, head):
                load_list(dve, olds, OLD_TILE, it)
                for k in range(BODY):
                    step(k, it * BODY + k, head)

            body(0, True)
            with dve.Fori(1, bodies) as it:
                dve.wait_ge(lists_in, it * 16 + 16)
                body(it, False)


def spread_tiles(v, n=GRP):
    return v.unsqueeze(1).to_broadcast([P, n, D])


def group_stats(dve, link, source, stats, mv, spare, mean_var, it):
    dve.memset(spare[:, 1:2], 0.0)
    for k in range(GRP):
        last = dve.bn_stats(stats[:, k, :], source(k))
    link(last)
    dve.memset(spare[:, 1:2], 0.0)
    for k in range(GRP):
        last = dve.bn_aggr(mv[:, k, :], stats[:, k, :])
    link(last)
    link(dve.tensor_copy(mean_var[:, bass.ds(it * GRP, GRP), :], mv[:, :, :]))


def one(v):
    return v.rearrange("p a d -> p (a d)")


def stage4(nc, gamma, beta, gate_w, gate_b, gw, gb, gate_in, w1, w1_sb, w1_in, x_all, acc, mean_var, rstd, nmr, norms):
    with ExitStack() as ctx:
        def sb(name, shape, dt=F32):
            return ctx.enter_context(nc.sbuf_tensor(name, shape, dt))

        def sem(name):
            return ctx.enter_context(nc.semaphore(name))

        gam = sb("gam", [P, D])
        bet = sb("bet", [P, D])
        stats = sb("stats4", [P, GRP, 6])
        mv = sb("mv4", [P, GRP, 2])
        mv_out = sb("mv_out", [P, GRP, 2])
        spare = sb("spare4", [P, 4])
        rden = sb("rden", [P, GRP, HEADS])
        var_g = sb("var_g4", [P, GRP])
        std_g = sb("std_g4", [P, GRP])
        rstd_g = sb("rstd_g4", [P, GRP])
        nmr_g = sb("nmr_g4", [P, GRP])
        xn = sb("xn4", [P, GRP, D])
        z = sb("z4", [P, 2, GRP, D])
        low = sb("low4", [P, 2, GRP, D])

        par_in = sem("par_in")
        dve_chain = sem("dve_chain4")
        pool_chain = sem("pool_chain4")
        beta_added = sem("beta_added")
        xn_ready = sem("xn_ready4")
        z_ready = sem("z_ready4")
        scaled = sem("scaled4")
        low_ready = sem("low_ready")
        exp_ready = sem("exp_ready")
        block = ctx.enter_context(nc.Block())

        def tile(k, it):
            return bass.ds(it * GRP + k, 1)

        def group(it):
            return bass.ds(it * GRP, GRP)

        @block.sync
        def _(sp):
            sp.dma_start(gam[:, :], gamma.unsqueeze(0).to_broadcast([P, D])).then_inc(par_in, 16)
            sp.dma_start(bet[:, :], beta.unsqueeze(0).to_broadcast([P, D])).then_inc(par_in, 16)
            sp.dma_start(gw[:, :, :], gate_w.rearrange("(a p) e -> p a e", p=P)).then_inc(gate_in, 16)
            sp.dma_start(gb[:, :], gate_b.unsqueeze(0)).then_inc(gate_in, 16)
            for q in range(4):
                e = slice(EXPERTS // 4 * q, EXPERTS // 4 * (q + 1))
                sp.dma_start(w1_sb[:, e, :, :].rearrange("p e a f -> p (e a) f"),
                             w1[e, :, :].rearrange("e (a p) f -> p (e a) f", p=P)).then_inc(w1_in, 16)

        def over_passes(eng, one_pass, link=None, links=0):
            for g in range(3):
                one_pass(g, g % 2, True, g >= 1, g >= 2)
            with eng.Fori(0, (NGRP - 3) // 2) as it:
                if link:
                    link.loop(it, 0, 2 * links)
                one_pass(it * 2 + 3, 1, True, True, True)
                one_pass(it * 2 + 4, 0, True, True, True)
            if link:
                link.end((NGRP - 3) // 2)
            for g in range(NGRP, NGRP + 2):
                one_pass(g, g % 2, False, g == NGRP, True)

        @block.scalar
        def _(act):
            act.preload_act_table(ACT.Exp)

            def one_pass(g, s, this, before, two_before):
                if this:
                    for k in range(GRP):
                        act.activation(xn[:, k, :], one(x_all[:, tile(k, g), :]), ACT.Identity,
                                       bias=nmr[:, tile(k, g)], scale=rstd[:, tile(k, g)]).then_inc(xn_ready, 1)
                if two_before:
                    act.wait_ge(low_ready, g - 1)
                    act.activation(low[:, s, :, :], low[:, s, :, :], ACT.Exp).then_inc(exp_ready, 1)
                if before:
                    act.wait_ge(norms.scale_ready, g + 1)
                    for k in range(GRP):
                        act.activation(z[:, 1 - s, k, :], acc[:, tile(k, g - 1), 0:D].rearrange("p a d -> p (a d)"),
                                       ACT.Identity, bias=nmr_g[:, k:k + 1], scale=rstd_g[:, k:k + 1]).then_inc(z_ready, 1)
                if this:
                    act.wait_ge(norms.var_ready, g + 2)
                    act.activation(std_g[:, :], var_g[:, :], ACT.Sqrt).then_inc(norms.std_ready, 1)
                    act.preload_act_table(ACT.Exp)

            over_passes(act, one_pass)
            act.wait_ge(norms.var_ready, NGRP + 2)
            act.activation(rstd[:, :], nmr[:, :], ACT.Sqrt).then_inc(norms.std_ready, 1)

        @block.gpsimd
        def _(pool):
            link = Chain(pool, pool_chain)
            pool.wait_ge(par_in, 32)

            def one_pass(g, s, this, before, two_before):
                if before:
                    pool.wait_ge(scaled, g)
                    here = z[:, 1 - s, :, :]
                    link(pool.tensor_tensor(here, here, spread_tiles(bet[:, :]), ALU.add))
                    pool.sem_inc(beta_added, 1)
                    pool.tensor_scalar(low[:, 1 - s, :, :], here, 0.0, None, ALU.min).then_inc(low_ready, 1)

            over_passes(pool, one_pass, link, 1)

        @block.vector
        def _(dve):
            link = Chain(dve, dve_chain)
            dve.wait_ge(par_in, 32)

            def one_pass(g, s, this, before, two_before):
                if before:
                    dve.wait_ge(norms.std_ready, g + 1)
                    link(dve.reciprocal(rstd_g[:, :], std_g[:, :]))
                    dve.scalar_tensor_tensor(nmr_g[:, :], mv[:, :, 0], -1.0, rstd_g[:, :], ALU.mult,
                                             ALU.mult).then_inc(norms.scale_ready, 1)
                if this:
                    link(dve.tensor_scalar(rden[:, :, :], acc[:, group(g), D:SUM], 1e-30, None, ALU.max))
                    link(dve.reciprocal(rden[:, :, :], rden[:, :, :]))
                    num = acc[:, group(g), 0:D].rearrange("p k (h d) -> p k h d", d=HD)
                    link(dve.tensor_tensor(num, num, rden[:, :, :].unsqueeze(3).to_broadcast([P, GRP, HEADS, HD]), ALU.mult))
                    dve.wait_ge(xn_ready, g * GRP + GRP)
                    rows = acc[:, group(g), 0:D]
                    link(dve.tensor_tensor(rows, rows, xn[:, :, :], ALU.add))
                    dve.memset(spare[:, 0:1], 0.0)
                    for k in range(GRP):
                        last = dve.bn_stats(stats[:, k, :], one(acc[:, tile(k, g), 0:D]))
                    link(last)
                    dve.memset(spare[:, 1:2], 0.0)
                    for k in range(GRP):
                        last = dve.bn_aggr(mv[:, k, :], stats[:, k, :])
                    link(last)
                    dve.tensor_scalar(var_g[:, :], mv[:, :, 1], EPS, None, ALU.add).then_inc(norms.var_ready, 1)
                if two_before:
                    dve.wait_ge(exp_ready, g - 1)
                    link(dve.scalar_tensor_tensor(low[:, s, :, :], z[:, s, :, :], 0.0, low[:, s, :, :], ALU.max, ALU.add))
                if before:
                    dve.wait_ge(z_ready, g * GRP)
                    here = z[:, 1 - s, :, :]
                    dve.tensor_tensor(here, here, spread_tiles(gam[:, :]), ALU.mult).then_inc(scaled, 1)
                if two_before:
                    rows = x_all[:, group(g - 2), :]
                    link(dve.scalar_tensor_tensor(rows, low[:, s, :, :], -1.0, rows, ALU.add, ALU.add))
                    group_stats(dve, link, lambda k: one(x_all[:, tile(k, g - 2), :]), stats, mv_out, spare[:, 2:4],
                                mean_var, g - 2)

            over_passes(dve, one_pass, link, 12)
            scales(dve, link, mean_var, rstd, nmr, norms, NGRP + 2)


def route(nc, gw, gb, gate_in, w2, w2_sb, w2_in, dispatched, x_all, ident, rstd, nmr, slots, gates, taken):
    with ExitStack() as ctx:
        def sb(name, shape, dt=F32):
            return ctx.enter_context(nc.sbuf_tensor(name, shape, dt))

        def pb(name, shape, dt=F32):
            return ctx.enter_context(nc.psum_tensor(name, shape, dt))

        def sem(name):
            return ctx.enter_context(nc.semaphore(name))

        ones_row = sb("ones_row", [1, P])
        ones_sq = sb("ones_sq", [P, P], BF16)
        before = sb("before", [P, P], BF16)
        expert_no = sb("expert_no", [P, EXPERTS])
        expert_row = sb("expert_row", [P, EXPERTS])
        valid = sb("valid", [P, TILES])
        pads = sb("pads", [P, TILES, 2])
        spare = sb("spare_r", [P, 1])
        y = sb("y", [P, 2, GRP, D])
        yT = sb("yT", [P, GRP, D])
        top = sb("top", [P, GRP, 8])
        top_i = sb("top_i", [P, GRP, 8], U32)
        top_f = sb("top_f", [P, GRP, 2])
        logits = sb("logits", [P, GRP, EXPERTS])
        diff = sb("diff", [P, GRP])
        ediff = sb("ediff", [P, GRP])
        rsum = sb("rsum", [P, GRP])
        pick = sb("pick", [P, 2, GRP, EXPERTS])
        both = sb("both4", [P, GRP, EXPERTS])
        both_h = sb("both_h", [P, GRP, EXPERTS], BF16)
        base = sb("base", [P, GRP + 1, EXPERTS])
        place = sb("place", [P, GRP, EXPERTS])
        hit = sb("hit", [P, 2, GRP, EXPERTS])
        slot_f = sb("slot_f", [P, 2, GRP])
        slot_g = sb("slot_g", [P, 2, 2, GRP], I32)
        ps_t = [pb(f"ps4_t{i}", [P, 512]) for i in range(2)]
        ps_l = pb("ps4_l", [P, 512])
        ps_before = pb("ps4_before", [P, 512])
        ps_total = pb("ps4_total", [P, 512])

        consts = sem("consts4")
        dve_chain = sem("dve_chain_r")
        y_ready = sem("y_ready")
        y_tr = sem("y_tr")
        yT_ready = sem("yT_ready")
        logits_done = sem("logits_done")
        logits_read = sem("logits_read")
        diff_ready = sem("diff_ready")
        ediff_ready = sem("ediff_ready")
        both_ready = sem("both_ready4")
        ranks_done = sem("ranks_done")
        slots_ready = sem("slots_ready")
        pool_turn = sem("pool_turn4")
        sent = [sem(f"sent{i}") for i in range(2)]
        SENT = 16 * 2 * GRP
        block = ctx.enter_context(nc.Block())

        def tile(k, g):
            return bass.ds(g * GRP + k, 1)

        def group(g):
            return bass.ds(g * GRP, GRP)

        def over_groups(eng, body):
            body(0, 0, None)
            body(1, 1, None)
            with eng.Fori(1, NGRP // 2) as it:
                body(it * 2, 0, it)
                body(it * 2 + 1, 1, it)
            body(NGRP - 1, 0, NGRP // 2)

        @block.sync
        def _(sp):
            for q in range(4):
                e = slice(EXPERTS // 4 * q, EXPERTS // 4 * (q + 1))
                sp.dma_start(w2_sb[:, e, :, :].rearrange("p e a f -> p (e a) f"),
                             w2[e, :, :].rearrange("e (a p) f -> p (e a) f", p=P)).then_inc(w2_in, 16)

        @block.gpsimd
        def _(pool):
            pool.memset(ones_row[:, :], 1.0).then_inc(consts, 1)
            pool.memset(ones_sq[:, :], 1.0).then_inc(consts, 1)
            pool.memset(before[:, :], 1.0).then_inc(consts, 1)
            pool.memset(valid[:, :], 1.0).then_inc(consts, 1)
            pool.memset(pads[:, :, :], 0.0).then_inc(consts, 1)
            pool.memset(base[:, 0, :], 0.0).then_inc(consts, 1)
            pool.iota(expert_no[:, :], pattern=[[1, EXPERTS]], base=0, channel_multiplier=0,
                      allow_small_or_imprecise_dtypes=True).then_inc(consts, 1)
            pool.iota(expert_row[:, :], pattern=[[CAP, EXPERTS]], base=0, channel_multiplier=0,
                      allow_small_or_imprecise_dtypes=True).then_inc(consts, 1)
            pool.wait_ge(consts, 8)
            pool.affine_select(out=before[:, :], in_=before[:, :], compare_op=ALU.is_gt, fill=0.0, base=0,
                               pattern=[[1, P]], channel_multiplier=-1).then_inc(consts, 1)
            pool.affine_select(out=valid[:, FULL:TILES], in_=valid[:, FULL:TILES], compare_op=ALU.is_gt, fill=0.0,
                               base=LAST, pattern=[[0, 1]], channel_multiplier=-1).then_inc(consts, 1)
            pool.iota(pads[:, FULL, :], pattern=[[P, 2]], base=PADROWS, channel_multiplier=1,
                      allow_small_or_imprecise_dtypes=True).then_inc(consts, 1)
            pool.wait_ge(consts, 11)
            pool.affine_select(out=pads[:, FULL, :], in_=pads[:, FULL, :], compare_op=ALU.is_ge, fill=0.0,
                               base=-LAST, pattern=[[0, 2]], channel_multiplier=1).then_inc(consts, 1)
            pool.wait_ge(consts, 12)

            def send(g, s, n):
                pool.wait_ge(slots_ready, g + 1)
                pool.sem_inc(pool_turn, 1)
                for k in range(GRP):
                    for c in range(2):
                        pool.indirect_dma_start(dispatched, bass.IndirectOffsetOnAxis(ap=slot_g[:, s, c, k:k + 1], axis=0),
                                                y[:, s, k, :], None).then_inc(sent[s], 16)

            over_groups(pool, send)
            pool.wait_ge(sent[0], SENT * ((NGRP + 1) // 2))
            pool.wait_ge(sent[1], SENT * (NGRP // 2))

        @block.scalar
        def _(act):
            act.preload_act_table(ACT.Exp)

            def norm(g, s, k):
                act.activation(y[:, s, k, :], one(x_all[:, tile(k, g), :]), ACT.Identity,
                               bias=nmr[:, tile(k, g)], scale=rstd[:, tile(k, g)]).then_inc(y_ready, 1)

            def router(g, s, n):
                if n is not None:
                    act.wait_ge(sent[s], n * SENT)
                norm(g, s, 0)
                for k in range(GRP):
                    if k < GRP - 1:
                        norm(g, s, k + 1)
                    act.wait_ge(y_tr, g * GRP + k + 1)
                    if not (n is None and s == 0):
                        act.wait_ge(logits_done, g)
                    act.activation(yT[:, k, :], ps_t[k % 2][:, 0:D], ACT.Copy).then_inc(yT_ready, 1)
                act.wait_ge(diff_ready, g + 1)
                act.activation(ediff[:, :], diff[:, :], ACT.Exp).then_inc(ediff_ready, 1)

            over_groups(act, router)

        @block.tensor
        def _(pe):
            pe.wait_ge(gate_in, 32)
            pe.wait_ge(consts, 12)

            def router(g, s, n):
                first = n is None and s == 0
                if not first:
                    pe.wait_ge(logits_read, g)

                def turn(k):
                    pe.wait_ge(y_ready, g * GRP + k + 1)
                    if not (first and k < 2):
                        pe.wait_ge(yT_ready, g * GRP + k - (1 if k else 0))
                    for a in range(KD):
                        last = pe.transpose(ps_t[k % 2][:, a * P:(a + 1) * P], y[:, s, k, a * P:(a + 1) * P], ident[:, :])
                    last.then_inc(y_tr, 1)

                turn(0)
                for k in range(GRP):
                    if k < GRP - 1:
                        turn(k + 1)
                    pe.wait_ge(yT_ready, g * GRP + k + 1)
                    to = ps_l[:, k * EXPERTS:(k + 1) * EXPERTS]
                    for a in range(KD):
                        pe.matmul(to, yT[:, k, a * P:(a + 1) * P], gw[:, a, :], start=(a == 0), stop=False)
                    last = pe.matmul(to, ones_row[:, :], gb[:, :], start=False, stop=True)
                last.then_inc(logits_done, 1)
                pe.wait_ge(both_ready, g + 1)
                flat = both_h[:, :, :].rearrange("p k e -> p (k e)")
                pe.matmul(ps_before[:, 0:GRP * EXPERTS], before[:, :], flat, start=True, stop=True)
                pe.matmul(ps_total[:, 0:GRP * EXPERTS], ones_sq[:, :], flat, start=True, stop=True).then_inc(ranks_done, 1)

            over_groups(pe, router)

        @block.vector
        def _(dve):
            link = Chain(dve, dve_chain)
            dve.wait_ge(consts, 12)

            def experts(v):
                return v.unsqueeze(1).to_broadcast([P, GRP, EXPERTS])

            def per_tile(v):
                return v.unsqueeze(2).to_broadcast([P, GRP, EXPERTS])

            def router(it, s, n):
                dve.wait_ge(logits_done, it + 1)
                link(dve.tensor_copy(logits[:, :, :].rearrange("p k e -> p (k e)"), ps_l[:, 0:GRP * EXPERTS]))
                dve.memset(spare[:, :], 0.0).then_inc(logits_read, 1)
                for k in range(GRP):
                    last = dve.max(top[:, k, :], logits[:, k, :])
                link(last)
                dve.memset(spare[:, :], 0.0)
                for k in range(GRP):
                    last = dve.max_index(top_i[:, k, :], top[:, k, :], logits[:, k, :])
                link(last)
                dve.tensor_tensor(diff[:, :], top[:, :, 1], top[:, :, 0], ALU.subtract).then_inc(diff_ready, 1)
                link(dve.tensor_copy(top_f[:, :, :], top_i[:, :, 0:2]))
                for c in range(2):
                    last = dve.tensor_tensor(pick[:, c, :, :], experts(expert_no[:, :]), per_tile(top_f[:, :, c]), ALU.is_equal)
                link(last)
                link(dve.tensor_tensor(both[:, :, :], pick[:, 0, :, :], pick[:, 1, :, :], ALU.add))
                dve.tensor_tensor(both_h[:, :, :], both[:, :, :], per_tile(valid[:, group(it)]), ALU.mult).then_inc(both_ready, 1)
                dve.wait_ge(ediff_ready, it + 1)
                link(dve.tensor_scalar(rsum[:, :], ediff[:, :], 1.0, None, ALU.add))
                link(dve.reciprocal(rsum[:, :], rsum[:, :]))
                dve.tensor_copy(gates[:, group(it), 0], rsum[:, :])
                dve.tensor_tensor(gates[:, group(it), 1], rsum[:, :], ediff[:, :], ALU.mult)
                dve.wait_ge(ranks_done, it + 1)
                for k in range(GRP):
                    link(dve.tensor_tensor(base[:, k + 1, :], base[:, k, :], ps_total[:, k * EXPERTS:(k + 1) * EXPERTS], ALU.add))
                link(dve.tensor_tensor(place[:, :, :], base[:, 0:GRP, :],
                                       ps_before[:, 0:GRP * EXPERTS].rearrange("p (k e) -> p k e", k=GRP), ALU.add))
                link(dve.tensor_tensor(place[:, :, :], place[:, :, :], experts(expert_row[:, :]), ALU.add))
                for c in range(2):
                    last = dve.tensor_tensor(hit[:, c, :, :], place[:, :, :], pick[:, c, :, :], ALU.mult)
                link(last)
                link(dve.tensor_reduce(slot_f[:, :, :], hit[:, :, :, :], AX.X, ALU.add))
                v2 = valid[:, group(it)].unsqueeze(1).to_broadcast([P, 2, GRP])
                link(dve.tensor_tensor(slot_f[:, :, :], slot_f[:, :, :], v2, ALU.mult))
                link(dve.tensor_tensor(slot_f[:, :, :], slot_f[:, :, :], pads[:, group(it), :].rearrange("p k c -> p c k"), ALU.add))
                if n is not None:
                    dve.wait_ge(sent[s], n * SENT)
                dve.tensor_copy(slots[:, group(it), :].rearrange("p k c -> p c k"), slot_f[:, :, :])
                dve.tensor_copy(slot_g[:, s, :, :], slot_f[:, :, :]).then_inc(slots_ready, 1)
                link(dve.tensor_copy(base[:, 0, :], base[:, GRP, :]))

            ROUTER_LINKS = 22
            router(0, 0, None)
            router(1, 1, None)
            with dve.Fori(1, NGRP // 2) as it:
                link.loop(it, 1, 2 * ROUTER_LINKS)
                router(it * 2, 0, it)
                router(it * 2 + 1, 1, it)
            link.end(NGRP // 2 - 1)
            router(NGRP - 1, 0, NGRP // 2)
            link(dve.tensor_copy(taken[:, :], base[:, 0, :]))


def scales(dve, link, mean_var, rstd, nmr, norms, n):
    dve.tensor_scalar(nmr[:, :], mean_var[:, :, 1], EPS, None, ALU.add).then_inc(norms.var_ready, 1)
    dve.wait_ge(norms.std_ready, n)
    link(dve.reciprocal(rstd[:, :], rstd[:, :]))
    dve.scalar_tensor_tensor(nmr[:, :], mean_var[:, :, 0], -1.0, rstd[:, :], ALU.mult, ALU.mult).then_inc(norms.scale_ready, 1)


def stage5(nc, dispatched, taken, slots, rows_l, expert_l, passes_i):
    with ExitStack() as ctx:
        def sb(name, shape, dt=F32):
            return ctx.enter_context(nc.sbuf_tensor(name, shape, dt))

        def sem(name):
            return ctx.enter_context(nc.semaphore(name))

        X1 = EXPERTS + 1
        L = FFN_LIST
        zeros = sb("zeros", [P, D])
        need_i = sb("need_i", [P, EXPERTS], I32)
        need = sb("need", [P, EXPERTS])
        ones = sb("ones5", [P, EXPERTS])
        begin = sb("begin", [P, X1])
        key = sb("key5", [P, X1])
        delta = sb("delta5", [P, X1])
        region = sb("region", [P, X1])
        tile_no = sb("tile_no", [P, L])
        ge = sb("ge5", [P, L, X1])
        slot_f = sb("slot_f5", [P, TILES * 2])
        shift_by = sb("shift_by", [P, TILES * 2])
        over = sb("over5", [P, TILES * 2, X1])
        res = sb("res5", [P, L])
        row_end = sb("row_end", [P, EXPERTS])
        row_end_i = sb("row_end_i", [P, EXPERTS], I32)
        passes_f = sb("passes_f", [P, 1])
        consts = sem("consts5")
        dve_chain = sem("dve_chain5")
        ends_ready = sem("ends_ready")
        zeros_out = sem("zeros_out")
        block = ctx.enter_context(nc.Block())

        @block.gpsimd
        def _(pool):
            pool.memset(zeros[:, :], 0.0).then_inc(consts, 1)
            pool.iota(tile_no[:, :], pattern=[[1, L]], base=0, channel_multiplier=0,
                      allow_small_or_imprecise_dtypes=True).then_inc(consts, 1)
            pool.iota(region[:, :], pattern=[[CAP, X1]], base=0, channel_multiplier=0,
                      allow_small_or_imprecise_dtypes=True).then_inc(consts, 1)

        @block.sync
        def _(sp):
            sp.wait_ge(consts, 3)
            for j in range(FFN_SPARE):
                sp.dma_start(dispatched[PADFFN + j * P:PADFFN + (j + 1) * P, :], zeros[:, :]).then_inc(zeros_out, 16)
            sp.wait_ge(ends_ready, 1)
            for e in range(EXPERTS):
                end = sp.value_load(row_end_i[0:1, e:e + 1], min_val=0, max_val=DROWS - P)
                sp.dma_start(dispatched[bass.ds(end, P), :], zeros[:, :]).then_inc(zeros_out, 16)
            sp.wait_ge(zeros_out, 16 * (EXPERTS + FFN_SPARE))

        @block.vector
        def _(dve):
            link = Chain(dve, dve_chain)
            dve.wait_ge(consts, 3)
            link(dve.tensor_tensor(row_end[:, :], taken[:, :], region[:, 0:EXPERTS], ALU.add))
            dve.tensor_copy(row_end_i[:, :], row_end[:, :]).then_inc(ends_ready, 1)
            link(dve.tensor_scalar(need[:, :], taken[:, :], float(P - 1), None, ALU.add))
            link(dve.tensor_copy(need_i[:, :], need[:, :]))
            link(dve.tensor_scalar(need_i[:, :], need_i[:, :], P.bit_length() - 1, None, ALU.arith_shift_right))
            link(dve.tensor_copy(need[:, :], need_i[:, :]))
            dve.memset(ones[:, :], 1.0)
            link(dve.memset(begin[:, 0:1], 0.0))
            link(dve.tensor_tensor_scan(begin[:, 1:X1], ones[:, :], need[:, :], 0.0, ALU.mult, ALU.add))
            link(dve.scalar_tensor_tensor(key[:, :], begin[:, :], -float(P), region[:, :], ALU.mult, ALU.add))
            link(dve.tensor_scalar(key[:, EXPERTS:X1], key[:, EXPERTS:X1], float(PADFFN - PADROWS), None, ALU.add))
            link(dve.tensor_copy(delta[:, 0:1], key[:, 0:1]))
            link(dve.tensor_tensor(delta[:, 1:X1], key[:, 1:X1], key[:, 0:EXPERTS], ALU.subtract))
            link(dve.tensor_tensor(ge[:, :, :], tile_no[:, :].unsqueeze(2).to_broadcast([P, L, X1]),
                                   begin[:, :].unsqueeze(1).to_broadcast([P, L, X1]), ALU.is_ge))
            link(dve.tensor_reduce(res[:, :], ge[:, :, 1:X1], AX.X, ALU.add))
            dve.memset(expert_l[:, 0:4], 0)
            link(dve.tensor_scalar(expert_l[:, 4:L + 4], res[:, :], float(EXPERTS - 1), None, ALU.min))
            link(dve.tensor_tensor(ge[:, :, :], ge[:, :, :], delta[:, :].unsqueeze(1).to_broadcast([P, L, X1]), ALU.mult))
            link(dve.tensor_reduce(res[:, :], ge[:, :, :], AX.X, ALU.add))
            link(dve.scalar_tensor_tensor(res[:, :], tile_no[:, :], float(P), res[:, :], ALU.mult, ALU.add))
            link(dve.tensor_scalar(rows_l[:, :], res[:, :], float(DROWS - P), None, ALU.min))
            flat = slots[:, :, :].rearrange("p t c -> p (t c)")
            link(dve.tensor_copy(slot_f[:, :], flat))
            link(dve.tensor_tensor(over[:, :, :], slot_f[:, :].unsqueeze(2).to_broadcast([P, TILES * 2, X1]),
                                   region[:, :].unsqueeze(1).to_broadcast([P, TILES * 2, X1]), ALU.is_ge))
            link(dve.tensor_tensor(over[:, :, :], over[:, :, :], delta[:, :].unsqueeze(1).to_broadcast([P, TILES * 2, X1]), ALU.mult))
            link(dve.tensor_reduce(shift_by[:, :], over[:, :, :], AX.X, ALU.add))
            link(dve.tensor_tensor(flat, slot_f[:, :], shift_by[:, :], ALU.subtract))
            link(dve.tensor_scalar(passes_f[:, :], begin[:, EXPERTS:X1], float(FFN_LAG + FFN_BODY - 1), None, ALU.add))
            link(dve.tensor_copy(passes_i[:, :], passes_f[:, :]))
            link(dve.tensor_scalar(passes_i[:, :], passes_i[:, :], FFN_BODY.bit_length() - 1, None, ALU.arith_shift_right))


def stage6(nc, b1, b2, w1_sb, w2_sb, w1_in, w2_in, dispatched, expert_out, ident, rows_l, expert_l, passes_i):
    with ExitStack() as ctx:
        def sb(name, shape, dt=F32):
            return ctx.enter_context(nc.sbuf_tensor(name, shape, dt))

        def pb(name, shape, dt=F32):
            return ctx.enter_context(nc.psum_tensor(name, shape, dt))

        def sem(name):
            return ctx.enter_context(nc.semaphore(name))

        B = FFN_BODY
        b1T = sb("b1T", [P, EXPERTS, KF])
        b2_t = sb("b2_t", [P, B, D])
        xt = sb("xt", [P, B, D])
        xT = sb("xT", [P, 2, D])
        hid = sb("hid", [P, 2, FF])
        hidT = sb("hidT", [P, 2, FF])
        o_sb = sb("o_sb", [P, 2, D])
        ps_x = [pb(f"ps_x{i}", [P, 512]) for i in range(2)]
        ps_h = [pb(f"ps5_h{i}", [P, 512]) for i in range(2)]
        ps_ht = [pb(f"ps_ht{i}", [P, 512]) for i in range(2)]
        ps_o = [pb(f"ps_o{i}", [P, 512]) for i in range(2)]

        b1_in = sem("b1_in")
        b2_in = [sem(f"b2_in{i}") for i in range(B)]
        x_in = [sem(f"x5_in{i}") for i in range(B)]
        x_tr = sem("x_tr")
        xT_ready = sem("xT_ready")
        h_done = sem("h_done")
        h_copied = sem("h_copied")
        h_tr = sem("h_tr")
        hT_ready = sem("hT_ready")
        o_done = sem("o_done")
        o_ready = sem("o_ready")
        o_out = [sem(f"o_out{i}") for i in range(2)]
        sp_turn = sem("sp_turn5")
        block = ctx.enter_context(nc.Block())
        MAXPASS = (MAXFFN + FFN_LAG + B - 1) // B

        def pass_count(eng):
            return eng.value_load(passes_i[0:1, 0:1], min_val=3, max_val=MAXPASS)

        def expert(eng, i, back):
            return eng.value_load(expert_l[0:1, bass.ds(i + (4 - back), 1)], min_val=0, max_val=EXPERTS - 1)

        def row(eng, i):
            return eng.value_load(rows_l[0:1, bass.ds(i, 1)], min_val=0, max_val=DROWS - P)

        @block.sync
        def _(sp):
            passes = pass_count(sp)

            def load(s, i, head):
                r = row(sp, i)
                if not head:
                    sp.wait_ge(x_tr, i - B + 1)
                    sp.sem_inc(sp_turn, 1)
                sp.dma_start(xt[:, s, :], dispatched[bass.ds(r, P), :]).then_inc(x_in[s], 16)

            def store(s, i):
                sp.wait_ge(o_ready, i + 1)
                sp.sem_inc(sp_turn, 1)
                sp.dma_start(expert_out[bass.ds(i * P, P), :], o_sb[:, s, :]).then_inc(o_out[s], 16)

            def load_b2(s, i):
                e = expert(sp, i, 0)
                sp.dma_start(b2_t[:, s, :], b2[bass.ds(e, 1), :].to_broadcast([P, D])).then_inc(b2_in[s], 16)

            for i in range(FFN_AHEAD):
                load(i, i, True)
            for i in range(B):
                load_b2(i, i)
            for i in range(B):
                load((i + FFN_AHEAD) % B, i + FFN_AHEAD, i + FFN_AHEAD < B)
                if i >= FFN_LAG:
                    store((i - FFN_LAG) % 2, i - FFN_LAG)
                    load_b2((i + 1) % B, i + 1)
            with sp.Fori(1, passes) as it:
                for k in range(B):
                    load((k + FFN_AHEAD) % B, it * B + k + FFN_AHEAD, False)
                    store((k - FFN_LAG) % 2, it * B + (k - FFN_LAG))
                    load_b2((k + 1) % B, it * B + (k + 1))
            sp.sem_inc(o_out[0], 16)
            sp.sem_inc(o_out[1], 32)
            for q in range(2):
                sp.wait_ge(o_out[q], passes * (16 * B // 2))
            for k in range(B):
                sp.wait_ge(b2_in[k], passes * 16 + (16 if k == 0 else 0))
            sp.sem_inc(sp_turn, 1)

        @block.scalar
        def _(act):
            act.dma_start(b1T[:, :, :].rearrange("p e a -> p (e a)"), b1.rearrange("e (a p) -> p (e a)", p=P)).then_inc(b1_in, 16)
            act.preload_act_table(ACT.Relu)
            act.wait_ge(b1_in, 16)
            passes = pass_count(act)

            def step(k, i, head):
                s = k % 2
                act.wait_ge(x_tr, i + 1)
                if not (head and i < 2):
                    act.wait_ge(h_done, i - 1)
                act.activation(xT[:, s, :], ps_x[s][:, 0:D], ACT.Copy).then_inc(xT_ready, 1)
                if not (head and i < 2):
                    e = expert(act, i, 2)
                    act.wait_ge(h_tr, i - 1)
                    if not (head and i < 4):
                        act.wait_ge(o_done, i - 3)
                    for j in range(KF):
                        last = act.activation(hidT[:, s, j * P:(j + 1) * P], ps_ht[s][:, j * P:(j + 1) * P], ACT.Relu,
                                              bias=b1T[:, bass.ds(e, 1), j:j + 1].rearrange("p a b -> p (a b)"))
                    last.then_inc(hT_ready, 1)

            for i in range(2 * B):
                step(i % B, i, True)
            with act.Fori(2, passes) as it:
                for k in range(B):
                    step(k, it * B + k, False)

        @block.tensor
        def _(pe):
            pe.wait_ge(w1_in, 64)
            pe.wait_ge(w2_in, 64)
            passes = pass_count(pe)

            def step(k, i, head):
                s, o = k % 2, 1 - k % 2
                pe.wait_ge(x_in[k], 16 * (i // B + 1) if head else (i - k) * (16 // B) + 16)
                if not (head and i < 2):
                    pe.wait_ge(xT_ready, i - 1)
                for a in range(KD):
                    last = pe.transpose(ps_x[s][:, a * P:(a + 1) * P], xt[:, k, a * P:(a + 1) * P], ident[:, :])
                last.then_inc(x_tr, 1)
                if not (head and i < 1):
                    e = expert(pe, i, 1)
                    pe.wait_ge(xT_ready, i)
                    if not (head and i < 3):
                        pe.wait_ge(h_copied, i - 2)
                    for a in range(KD):
                        last = pe.matmul(ps_h[o][:, :], xT[:, o, a * P:(a + 1) * P],
                                         w1_sb[:, bass.ds(e, 1), a, :].rearrange("p a b -> p (a b)"),
                                         start=(a == 0), stop=(a == KD - 1))
                    last.then_inc(h_done, 1)
                if not (head and i < 2):
                    pe.wait_ge(h_copied, i - 1)
                    if not (head and i < 4):
                        pe.wait_ge(hT_ready, i - 3)
                    for j in range(KF):
                        last = pe.transpose(ps_ht[s][:, j * P:(j + 1) * P], hid[:, s, j * P:(j + 1) * P], ident[:, :])
                    last.then_inc(h_tr, 1)
                if not (head and i < 3):
                    e = expert(pe, i, 3)
                    pe.wait_ge(hT_ready, i - 2)
                    if not (head and i < 5):
                        pe.wait_ge(o_ready, i - 4)
                    for j in range(KF):
                        last = pe.matmul(ps_o[o][:, 0:D], hidT[:, o, j * P:(j + 1) * P],
                                         w2_sb[:, bass.ds(e, 1), j, :].rearrange("p a b -> p (a b)"),
                                         start=(j == 0), stop=(j == KF - 1))
                    last.then_inc(o_done, 1)

            for i in range(2 * B):
                step(i % B, i, True)
            with pe.Fori(2, passes) as it:
                for k in range(B):
                    step(k, it * B + k, False)

        @block.vector
        def _(dve):
            passes = pass_count(dve)

            def step(k, i, head):
                o = 1 - k % 2
                if not (head and i < 1):
                    dve.wait_ge(h_done, i)
                    if not (head and i < 3):
                        dve.wait_ge(h_tr, i - 2)
                    dve.tensor_copy(hid[:, o, :], ps_h[o][:, :]).then_inc(h_copied, 1)
                if not (head and i < 3):
                    dve.wait_ge(b2_in[(k - 3) % B], 16 * ((i - 3) // B + 1) if head else (i - 3 - (k - 3) % B) * (16 // B) + 16)
                    dve.wait_ge(o_done, i - 2)
                    if not (head and i < 5):
                        dve.wait_ge(o_out[o], ((i - 3) // 2) * 16 if head else (i - 3 - o) * 8)
                    dve.tensor_tensor(o_sb[:, o, :], ps_o[o][:, 0:D], b2_t[:, (k - 3) % B, :], ALU.add).then_inc(o_ready, 1)

            for i in range(2 * B):
                step(i % B, i, True)
            with dve.Fori(2, passes) as it:
                for k in range(B):
                    step(k, it * B + k, False)


def stage7(nc, fgamma, fbeta, expert_out, out, x_all, rstd, nmr, slots, gates):
    with ExitStack() as ctx:
        def sb(name, shape, dt=F32):
            return ctx.enter_context(nc.sbuf_tensor(name, shape, dt))

        def sem(name):
            return ctx.enter_context(nc.semaphore(name))

        gam = sb("fgam", [P, D])
        bet = sb("fbet", [P, D])
        slot_g = sb("slot_g7", [P, 2, GRP, 2], I32)
        gate_g = sb("gate_g7", [P, GRP, 2])
        back = sb("back", [P, 2, GRP, 2, D])
        y = sb("y7", [P, GRP, D])
        part = sb("part", [P, GRP, D])
        moe = sb("moe", [P, 2, GRP, D])
        stats = sb("stats7", [P, GRP, 6])
        mv = sb("mv7", [P, GRP, 2])
        spare = sb("spare7", [P, 2])
        var_g = sb("var_g", [P, GRP])
        std_g = sb("std_g", [P, GRP])
        rstd_g = sb("rstd_g", [P, GRP])
        nmr_g = sb("nmr_g", [P, GRP])
        normed = sb("normed", [P, 2, GRP, D])

        par_in = sem("par_in7")
        dve_chain = sem("dve_chain7")
        slots_staged = sem("slots_staged")
        pool_turn = sem("pool_turn7")
        came = [sem(f"came{i}") for i in range(2)]
        y_ready = sem("y_ready7")
        group_used = sem("group_used7")
        norm_ready = sem("norm_ready7")
        out_ready = sem("out_ready")
        var_ready = sem("var_ready7")
        std_ready = sem("std_ready7")
        scale_ready = sem("scale_ready7")
        out_sent = [sem(f"out_sent{i}") for i in range(2)]
        block = ctx.enter_context(nc.Block())

        def tile(k, it):
            return bass.ds(it * GRP + k, 1)

        def group(it):
            return bass.ds(it * GRP, GRP)

        PASS_LINKS = 9

        def over_groups(eng, body):
            body(0, 0)
            with eng.Fori(0, (NGRP - 3) // 2) as it:
                body(it * 2 + 1, 1)
                body(it * 2 + 2, 0)

        def over_passes(eng, one_pass, link=None):
            one_pass(0, 0, None)
            with eng.Fori(0, (NGRP - 3) // 2) as it:
                if link:
                    link.loop(it, 0, 2 * PASS_LINKS)
                one_pass(it * 2 + 1, 1, it)
                one_pass(it * 2 + 2, 0, it)
            if link:
                link.end((NGRP - 3) // 2)
            for g in (NGRP - 2, NGRP - 1):
                one_pass(g, g % 2, (NGRP - 3) // 2, more=False)

        @block.gpsimd
        def _(pool):
            def fetch(g, s, last=False):
                pool.wait_ge(slots_staged, g + 1)
                pool.sem_inc(pool_turn, 1)
                for k in range(GRP):
                    m = LAST if last and k == GRP - 1 else P
                    for c in range(2):
                        pool.indirect_dma_start(back[0:m, s, k, c, :], None, expert_out,
                                                bass.IndirectOffsetOnAxis(ap=slot_g[0:m, s, k, c:c + 1], axis=0)).then_inc(came[s], 16)

            over_groups(pool, fetch)
            fetch(NGRP - 2, 1)
            fetch(NGRP - 1, 0, last=True)

        @block.scalar
        def _(act):
            def norm_sum(g, s, n):
                act.wait_ge(out_sent[s], n * 16 + 16)
                act.wait_ge(scale_ready, g + 1)
                for k in range(GRP):
                    act.activation(normed[:, s, k, :], moe[:, s, k, :], ACT.Identity,
                                   bias=nmr_g[:, k:k + 1], scale=rstd_g[:, k:k + 1]).then_inc(norm_ready, 1)

            def one_pass(g, s, n, more=True):
                for k in range(GRP):
                    if n is not None:
                        act.wait_ge(group_used, g)
                    act.activation(y[:, k, :], one(x_all[:, tile(k, g), :]), ACT.Identity,
                                   bias=nmr[:, tile(k, g)], scale=rstd[:, tile(k, g)]).then_inc(y_ready, 1)
                if n is not None:
                    norm_sum(g - 1, 1 - s, n)
                act.wait_ge(var_ready, g + 1)
                act.activation(std_g[:, :], var_g[:, :], ACT.Sqrt).then_inc(std_ready, 1)
                act.preload_act_table(ACT.Identity)

            act.preload_act_table(ACT.Identity)
            over_passes(act, one_pass)
            norm_sum(NGRP - 1, 0, NGRP // 2)

        @block.vector
        def _(dve):
            link = Chain(dve, dve_chain)
            dve.memset(back[:, 0, GRP - 1, :, :], 0.0)

            def stage_slots(g, s):
                link(dve.tensor_copy(slot_g[:, s, :, :], slots[:, bass.ds(g * GRP, GRP), :]))
                dve.memset(spare[:, 0:1], 0.0).then_inc(slots_staged, 1)

            def gather_sum(g, s):
                link(dve.tensor_copy(gate_g[:, :, :], gates[:, group(g), :]))
                dve.wait_ge(came[s], (g - s) * (16 * GRP) + 32 * GRP)
                dve.wait_ge(y_ready, g * GRP + GRP)
                for c in range(2):
                    for k in range(GRP):
                        last = dve.scalar_tensor_tensor(part[:, k, :] if c == 0 else moe[:, s, k, :],
                                                        back[:, s, k, c, :], gate_g[:, k, c:c + 1],
                                                        y[:, k, :] if c == 0 else part[:, k, :], ALU.mult, ALU.add)
                    link(last)
                dve.memset(spare[:, 0:1], 0.0).then_inc(group_used, 1)
                for k in range(GRP):
                    last = dve.bn_stats(stats[:, k, :], moe[:, s, k, :])
                link(last)
                dve.memset(spare[:, 1:2], 0.0)
                for k in range(GRP):
                    last = dve.bn_aggr(mv[:, k, :], stats[:, k, :])
                link(last)
                dve.tensor_scalar(var_g[:, :], mv[:, :, 1], EPS, None, ALU.add).then_inc(var_ready, 1)

            def scale(g):
                dve.wait_ge(std_ready, g + 1)
                link(dve.reciprocal(rstd_g[:, :], std_g[:, :]))
                dve.scalar_tensor_tensor(nmr_g[:, :], mv[:, :, 0], -1.0, rstd_g[:, :], ALU.mult, ALU.mult).then_inc(scale_ready, 1)

            def finish(g, s):
                rows = normed[:, s, :, :]
                dve.wait_ge(norm_ready, g * GRP + GRP)
                link(dve.tensor_tensor(rows, rows, spread_tiles(gam[:, :]), ALU.mult))
                link(dve.tensor_tensor(rows, rows, spread_tiles(bet[:, :]), ALU.add))
                dve.tensor_tensor(rows, rows, x_all[:, group(g), :], ALU.add).then_inc(out_ready, 1)

            def one_pass(g, s, n, more=True):
                if n is not None:
                    scale(g - 1)
                gather_sum(g, s)
                if more:
                    stage_slots(g + 2, s)
                if n is not None:
                    finish(g - 1, 1 - s)

            dve.wait_ge(par_in, 32)
            for g in range(2):
                stage_slots(g, g)
            over_passes(dve, one_pass, link)
            scale(NGRP - 1)
            finish(NGRP - 1, 0)

        @block.sync
        def _(sp):
            sp.dma_start(gam[:, :], fgamma.unsqueeze(0).to_broadcast([P, D])).then_inc(par_in, 16)
            sp.dma_start(bet[:, :], fbeta.unsqueeze(0).to_broadcast([P, D])).then_inc(par_in, 16)
            for s in range(2):
                sp.sem_inc(out_sent[s], 16)
            for it in range(NGRP):
                sp.wait_ge(out_ready, it + 1)
                t0 = it * GRP
                nt = GRP if it < NGRP - 1 else GRP - 1
                sp.dma_start(out[t0 * P:(t0 + nt) * P, :].rearrange("(t p) d -> p t d", p=P),
                             normed[:, it % 2, 0:nt, :]).then_inc(out_sent[it % 2], 16)
            last = (NGRP - 1) % 2
            sp.dma_start(out[FULL * P:N, :], normed[0:LAST, last, GRP - 1, :]).then_inc(out_sent[last], 16)
            sp.wait_ge(out_sent[last], 16 * ((NGRP + 1) // 2 + 2))
            sp.wait_ge(out_sent[1 - last], 16 * (NGRP // 2 + 1))


_INS = ["x", "src", "dst", "L0_gnn_W", "L0_gnn_a_src", "L0_gnn_a_dst", "L0_gnn_gamma", "L0_gnn_beta", "L0_ffn_gate_w",
        "L0_ffn_gate_b", "L0_ffn_w1", "L0_ffn_b1", "L0_ffn_w2", "L0_ffn_b2", "L0_ffn_gamma", "L0_ffn_beta"]


def kernel(**inputs):
    import concourse.bacc as _bacc
    from concourse.bass_utils import run_bass_kernel_spmd as _run

    nc = _bacc.Bacc("TRN2", target_bir_lowering=False, num_devices=1)
    arrays, args = {}, []
    for name in _INS:
        a = np.ascontiguousarray(inputs[name])
        arrays[f"in_{name}_dram"] = a
        args.append(nc.dram_tensor(f"in_{name}_dram", a.shape, mybir.dt.from_np(a.dtype), kind="ExternalInput").ap())
    args.append(nc.dram_tensor("out_0_dram", (N, D), F32, kind="ExternalOutput").ap())
    build(nc, *args)
    r = _run(nc, [arrays], core_ids=[0])
    return r.results[0]["out_0_dram"]
```
